# Optimizing a Trainium2 kernel written in Bass

```python
import numpy as np
import jax
import jax.numpy as jnp

def _softmax(x, axis=-1):
    return jax.nn.softmax(x, axis=axis)

def _gelu(x):
    return jax.nn.gelu(x, approximate=True)

def _silu(x):
    return jax.nn.silu(x)

def _sigmoid(x):
    return jax.nn.sigmoid(x)

def _layernorm(x, axis=-1, eps=1e-05):
    m = jnp.mean(x, axis=axis, keepdims=True)
    v = jnp.var(x, axis=axis, keepdims=True)
    return (x - m) / jnp.sqrt(v + eps)

def _scatter_add(tgt, idx, src, axis=0):
    return tgt.at[idx].add(src)

def _segment_sum(src, seg, n):
    return jax.ops.segment_sum(src, seg, n)
kernel_name = 'mk_prb_d2_jaxref_r8_9ec310'

def setup_inputs(seed: int=0):
    np.random.seed(seed)
    _w = jnp.asarray

    def _L0_attn_setup():
        import jax, jax.numpy as jnp
        import numpy as np
        D_MODEL = 128
        N_HEADS = 16
        LATENT_HEADS = 8
        LATENT_DIM = 64
        N_LATENTS = 64
        WINDOW = 32
        HEAD_DIM = D_MODEL // N_HEADS
        LAT_HD = LATENT_DIM // LATENT_HEADS
        B, S = (2, 512)

        def _pool_to_latents(x):
            Bx, Sx, C = x.shape
            chunk = max(1, Sx // N_LATENTS)
            return x.reshape(Bx, N_LATENTS, chunk, C).mean(axis=2)

        def _local_window_attn(Q, K, V):
            Bx, H, Sx, D = Q.shape
            W = WINDOW
            nb = Sx // W
            Qb = Q.reshape(Bx, H, nb, W, D)
            Kp = jnp.pad(K, ((0, 0), (0, 0), (W, 0), (0, 0))).reshape(Bx, H, nb + 1, W, D)
            Vp = jnp.pad(V, ((0, 0), (0, 0), (W, 0), (0, 0))).reshape(Bx, H, nb + 1, W, D)
            Kw = jnp.concatenate([Kp[:, :, :-1], Kp[:, :, 1:]], axis=3)
            Vw = jnp.concatenate([Vp[:, :, :-1], Vp[:, :, 1:]], axis=3)
            i = jnp.arange(W)[:, None]
            j = jnp.arange(2 * W)[None, :]
            base = (j > i) & (j <= i + W)
            blk0 = (jnp.arange(nb) > 0)[:, None, None] | (j >= W)[None, :, :]
            mask = base[None, :, :] & blk0
            sc = jnp.einsum('bhnid,bhnjd->bhnij', Qb, Kw) / np.sqrt(D).astype(np.float32)
            sc = jnp.where(mask[None, None], sc, -jnp.inf)
            p = jax.nn.softmax(sc, axis=-1)
            out = jnp.einsum('bhnij,bhnjd->bhnid', p, Vw)
            return out.reshape(Bx, H, Sx, D)
        key = jax.random.key(seed)
        ks = jax.random.split(key, 11)
        std = 0.02
        w = lambda k, shp: jax.random.normal(k, shp, jnp.float32) * std
        return {'x': jax.random.normal(ks[0], (B, S, D_MODEL), jnp.float32), 'wq': w(ks[1], (D_MODEL, D_MODEL)), 'wk': w(ks[2], (D_MODEL, D_MODEL)), 'wv': w(ks[3], (D_MODEL, D_MODEL)), 'wgq': w(ks[4], (D_MODEL, LATENT_DIM)), 'wgk': w(ks[5], (D_MODEL, LATENT_DIM)), 'wgv': w(ks[6], (D_MODEL, LATENT_DIM)), 'r_out_w': w(ks[7], (LATENT_DIM, D_MODEL)), 'gate_local_w': w(ks[8], (N_HEADS, HEAD_DIM)), 'gate_remote_w': w(ks[9], (N_HEADS, HEAD_DIM)), 'w_out': w(ks[10], (D_MODEL, D_MODEL))}
    _L0_attn_in = _L0_attn_setup()

    def _L0_ffn_setup():
        import jax, jax.numpy as jnp
        import numpy as np
        key = jax.random.key(seed)
        ks = jax.random.split(key, 4)
        B, T, M, E, F = (4, 256, 128, 8, 512)
        hidden_states = jax.random.normal(ks[0], (B, T, M), dtype=jnp.float32)
        wg = jax.random.normal(ks[1], (M, E), dtype=jnp.float32) * (1.0 / np.sqrt(M))
        w1 = jax.random.normal(ks[2], (E, M, F), dtype=jnp.float32) * (1.0 / np.sqrt(M))
        b1 = jnp.zeros((E, F), dtype=jnp.float32)
        w2 = jax.random.normal(ks[3], (E, F, M), dtype=jnp.float32) * (1.0 / np.sqrt(F))
        b2 = jnp.zeros((E, M), dtype=jnp.float32)
        return {'hidden_states': hidden_states, 'wg': wg, 'w1': w1, 'b1': b1, 'w2': w2, 'b2': b2}
    _L0_ffn_in = _L0_ffn_setup()

    def _L1_attn_setup():
        import jax, jax.numpy as jnp
        import numpy as np
        NUM_HEADS = 16
        D_MODEL = 128
        HEAD_DIM = D_MODEL // NUM_HEADS
        EPS = 1e-06

        def _feature_map(x):
            return jax.nn.elu(x) + 1.0
        key = jax.random.key(seed)
        ks = jax.random.split(key, 9)
        B, S, D = (4, 1024, D_MODEL)
        scale = 1.0 / np.sqrt(D)
        inputs_q = jax.random.normal(ks[0], (B, S, D), dtype=jnp.float32)
        Wq = jax.random.normal(ks[1], (D, D), dtype=jnp.float32) * scale
        Wk = jax.random.normal(ks[2], (D, D), dtype=jnp.float32) * scale
        Wv = jax.random.normal(ks[3], (D, D), dtype=jnp.float32) * scale
        Wo = jax.random.normal(ks[4], (D, D), dtype=jnp.float32) * scale
        bq = jnp.zeros((D,), jnp.float32)
        bk = jnp.zeros((D,), jnp.float32)
        bv = jnp.zeros((D,), jnp.float32)
        bo = jnp.zeros((D,), jnp.float32)
        return {'inputs_q': inputs_q, 'Wq': Wq, 'bq': bq, 'Wk': Wk, 'bk': bk, 'Wv': Wv, 'bv': bv, 'Wo': Wo, 'bo': bo}
    _L1_attn_in = _L1_attn_setup()

    def _L1_ffn_setup():
        import jax, jax.numpy as jnp
        import numpy as np
        E, H, F, K = (8, 128, 256, 2)
        B, S = (2, 256)
        key = jax.random.key(seed)
        ks = jax.random.split(key, 8)

        def w(k, shape, fan_in):
            return jax.random.normal(k, shape, jnp.float32) / np.float32(np.sqrt(fan_in))
        return {'x': jax.random.normal(ks[0], (B, S, H), jnp.float32), 'Wgate': w(ks[1], (H, E), H), 'bgate': jnp.zeros((E,), jnp.float32), 'W1': w(ks[2], (E, H, F), H), 'b1': jnp.zeros((E, F), jnp.float32), 'W2': w(ks[3], (E, H, F), H), 'b2': jnp.zeros((E, F), jnp.float32), 'Wg': w(ks[4], (E, F, F), F), 'bg': jnp.zeros((E, F), jnp.float32), 'Wl': w(ks[5], (E, F, F), F), 'bl': jnp.zeros((E, F), jnp.float32), 'W3': w(ks[6], (E, F, H), F), 'b3': jnp.zeros((E, H), jnp.float32)}
    _L1_ffn_in = _L1_ffn_setup()
    _d = {'L0_attn_x': _L0_attn_in['x'], 'L0_attn_wq': _L0_attn_in['wq'], 'L0_attn_wk': _L0_attn_in['wk'], 'L0_attn_wv': _L0_attn_in['wv'], 'L0_attn_wgq': _L0_attn_in['wgq'], 'L0_attn_wgk': _L0_attn_in['wgk'], 'L0_attn_wgv': _L0_attn_in['wgv'], 'L0_attn_r_out_w': _L0_attn_in['r_out_w'], 'L0_attn_gate_local_w': _L0_attn_in['gate_local_w'], 'L0_attn_gate_remote_w': _L0_attn_in['gate_remote_w'], 'L0_attn_w_out': _L0_attn_in['w_out'], 'L0_ffn_wg': _L0_ffn_in['wg'], 'L0_ffn_w1': _L0_ffn_in['w1'], 'L0_ffn_b1': _L0_ffn_in['b1'], 'L0_ffn_w2': _L0_ffn_in['w2'], 'L0_ffn_b2': _L0_ffn_in['b2'], 'L1_attn_Wq': _L1_attn_in['Wq'], 'L1_attn_bq': _L1_attn_in['bq'], 'L1_attn_Wk': _L1_attn_in['Wk'], 'L1_attn_bk': _L1_attn_in['bk'], 'L1_attn_Wv': _L1_attn_in['Wv'], 'L1_attn_bv': _L1_attn_in['bv'], 'L1_attn_Wo': _L1_attn_in['Wo'], 'L1_attn_bo': _L1_attn_in['bo'], 'L1_ffn_Wgate': _L1_ffn_in['Wgate'], 'L1_ffn_bgate': _L1_ffn_in['bgate'], 'L1_ffn_W1': _L1_ffn_in['W1'], 'L1_ffn_b1': _L1_ffn_in['b1'], 'L1_ffn_W2': _L1_ffn_in['W2'], 'L1_ffn_b2': _L1_ffn_in['b2'], 'L1_ffn_Wg': _L1_ffn_in['Wg'], 'L1_ffn_bg': _L1_ffn_in['bg'], 'L1_ffn_Wl': _L1_ffn_in['Wl'], 'L1_ffn_bl': _L1_ffn_in['bl'], 'L1_ffn_W3': _L1_ffn_in['W3'], 'L1_ffn_b3': _L1_ffn_in['b3']}
    _x0 = _d['L0_attn_x']
    _d['L0_attn_x'] = jax.random.normal(jax.random.fold_in(jax.random.key(seed), 1), (2, 1024, 128), dtype=_x0.dtype)
    del _x0
    return _d

def reference(L0_attn_x, L0_attn_wq, L0_attn_wk, L0_attn_wv, L0_attn_wgq, L0_attn_wgk, L0_attn_wgv, L0_attn_r_out_w, L0_attn_gate_local_w, L0_attn_gate_remote_w, L0_attn_w_out, L0_ffn_wg, L0_ffn_w1, L0_ffn_b1, L0_ffn_w2, L0_ffn_b2, L1_attn_Wq, L1_attn_bq, L1_attn_Wk, L1_attn_bk, L1_attn_Wv, L1_attn_bv, L1_attn_Wo, L1_attn_bo, L1_ffn_Wgate, L1_ffn_bgate, L1_ffn_W1, L1_ffn_b1, L1_ffn_W2, L1_ffn_b2, L1_ffn_Wg, L1_ffn_bg, L1_ffn_Wl, L1_ffn_bl, L1_ffn_W3, L1_ffn_b3):

    def _L0_attn_ref(x, wq, wk, wv, wgq, wgk, wgv, r_out_w, gate_local_w, gate_remote_w, w_out):
        import jax, jax.numpy as jnp
        import numpy as np
        D_MODEL = 128
        N_HEADS = 16
        LATENT_HEADS = 8
        LATENT_DIM = 64
        N_LATENTS = 64
        WINDOW = 32
        HEAD_DIM = D_MODEL // N_HEADS
        LAT_HD = LATENT_DIM // LATENT_HEADS
        B, S = (2, 512)

        def _pool_to_latents(x):
            Bx, Sx, C = x.shape
            chunk = max(1, Sx // N_LATENTS)
            return x.reshape(Bx, N_LATENTS, chunk, C).mean(axis=2)

        def _local_window_attn(Q, K, V):
            Bx, H, Sx, D = Q.shape
            W = WINDOW
            nb = Sx // W
            Qb = Q.reshape(Bx, H, nb, W, D)
            Kp = jnp.pad(K, ((0, 0), (0, 0), (W, 0), (0, 0))).reshape(Bx, H, nb + 1, W, D)
            Vp = jnp.pad(V, ((0, 0), (0, 0), (W, 0), (0, 0))).reshape(Bx, H, nb + 1, W, D)
            Kw = jnp.concatenate([Kp[:, :, :-1], Kp[:, :, 1:]], axis=3)
            Vw = jnp.concatenate([Vp[:, :, :-1], Vp[:, :, 1:]], axis=3)
            i = jnp.arange(W)[:, None]
            j = jnp.arange(2 * W)[None, :]
            base = (j > i) & (j <= i + W)
            blk0 = (jnp.arange(nb) > 0)[:, None, None] | (j >= W)[None, :, :]
            mask = base[None, :, :] & blk0
            sc = jnp.einsum('bhnid,bhnjd->bhnij', Qb, Kw) / np.sqrt(D).astype(np.float32)
            sc = jnp.where(mask[None, None], sc, -jnp.inf)
            p = jax.nn.softmax(sc, axis=-1)
            out = jnp.einsum('bhnij,bhnjd->bhnid', p, Vw)
            return out.reshape(Bx, H, Sx, D)
        Bx, Sx, _ = x.shape
        chunk = max(1, Sx // N_LATENTS)
        Q = (x @ wq).reshape(Bx, Sx, N_HEADS, HEAD_DIM).transpose(0, 2, 1, 3)
        K = (x @ wk).reshape(Bx, Sx, N_HEADS, HEAD_DIM).transpose(0, 2, 1, 3)
        V = (x @ wv).reshape(Bx, Sx, N_HEADS, HEAD_DIM).transpose(0, 2, 1, 3)
        local = _local_window_attn(Q, K, V)
        GQ = (x @ wgq).reshape(Bx, Sx, LATENT_HEADS, LAT_HD).transpose(0, 2, 1, 3)
        GK = _pool_to_latents(x @ wgk).reshape(Bx, N_LATENTS, LATENT_HEADS, LAT_HD).transpose(0, 2, 1, 3)
        GV = _pool_to_latents(x @ wgv).reshape(Bx, N_LATENTS, LATENT_HEADS, LAT_HD).transpose(0, 2, 1, 3)
        lsc = jnp.einsum('bhsd,bhnd->bhsn', GQ, GK) / np.sqrt(LAT_HD).astype(np.float32)
        lmask = jnp.arange(N_LATENTS)[None, :] <= (jnp.arange(Sx) // chunk)[:, None]
        lsc = jnp.where(lmask[None, None], lsc, -jnp.inf)
        lp = jax.nn.softmax(lsc, axis=-1)
        rem = jnp.einsum('bhsn,bhnd->bhsd', lp, GV)
        rem = rem.transpose(0, 2, 1, 3).reshape(Bx, Sx, LATENT_DIM) @ r_out_w
        rem = rem.reshape(Bx, Sx, N_HEADS, HEAD_DIM).transpose(0, 2, 1, 3)
        gl = jax.nn.sigmoid(jnp.einsum('bhsd,hd->bhs', Q, gate_local_w))[..., None]
        gr = jax.nn.sigmoid(jnp.einsum('bhsd,hd->bhs', Q, gate_remote_w))[..., None]
        out = gl * local + gr * rem
        out = out.transpose(0, 2, 1, 3).reshape(Bx, Sx, D_MODEL)
        return out @ w_out

    def _L0_ffn_ref(hidden_states, wg, w1, b1, w2, b2):
        import jax, jax.numpy as jnp
        import numpy as np
        B, T, M = hidden_states.shape
        E = wg.shape[1]
        S = B * T
        MIN_CAPACITY = 4
        C = max((S + E - 1) // E, MIN_CAPACITY)
        x = hidden_states.reshape(S, M)
        logits = x @ wg
        gates = jax.nn.softmax(logits, axis=-1)
        idx = jnp.argmax(gates, axis=-1)
        mask1 = jax.nn.one_hot(idx, E, dtype=gates.dtype)
        l_aux = jnp.sum(gates.mean(0) * mask1.mean(0)) * E
        locations1 = jnp.cumsum(mask1, axis=0) - 1.0
        mask1 = mask1 * (locations1 < C)
        gates1_s = jnp.sum(gates * mask1, axis=1)
        loc_s = jnp.sum(locations1 * mask1, axis=1).astype(jnp.int32)
        loc_sc = jax.nn.one_hot(loc_s, C, dtype=gates.dtype)
        combine_weights = jnp.einsum('se,sc->sec', gates1_s[:, None] * mask1, loc_sc)
        dispatch_mask = (combine_weights > 0).astype(x.dtype)
        dispatched = jnp.einsum('sec,sm->ecm', dispatch_mask, x)
        h = jax.nn.gelu(jnp.einsum('ecm,emf->ecf', dispatched, w1) + b1[:, None, :])
        expert_out = jnp.einsum('ecf,efm->ecm', h, w2) + b2[:, None, :]
        out = jnp.einsum('sec,ecm->sm', combine_weights, expert_out)
        return out.reshape(B, T, M)

    def _L1_attn_ref(inputs_q, Wq, bq, Wk, bk, Wv, bv, Wo, bo):
        import jax, jax.numpy as jnp
        import numpy as np
        NUM_HEADS = 16
        D_MODEL = 128
        HEAD_DIM = D_MODEL // NUM_HEADS
        EPS = 1e-06

        def _feature_map(x):
            return jax.nn.elu(x) + 1.0
        B, S, D = inputs_q.shape
        H, Dh = (NUM_HEADS, HEAD_DIM)
        q = (inputs_q @ Wq + bq).reshape(B, S, H, Dh)
        k = (inputs_q @ Wk + bk).reshape(B, S, H, Dh)
        v = (inputs_q @ Wv + bv).reshape(B, S, H, Dh)
        q = _feature_map(q)
        k = _feature_map(k)
        kv = jnp.einsum('bkhd,bkhm->bhdm', k, v)
        out = jnp.einsum('bqhd,bhdm->bqhm', q, kv)
        normalizer = jnp.einsum('bqhd,bkhd->bqh', q, k)
        normalizer = jnp.maximum(normalizer, EPS)
        out = out / normalizer[..., None]
        out = out.reshape(B, S, D)
        return out @ Wo + bo

    def _L1_ffn_ref(x, Wgate, bgate, W1, b1, W2, b2, Wg, bg, Wl, bl, W3, b3):
        import jax, jax.numpy as jnp
        import numpy as np
        E, H, F, K = (8, 128, 256, 2)
        B, S = (2, 256)
        gout = x @ Wgate + bgate
        topv, topi = jax.lax.top_k(gout, K)
        topw = jax.nn.softmax(topv, axis=-1)
        combine = jnp.sum(jax.nn.one_hot(topi, E, dtype=x.dtype) * topw[..., None], axis=-2)
        x1 = jnp.einsum('bsh,ehf->bsef', x, W1) + b1
        x2 = jnp.einsum('bsh,ehf->bsef', x, W2) + b2
        z = x1 * x2
        g = jnp.einsum('bsef,efg->bseg', z, Wg) + bg
        o = g * jax.nn.sigmoid(g) * (jnp.einsum('bsef,efg->bseg', z, Wl) + bl)
        y = jnp.einsum('bsef,efh->bseh', o, W3) + b3
        return jnp.einsum('bse,bseh->bsh', combine, y)
    x = L0_attn_x
    xn = _layernorm(x, axis=-1)
    x = x + _L0_attn_ref(xn, L0_attn_wq, L0_attn_wk, L0_attn_wv, L0_attn_wgq, L0_attn_wgk, L0_attn_wgv, L0_attn_r_out_w, L0_attn_gate_local_w, L0_attn_gate_remote_w, L0_attn_w_out) + _L0_ffn_ref(xn, L0_ffn_wg, L0_ffn_w1, L0_ffn_b1, L0_ffn_w2, L0_ffn_b2)
    xn = _layernorm(x, axis=-1)
    x = x + _L1_attn_ref(xn, L1_attn_Wq, L1_attn_bq, L1_attn_Wk, L1_attn_bk, L1_attn_Wv, L1_attn_bv, L1_attn_Wo, L1_attn_bo) + _L1_ffn_ref(xn, L1_ffn_Wgate, L1_ffn_bgate, L1_ffn_W1, L1_ffn_b1, L1_ffn_W2, L1_ffn_b2, L1_ffn_Wg, L1_ffn_bg, L1_ffn_Wl, L1_ffn_bl, L1_ffn_W3, L1_ffn_b3)
    return x

_drawn_inputs = setup_inputs


def setup_inputs(seed=0):
    import zlib

    import numpy as np

    out = dict(_drawn_inputs(seed))
    spreads = {'L0_ffn_b1': (0.0, 0.1),
     'L0_ffn_b2': (0.0, 0.1),
     'L1_attn_bq': (0.0, 0.8),
     'L1_attn_bk': (0.0, 0.8),
     'L1_attn_bv': (0.0, 0.1),
     'L1_attn_bo': (0.0, 0.1),
     'L1_ffn_bgate': (0.0, 0.1),
     'L1_ffn_b1': (0.0, 0.1),
     'L1_ffn_b2': (0.0, 0.1),
     'L1_ffn_bg': (0.0, 0.1),
     'L1_ffn_bl': (0.0, 0.1),
     'L1_ffn_b3': (0.0, 0.1)}
    factors = {'L0_attn_wq': 8.0,
     'L0_attn_wk': 8.0,
     'L0_attn_wgq': 8.0,
     'L0_attn_wgk': 8.0,
     'L0_attn_wgv': 8.0,
     'L0_attn_r_out_w': 8.0,
     'L0_attn_gate_local_w': 8.0,
     'L0_attn_gate_remote_w': 8.0,
     'L1_attn_Wq': 4.656}
    for name, (base, spread) in spreads.items():
        noise = np.random.default_rng([zlib.crc32(name.encode()), seed]).standard_normal(out[name].shape)
        drawn = base * np.exp(spread * noise) if base else spread * noise
        out[name] = jnp.asarray(drawn.astype(out[name].dtype))
    for name, factor in factors.items():
        out[name] = (out[name] * factor).astype(out[name].dtype)
    return out
```

```python
from contextlib import ExitStack

import numpy as np

import concourse.bass as bass
from concourse import mybir

F32 = mybir.dt.float32
BF16 = mybir.dt.bfloat16
I32 = mybir.dt.int32
U32 = mybir.dt.uint32
ALU = mybir.AluOpType
ACT = mybir.ActivationFunctionType
X = mybir.AxisListType.X

P = 128
B, S = 2, 1024
N = B * S
T = N // P
E = 8
WIN = 32
NLAT = 64
CH = 256
NCH = S // CH
NB = CH // WIN
NP2 = NB // 2
UL, UG = 4, 2
U = UL + UG
HD = 8
VW = HD + 1
NEG = -1e30
F0 = 512
CAP = N // E
J0 = E * CAP // P
F1 = 256
J1 = 2 * N // P + E - 1
W12, WGL, W3 = 2 * F1, 4 * F1, 2 * P
BIAS1 = 4 * F1 + P

WEIGHTS = ["wq", "wk", "wv", "wout", "rout", "Wq", "Wk", "Wv", "Wo"]
COL = {name: 128 * i for i, name in enumerate(WEIGHTS)}
at = 128 * len(WEIGHTS)
for name, width in (("wgq", 64), ("wgk", 64), ("wgv", 64), ("wg", 8), ("Wgate", 8), ("glw", 1), ("grw", 1), ("bq", 1)):
    COL[name] = at
    at += width
NW = at
CF = {}
at = 0
for name, width in (("ident", 128), ("heads", 128), ("heads_hgd", 128), ("mine", 4), ("iota_e", 8), ("iota_j", J1),
                    ("trash0", J0), ("trash1", J1), ("reset", 128), ("thresholds", 16), ("thresholds_one", E), ("part", 1), ("hi", 2 * T)):
    CF[name] = at
    at += width
NCF = at
CB = {}
at = 0
for name, width in (("before", 128), ("ones", 128), ("iota", 128), ("spread", 128), ("local", 2 * 512), ("latent", 4 * 512)):
    CB[name] = at
    at += width
NCB = at


def constants():
    p = np.arange(P)
    f = {"ident": np.eye(P), "heads": p[:, None] // HD == p[None] // HD}
    c = np.arange(P)
    head_of = 4 * (c // 8 % 4) + c // 32
    f["heads_hgd"] = p[:, None] // HD == head_of[None]
    f["mine"] = (p[:, None] // HD % 4 == np.arange(4)[None]) / np.sqrt(np.float32(HD))
    f["iota_e"] = np.broadcast_to(np.arange(E), (P, E))
    f["iota_j"] = np.broadcast_to(np.arange(J1), (P, J1))
    f["trash0"] = N + P * np.arange(J0)[None] + p[:, None]
    f["trash1"] = 2 * N + P * np.arange(J1)[None] + p[:, None]
    f["reset"] = np.broadcast_to(np.arange(P) % T != 0, (P, P))
    f["thresholds"] = np.broadcast_to(P * np.arange(16), (P, 16))
    f["thresholds_one"] = np.ones((P, E))
    f["part"] = p[:, None]
    f["hi"] = np.broadcast_to(1 + np.arange(2 * T), (P, 2 * T))
    b = {"before": p[:, None] < p[None], "ones": np.ones((P, P)), "iota": np.broadcast_to(p, (P, P))}
    i = p[:, None] % WIN
    b["spread"] = i == p[None] % WIN
    j = np.arange(512)[None] % 64
    local = (j > i) & (j <= i + WIN)
    first = local & ((np.arange(512)[None] >= 64) | (j >= WIN))
    b["local"] = np.where(np.concatenate([first, local], 1), 0, NEG)
    s = 32 * (np.arange(4 * 512)[None] // 64) + i
    b["latent"] = np.where(np.arange(4 * 512)[None] % 64 <= s // (S // NLAT), 0, NEG)
    cf, cb = np.zeros((P, NCF), np.float32), np.zeros((P, NCB), mybir.dt.np(BF16))
    for src, dst, cols in ((f, cf, CF), (b, cb, CB)):
        for k, v in src.items():
            dst[:, cols[k]:cols[k] + v.shape[1]] = v
    return cf, cb


class Steps:

    def __init__(self, eng, sem):
        self.eng, self.sem, self.n, self.base = eng, sem, 0, 0

    def __call__(self, ins):
        self.mark(ins)
        self.wait()

    def mark(self, ins):
        ins.then_inc(self.sem, 1)
        self.n += 1

    def wait(self, back=0):
        self.eng.wait_ge(self.sem, self.base + (self.n - back))


def turns(eng, step, peel, trips, unroll, total):
    for i in range(peel):
        step(0, i, True)
    with eng.Fori(0, trips) as q:
        for k in range(peel, peel + unroll):
            step(q, k, False)
    for i in range(peel + trips * unroll, total):
        step(0, i, True)


def expert_turns(eng, step):
    turns(eng, step, 2, 2, 2, E + 1)


def tile_turns(eng, step):
    turns(eng, step, 4, 8, 4, J1 + 4)


def program(nc, ins, out):
    ctx = ExitStack()

    def sb(name, shape, dt=F32):
        return ctx.enter_context(nc.sbuf_tensor(name, shape, dt))

    def sem(name):
        return ctx.enter_context(nc.semaphore(name))

    def dram(name, rows):
        return nc.dram_tensor(name, [rows, P], F32, kind="Internal").ap()

    xn0_rows, xn1_rows = dram("xn0_rows", N), dram("xn1_rows", N)
    y0_rows = dram("y0_rows", N + J0 * P)
    y1_rows = dram("y1_rows", 2 * N + J1 * P)

    with ctx:
        wts, cf, cb = sb("wts", [P, NW]), sb("cf", [P, NCF]), sb("cb", [P, NCB], BF16)
        rows1 = sb("rows1", [P, 3 * P + E])
        x = sb("x", [P, T, P])
        xn = sb("xn", [P, T, P])
        xnT = sb("xnT", [P, B, WIN + S])
        stats, mv, var, sq, rstd = sb("stats", [P, T, 6]), sb("mv", [P, T, 2]), sb("var", [P, T]), sb("sq", [P, T]), sb("rstd", [P, T])
        gate_w = sb("gate_w", [P, 2, P])
        lg, oh, oh2 = sb("lg", [P, T, E]), sb("oh", [P, T, E]), sb("oh2", [P, T, E])
        ta, tb = sb("ta", [P, T, E]), sb("tb", [P, T, E])
        chosen, upto = sb("chosen", [P, E, T]), sb("upto", [P, E, T])
        chosen_bf, earlier_bf = sb("chosen_bf", [P, E, T], BF16), sb("earlier_bf", [P, E, T], BF16)
        total_bf = sb("total_bf", [P, E], BF16)
        pos = sb("pos", [P, E, T])
        m1, m2, id1, id2, esum, gate, keep, w1c, w2c, e21, own_pos = (
            sb("r_" + n, [P, T]) for n in ("m1", "m2", "id1", "id2", "esum", "gate", "keep", "w1c", "w2c", "e21", "own_pos"))
        slot, lo, hi = sb("slot", [P, 2, T]), sb("lo", [P, 2, T]), sb("hi", [P, 2, T])
        slot_i, lo_i, hi_i = sb("slot_i", [P, 2, T], I32), sb("lo_i", [P, 2, T], I32), sb("hi_i", [P, 2, T], I32)
        is_lo = sb("is_lo", [P, 4, P], BF16)
        is_hi = sb("is_hi", [P, 2 * T, J1])
        ids = sb("ids", [P, 2 * T, 2, J1], BF16)
        cnt, tiles, tiles_end, base = (sb("e_" + n, [P, E]) for n in ("cnt", "tiles", "end", "base"))
        over = sb("over", [P, E, 16])
        passed = sb("passed", [P, J1, E])
        te_f, te = sb("te_f", [P, J1]), sb("te", [P, J1], I32)
        inv, ra, rb = sb("inv", [P, 2, J1]), sb("ra", [P, J1]), sb("rb", [P, J1])
        rocc = sb("rocc", [P, J1])
        from0, to0 = sb("from0", [P, J0], I32), sb("to0", [P, J0], I32)
        from1, to1 = sb("from1", [P, J1], I32), sb("to1", [P, J1], I32)
        xw, sumT = sb("xw", [P, WIN + CH]), sb("sumT", [P, NLAT])
        qT, kT, gkT = sb("qT", [P, CH]), sb("kT", [P, WIN + CH]), sb("gkT", [64, NLAT])
        shared = sb("shared", [P, E * BIAS1])
        bias1 = shared[:].rearrange("p (e c) -> p e c", e=E)
        off = [0]

        def part(*dims):
            n = int(np.prod(dims))
            ap = shared[:, off[0]:off[0] + n]
            off[0] += n
            return ap

        qd = part(NB, 4, WIN).rearrange("p (b h i) -> p b h i", b=NB, h=4)
        gqd = part(NB, 4, WIN).rearrange("p (b h i) -> p b h i", b=NB, h=4)
        vd_flat, gvd_flat = part(NP2, UL, 2, 4, VW), part(UG, 2, 4, VW)
        vd = vd_flat.rearrange("p (c b h o) -> p c b h o", c=NP2 * UL, b=2, h=4)
        gvd = gvd_flat.rearrange("p (g b h o) -> p g b h o", g=UG, b=2, h=4)
        prob, probT = (part(2, 512).rearrange("p (r n) -> p r n", r=2) for _ in range(2))
        oall_flat = part(U, NB, 4, VW)
        oall = oall_flat.rearrange("p (u b h o) -> p u b h o", u=U, b=NB, h=4)
        att_flat, attT_flat = part(NB, 2, 32), part(NB, 2, 32)
        rmax, rsum = sb("rmax", [P, 2, NB]), sb("rsum", [P, U, NB])
        eg, sg = sb("eg", [P, 2, CH]), sb("sg", [P, 2, CH])
        near, mix = sb("near", [P, CH]), sb("mix", [P, CH])
        we = sb("we", [P, 2, 2 * F0 + 4])
        b2e = sb("b2e", [P, 2, P])
        xg, xgT = sb("xg", [P, 4, P]), sb("xgT", [P, 2 * P])
        hT = sb("hT", [P, 4, 2 * P])
        ysb = sb("ysb", [P, 4, P])

        ig, isc = sb("ig", [P, 4], I32), sb("isc", [P, 4], I32)
        w1s = sb("w1s", [P, E, W12 + WGL + W3])
        kraw, kmin, kexp, kf = (sb(n, [P, 2, P]) for n in ("kraw", "kmin", "kexp", "kf"))
        vf = sb("vf", [P, 2, P + 1])
        kvd, ksd, ksum = sb("kvd", [P, P]), sb("ksd", [P, P]), sb("ksum", [P, 1])
        qpos, qmin, qf, den, aT = (sb(n, [P, 512]) for n in ("qpos", "qmin", "qf", "den", "aT"))
        xtT = sb("xtT", [P, 2, P])
        z, zT, oT = sb("z", [P, F1]), sb("zT", [P, F1]), sb("oT", [P, F1])
        zeros, h12, hgl, sil, og = qmin, aT, qpos, den[:, 0:F1], qf[:].rearrange("p (r f) -> p r f", r=2)

        bank = [ctx.enter_context(nc.psum_tensor(f"bank{i}", [P, 512], F32)) for i in range(8)]

        hidden_bank = (1, 2, 4, 5)

        def w(name, width=P):
            return wts[:, COL[name]:COL[name] + width]

        def c(name, width):
            return cf[:, CF[name]:CF[name] + width]

        def cbf(name, width, start=0):
            return cb[:, CB[name] + start:CB[name] + start + width]

        ident = c("ident", P)

        s_x = [sem(f"x_in{i}") for i in range(4)]
        s_cst, s_wts, s_rows1 = sem("constants_in"), sem("weights_in"), sem("rows1_in")
        s_w1, s_bias1 = sem("w1_in"), sem("bias1_in")
        dve_own, pool_own = sem("dve_own"), sem("pool_own")
        s_zero, s_y0z, s_xn, s_xt, s_xTs, s_xnd = (sem(n) for n in (
            "buffers_filled", "y0_zeroed", "xn_ready", "x_turned", "xnT_ready", "xn_in_dram"))
        s_lg, s_gin, s_gexp, s_cnt, s_pos, s_posread, s_islo, s_inv, s_route = (sem(n) for n in (
            "logits", "gate_in", "gate_exp", "choices_ready", "positions", "positions_read", "is_lo_ready", "inverse",
            "routed"))
        s_gatew, s_xw, s_sum, s_p1, s_p2, s_p3, s_p4 = (sem(n) for n in (
            "gate_w_ready", "xw_ready", "sums_ready", "q_made", "k_made", "v_made", "gates_made"))
        m0_free, m1_free, xw_free = sem("m0_free"), sem("m1_free"), sem("xw_free")
        s_S, s_max, s_sub, s_exp, s_tr, s_pte, s_pv, s_oe = (sem(n) for n in (
            "scores", "maxima", "shifted", "probs", "probs_turned", "probT_ready", "weighted", "weighted_out"))
        s_gvd, s_p_att, s_g1, s_rem, s_mix, s_proj, s_x1 = (sem(n) for n in (
            "gvd_ready", "attT_ready", "dve_chunk", "remote_made", "mixed", "projected", "x_added"))
        s_we = [sem(f"we_in{i}") for i in range(2)]
        s_xg = [sem(f"rows_in{i}") for i in range(4)]
        s_ys = [sem(f"rows_out{i}") for i in range(4)]
        s_ig, s_isc, s_index_seen = sem("gather_index"), sem("scatter_index"), sem("index_seen")
        s_tx, s_xgT, s_h, s_gelu, s_y, s_ysb = (sem(n) for n in (
            "rows_turned", "rowsT_ready", "hidden", "gelu_done", "y_made", "y_ready"))
        s_y0 = [sem(f"y0_back{i}") for i in range(4)]
        s_bo, s_kv, s_kmin, s_kexp, s_kf, s_kvsum, s_kvd = (sem(n) for n in (
            "bo_added", "kv_made", "kmin_ready", "kexp_ready", "kf_ready", "kv_summed", "kvd_ready"))
        s_qp, s_qmin, s_qexp, s_qf, s_num, s_aT, s_o1, s_x2 = (sem(n) for n in (
            "q1_made", "qmin_ready", "qexp_ready", "qf_ready", "num_made", "aT_ready", "att1_made", "x2_added"))
        t_x, t_xTs, t_h, t_hb, t_z, t_zT, t_zTs, t_g, t_gb, t_sil, t_o, t_oT, t_oTs, t_y, t_ysb = (
            sem("t_" + n) for n in ("x", "xTs", "h", "hb", "z", "zT", "zTs", "g", "gb", "sil", "o", "oT", "oTs", "y", "ysb"))
        s_yk = [sem(f"y1_back{i}") for i in range(2)]
        s_res, s_out = sem("result"), sem("out_done")

        block = ctx.enter_context(nc.Block())

        def ids_of(layer):
            n, width = ((T, J0), (2 * T, J1))[layer]
            return ids[:].rearrange("p n a j -> p (n a j)")[:, 0:n * 2 * width].rearrange("p (n a j) -> p n a j", n=n, a=2)

        def x_tile_T(t):
            b, o = divmod(t * P, S)
            return xnT[:, b, WIN + o:WIN + o + P]

        @block.sync
        def _(sp):
            xv = ins["x"].rearrange("(t p) d -> p t d", p=P)
            for i in range(4):
                sp.dma_start(x[:, 4 * i:4 * i + 4, :], xv[:, 4 * i:4 * i + 4, :]).then_inc(s_x[i], 16)
            sp.dma_start(wts[:], ins["wts"]).then_inc(s_wts, 16)
            xd = xn0_rows.rearrange("(t p) d -> p t d", p=P)
            for i in range(4):
                sp.wait_ge(s_xn, i + 1)
                sp.dma_start(xd[:, 4 * i:4 * i + 4, :], xn[:, 4 * i:4 * i + 4, :]).then_inc(s_xnd, 16)
            for e in range(2):
                sp.dma_start(we[:, e, :], ins["we"][e]).then_inc(s_we[e], 16)
                sp.dma_start(b2e[:, e, :], ins["b2"][e:e + 1, :].partition_broadcast(P)).then_inc(s_we[e], 16)
            for i in range(2):
                sp.dma_start(w1s[:, E // 2 * i:E // 2 * (i + 1), :], ins["w1s"][:, E // 2 * i:E // 2 * (i + 1), :]).then_inc(s_w1, 16)
            for e in range(2, E):
                sp.wait_ge(s_y, 2 * (e - 1))
                sp.dma_start(we[:, e % 2, :], ins["we"][e]).then_inc(s_we[e % 2], 16)
                sp.wait_ge(s_ysb, 2 * (e - 1))
                sp.dma_start(b2e[:, e % 2, :], ins["b2"][e:e + 1, :].partition_broadcast(P)).then_inc(s_we[e % 2], 16)
            for k in range(4):
                sp.wait_ge(s_ys[k], 16 * (J0 // 4))
            yd = y0_rows[0:N, :].rearrange("(t p) d -> p t d", p=P)
            for i in range(4):
                sp.dma_start(xn[:, 4 * i:4 * i + 4, :], yd[:, 4 * i:4 * i + 4, :]).then_inc(s_y0[i], 16)
            xd = xn1_rows.rearrange("(t p) d -> p t d", p=P)
            for i in range(4):
                sp.wait_ge(s_xn, 4 + i + 1)
                sp.dma_start(xd[:, 4 * i:4 * i + 4, :], xn[:, 4 * i:4 * i + 4, :]).then_inc(s_xnd, 16)
            for k in range(4):
                sp.wait_ge(s_ys[k], 16 * (J0 // 4 + (J1 - k + 3) // 4))
            yd = y1_rows[0:2 * N, :].rearrange("(k t p) d -> k p t d", k=2, p=P)
            for b in range(B):
                sp.dma_start(xnT[:, b, 0:S].rearrange("p (t d) -> p t d", d=P), yd[0, :, 8 * b:8 * b + 8, :]).then_inc(s_yk[b], 16)
                sp.dma_start(xn[:, 8 * b:8 * b + 8, :], yd[1, :, 8 * b:8 * b + 8, :]).then_inc(s_yk[b], 16)
            ov = out.rearrange("(t p) d -> p t d", p=P)
            for b in range(B):
                sp.wait_ge(s_res, b + 1)
                sp.dma_start(ov[:, 8 * b:8 * b + 8, :], x[:, 8 * b:8 * b + 8, :]).then_inc(s_out, 16)
            sp.wait_ge(s_out, 16 * B)

        @block.gpsimd
        def _(pool):
            pool.memset(xnT[:, :, 0:WIN], 0.0).then_inc(s_zero, 1)
            pool.memset(sumT[:], 0.0).then_inc(s_zero, 1)
            pool.memset(zeros[:], 0.0).then_inc(s_zero, 1)
            pool.memset(att_flat, 0.0).then_inc(s_zero, 1)
            pool.memset(vd_flat, 0.0).then_inc(s_zero, 1)
            pool.memset(gvd_flat, 0.0).then_inc(s_zero, 1)
            pool.memset(vf[:, :, P:P + 1], 1.0).then_inc(s_zero, 1)
            pool.wait_ge(s_zero, 7)
            for blk in range(2):
                rows = slice(64 * blk, 64 * blk + 64)
                pool.memset(vd[rows, :, blk, :, HD], 1.0).then_inc(s_zero, 1)
                pool.memset(gvd[rows, :, blk, :, HD], 1.0).then_inc(s_zero, 1)
            zrows = y0_rows[0:N, :].rearrange("(p r) d -> p (r d)", p=P)
            for i in range(4):
                pool.dma_start(zrows[:, 512 * i:512 * i + 512], zeros[:]).then_inc(s_y0z, 16)
            pool.wait_ge(s_zero, 11)
            pool.wait_ge(s_xTs, 4)
            with pool.Fori(0, B) as b:
                for ch in range(NCH):
                    pool.wait_ge(xw_free, b * NCH + (ch + 1))
                    pool.tensor_copy(xw[:], xnT[:, bass.ds(b, 1), CH * ch:CH * ch + WIN + CH]
                                     .rearrange("p b s -> p (b s)")).then_inc(s_xw, 1)

            def gather(src, frm, j, k):
                slot_b = k[1] % 4
                pool.tensor_copy(ig[:, slot_b:slot_b + 1], frm[:, bass.ds(j, 1)]).then_inc(s_ig, 1)
                pool.wait_ge(s_ig, k[0] + 1)
                pool.sem_inc(s_index_seen, 1)
                pool.indirect_dma_start(
                    out=xg[:, slot_b, :], out_offset=None, in_=src,
                    in_offset=bass.IndirectOffsetOnAxis(ap=ig[:, slot_b:slot_b + 1].bitcast(U32), axis=0)
                ).then_inc(s_xg[slot_b], 16)

            def scatter(dst, to, j, k):
                slot_b = k[1] % 4
                pool.tensor_copy(isc[:, slot_b:slot_b + 1], to[:, bass.ds(j, 1)]).then_inc(s_isc, 1)
                pool.wait_ge(s_isc, k[0] + 1)
                pool.sem_inc(s_index_seen, 1)
                pool.indirect_dma_start(
                    out=dst, in_=ysb[:, slot_b, :], in_offset=None,
                    out_offset=bass.IndirectOffsetOnAxis(ap=isc[:, slot_b:slot_b + 1].bitcast(U32), axis=0)
                ).then_inc(s_ys[slot_b], 16)

            pool.wait_ge(s_cst, 32)
            pool.wait_ge(s_route, 1)
            pool.wait_ge(s_xnd, 64)
            pool.wait_ge(s_y0z, 64)
            for j in range(2):
                gather(xn0_rows, from0, j, (j, j))

            def expert(q, k, single):
                e = 2 * q + k
                if not single or k + 1 < E:
                    pool.wait_ge(s_tx, e)
                    for s in range(2):
                        j = 4 * q + (2 * (k + 1) + s)
                        gather(xn0_rows, from0, j, (j, 2 * (k + 1) + s))
                if not single or k >= 1:
                    for s in range(2):
                        j = 4 * q + (2 * (k - 1) + s)
                        pool.wait_ge(s_ysb, j + 1)
                        scatter(y0_rows, to0, j, (j, 2 * (k - 1) + s))

            expert_turns(pool, expert)
            pool.wait_ge(s_rows1, 16)
            pool.wait_ge(s_xn, 8)
            pool.tensor_tensor(x[:], x[:], rows1[:, 2 * P:3 * P].unsqueeze(1).broadcast_to([P, T, P]), ALU.add).then_inc(s_bo, 1)
            pool.wait_ge(s_route, 2)
            pool.wait_ge(s_xnd, 128)
            for j in range(3):
                gather(xn1_rows, from1, j, (J0 + j, j))

            def tile(q, k, single):
                i = 4 * q + k
                if not single or k + 3 < J1:
                    pool.wait_ge(t_x, i)
                    gather(xn1_rows, from1, i + 3, (J0 + i + 3, k + 3))
                if not single or 4 <= k:
                    pool.wait_ge(t_ysb, i - 3)
                    scatter(y1_rows, to1, i - 4, (J0 + i - 4, k - 4))

            tile_turns(pool, tile)

        @block.scalar
        def _(act):
            act.dma_start(cf[:], ins["cf"]).then_inc(s_cst, 16)
            act.dma_start(cb[:], ins["cb"]).then_inc(s_cst, 16)
            act.dma_start(rows1[:], ins["rows1"].partition_broadcast(P)).then_inc(s_rows1, 16)

            def evacuate_xT(layer):
                for i in range(4):
                    b, o = divmod(512 * i, S)
                    act.wait_ge(s_xt, 4 * layer + i + 1)
                    act.copy(xnT[:, b, WIN + o:WIN + o + 512], bank[i % 2][:]).then_inc(s_xTs, 1)

            def gate_exp(layer, n, src):
                act.wait_ge(s_gin, layer + 1)
                act.activation(n, src, ACT.Exp).then_inc(s_gexp, 1)

            evacuate_xT(0)
            gate_exp(0, tb[:], ta[:])
            act.wait_ge(s_cst, 32)
            act.wait_ge(s_zero, 11)

            with act.Fori(0, B) as b:
                for ch in range(NCH):
                    n = b * NCH + ch
                    un = n * U
                    act.wait_ge(s_p1, n + 1)
                    for hh in range(4):
                        act.activation(qd[:, :, hh, :], bank[6][:, 0:CH].rearrange("p (b i) -> p b i", i=WIN), ACT.Copy,
                                       scale=c("mine", 4)[:, hh:hh + 1])
                        act.activation(gqd[0:64, :, hh, :], bank[6][0:64, CH:2 * CH].rearrange("p (b i) -> p b i", i=WIN),
                                       ACT.Copy, scale=c("mine", 4)[0:64, hh:hh + 1])
                    act.copy(qT[:], bank[6][:, 0:CH]).then_inc(m0_free, 1)
                    act.wait_ge(s_p2, n + 1)
                    act.copy(kT[:], bank[7][:, 0:WIN + CH])
                    act.activation(gkT[0:64, :], bank[7][0:64, 320:384], ACT.Copy, scale=NLAT / S)
                    for blk in range(2):
                        act.activation(gvd[64 * blk:64 * blk + 64, :, blk, :, 0:HD],
                                       bank[7][0:64, 384:448].rearrange("p (g h d) -> p g h d", g=UG, h=4),
                                       ACT.Copy, scale=NLAT / S).then_inc(m1_free if blk else s_gvd, 1)
                    act.wait_ge(s_p4, n + 1)
                    act.activation(eg[:], bank[7][:].rearrange("p (a c) -> p a c", a=2), ACT.Exp, scale=-1.0).then_inc(m1_free, 1)

                    def turned(u):
                        act.wait_ge(s_tr, un + u + 1)
                        act.copy(probT[:, u % 2, :], bank[2 + u % 2][:]).then_inc(s_pte, 1)

                    def weighted(u):
                        act.wait_ge(s_pv, un + u + 1)
                        act.copy(oall_flat.rearrange("p (u n) -> p u n", u=U)[:, u, :], bank[4 + u % 2][:, 0:288]).then_inc(s_oe, 1)

                    for u in range(U):
                        act.wait_ge(s_sub, un + u + 1)
                        act.activation(prob[:, u % 2, :], prob[:, u % 2, :], ACT.Exp).then_inc(s_exp, 1)
                        turned(u)
                        if u >= 1:
                            weighted(u - 1)
                    weighted(U - 1)
            act.wait_ge(s_x1, B * NCH)
            act.dma_start(shared[:], ins["bias1"].partition_broadcast(P)).then_inc(s_bias1, 16)
            act.wait_ge(s_tx, 1)
            act.copy(xgT[:], bank[0][:, 0:2 * P]).then_inc(s_xgT, 1)

            def expert(q, k, single):
                if single and k >= E:
                    return
                e = 2 * q + k
                for f in range(4):
                    act.wait_ge(s_h, 4 * e + (f + 1))
                    act.activation(hT[:, f, :], bank[hidden_bank[f]][:, 0:2 * P], ACT.Gelu_apprx_tanh,
                                   bias=we[:, k % 2, 2 * F0 + f:2 * F0 + f + 1]).then_inc(s_gelu, 1)
                if not single or k + 1 < E:
                    act.wait_ge(s_tx, e + 2)
                    act.copy(xgT[:], bank[0][:, 0:2 * P]).then_inc(s_xgT, 1)

            expert_turns(act, expert)
            evacuate_xT(1)
            act.wait_ge(s_gin, 2)
            act.activation(e21[:], e21[:], ACT.Exp).then_inc(s_gexp, 1)
            for t in range(T):
                act.wait_ge(s_kmin, t + 1)
                act.activation(kexp[:, t % 2, :], kmin[:, t % 2, :], ACT.Exp).then_inc(s_kexp, 1)
                if t % 8 == 7:
                    for h in range(2):
                        act.wait_ge(s_qmin, t // 8 * 2 + h + 1)
                        act.activation(qmin[:], qmin[:], ACT.Exp).then_inc(s_qexp, 1)
            act.wait_ge(t_x, 1)
            act.copy(xtT[:, 0, :], bank[4][:, 0:P]).then_inc(t_xTs, 1)

            def tile(q, k, single):
                i = 4 * q + k
                if not single or 1 <= k <= J1:
                    act.wait_ge(t_zT, i)
                    act.copy(zT[:], bank[2][:, 0:F1]).then_inc(t_zTs, 1)
                if not single or 3 <= k < J1 + 3:
                    act.wait_ge(t_oT, i - 2)
                    act.copy(oT[:], bank[3][:, 0:F1]).then_inc(t_oTs, 1)
                if not single or k + 1 < J1:
                    act.wait_ge(t_x, i + 2)
                    act.copy(xtT[:, (k + 1) % 2, :], bank[4][:, 0:P]).then_inc(t_xTs, 1)
                if not single or 1 <= k <= J1:
                    act.wait_ge(t_gb, i)
                    act.activation(sil, hgl[:, 0:F1], ACT.Silu).then_inc(t_sil, 1)

            tile_turns(act, tile)

        @block.tensor
        def _(pe):
            pe.wait_ge(s_cst, 32)

            def turn_x(layer):
                for i in range(4):
                    pe.wait_ge(s_xn, 4 * layer + i + 1)
                    if i >= 2:
                        pe.wait_ge(s_xTs, 4 * layer + i - 1)
                    for k in range(4):
                        mm = pe.transpose(bank[i % 2][:, P * k:P * k + P], xn[:, 4 * i + k, :], ident)
                    mm.then_inc(s_xt, 1)

            def logits(layer, name):
                pe.wait_ge(s_wts, 16)
                for t in range(T):
                    pe.wait_ge(s_xTs, 4 * layer + t // 4 + 1)
                    mm = pe.matmul(bank[4][:, E * t:E * t + E], x_tile_T(t), w(name, E), start=True, stop=True)
                mm.then_inc(s_lg, 1)

            def prefix(layer):
                pe.wait_ge(s_cnt, layer + 1)
                pe.matmul(bank[5][:, 0:P], cbf("before", P), chosen_bf[:].rearrange("p e t -> p (e t)"), start=True, stop=False)
                pe.matmul(bank[5][:, 0:P], cbf("ones", P), earlier_bf[:].rearrange("p e t -> p (e t)"), start=False, stop=True)
                pe.matmul(bank[5][:, P:P + E], cbf("ones", P), total_bf[:], start=True, stop=True).then_inc(s_pos, 1)

            def inverse(layer, n, width, done):
                for i in range(n):
                    pe.wait_ge(s_islo, done + i + 1)
                    pe.matmul(bank[5][:, 0:2 * width], is_lo[:, i % 4, :], ids_of(layer)[:, i, :, :],
                              start=(i == 0), stop=(i == n - 1)).then_inc(s_inv, 1)

            turn_x(0)
            logits(0, "wg")
            prefix(0)
            inverse(0, T, J0, 0)
            pe.wait_ge(s_zero, 11)
            pe.wait_ge(s_gatew, 1)
            M0, M1 = bank[6], bank[7]

            with pe.Fori(0, B) as b:
                m0, m1 = [0], [0]

                def free(sem_, uses):
                    uses[0] += 1
                    pe.wait_ge(sem_, b * (3 * NCH) + uses[0])

                def scores(ch, n, u):
                    pe_bank = bank[u % 2]
                    if u >= 2:
                        pe.wait_ge(s_sub, n * U + (u - 1))
                    if u < UL:
                        mask = cbf("local", 512, 0 if ch == 0 else 512)
                    else:
                        mask = cbf("latent", 512, 512 * ch)
                    r = 32 * (u if u < UL else u - UL)
                    pe.matmul(pe_bank[:], cbf("spread", P)[r:r + 32, :], mask[r:r + 32, :], start=True, stop=False, skip_group_check=True)
                    for blk in range(NB):
                        q_, k_ = (qd, kT[r:r + 32, WIN * blk:WIN * blk + 64]) if u < UL else (gqd, gkT[r:r + 32, :])
                        mm = pe.matmul(pe_bank[:, 64 * blk:64 * blk + 64], q_[r:r + 32, blk, :, :].rearrange("p h i -> p (h i)"), k_,
                                       start=False, stop=(blk == NB - 1), skip_group_check=True)
                    mm.then_inc(s_S, 1)

                def turn(n, u):
                    pe.wait_ge(s_exp, n * U + (u + 1))
                    if u >= 2:
                        pe.wait_ge(s_pte, n * U + (u - 1))
                    for pr in range(NP2):
                        mm = pe.transpose(bank[2 + u % 2][:, P * pr:P * pr + P], prob[:, u % 2, P * pr:P * pr + P], ident)
                    mm.then_inc(s_tr, 1)

                def weigh(n, u):
                    pe.wait_ge(s_pte, n * U + (u + 1))
                    if u >= 2:
                        pe.wait_ge(s_oe, n * U + (u - 1))
                    for pr in range(NP2):
                        v_ = vd[:, UL * pr + u, :, :, :] if u < UL else gvd[:, u - UL, :, :, :]
                        mm = pe.matmul(bank[4 + u % 2][:, 72 * pr:72 * pr + 72], probT[:, u % 2, P * pr:P * pr + P],
                                       v_.rearrange("p b h o -> p (b h o)"), start=True, stop=True)
                    mm.then_inc(s_pv, 1)

                def remote(n):
                    free(m0_free, m0)
                    pe.wait_ge(s_p_att, n + 1)
                    pe.matmul(M0[:, 0:CH].rearrange("p (b i) -> p b i", i=32), w("rout"),
                              attT_flat.rearrange("p (b s i) -> p b s i", b=NB, s=2)[:, :, 1, :], start=True, stop=True).then_inc(s_rem, 1)

                def project(n):
                    pe.wait_ge(s_mix, n + 1)
                    free(m1_free, m1)
                    for t in range(2):
                        mm = pe.matmul(M1[:, P * t:P * t + P], mix[:, P * t:P * t + P], w("wout"), start=True, stop=True)
                    mm.then_inc(s_proj, 1)

                for ch in range(NCH):
                    n = b * NCH + ch
                    pe.wait_ge(s_xw, n + 1)
                    free(m0_free, m0)
                    pe.matmul(M0[:, 0:CH], w("wq"), xw[:, WIN:], start=True, stop=True)
                    pe.matmul(M0[0:64, CH:2 * CH], w("wgq", 64), xw[:, WIN:], start=True, stop=True).then_inc(s_p1, 1)
                    free(m1_free, m1)
                    pe.wait_ge(s_sum, n + 1)
                    pe.matmul(M1[:, 0:WIN + CH], w("wk"), xw[:], start=True, stop=True)
                    pe.matmul(M1[0:64, 320:384], w("wgk", 64), sumT[:], start=True, stop=True)
                    pe.matmul(M1[0:64, 384:448], sumT[:], w("wgv", 64), start=True, stop=True).then_inc(s_p2, 1)
                    free(m0_free, m0)
                    for pr in range(NP2):
                        for blk in range(2):
                            at_ = 64 * pr + WIN * blk
                            mm = pe.matmul(M0[64 * blk:64 * blk + 64, P * pr:P * pr + P], xw[:, at_:at_ + 64], w("wv"), start=True, stop=True)
                    mm.then_inc(s_p3, 1)
                    pe.wait_ge(s_p3, n + 1)
                    pe.sem_inc(xw_free, 1)
                    free(m1_free, m1)
                    for a in range(2):
                        mm = pe.matmul(M1[:, CH * a:CH * a + CH], gate_w[:, a, :], qT[:], start=True, stop=True)
                    mm.then_inc(s_p4, 1)
                    scores(ch, n, 0)
                    scores(ch, n, 1)
                    for u in range(U):
                        turn(n, u)
                        if u + 2 < U:
                            scores(ch, n, u + 2)
                        weigh(n, u)
                    remote(n)
                    project(n)

            def turn_rows(j0, k):
                for s in range(2):
                    kb = k[1] + s
                    pe.wait_ge(s_xg[kb % 4], 16 * (k[0] + kb // 4 + 1))
                    mm = pe.transpose(bank[0][:, P * s:P * s + P], xg[:, kb % 4, :], ident)
                mm.then_inc(s_tx, 1)

            turn_rows(0, (0, 0))

            def expert(q, k, single):
                if single and k >= E:
                    return
                e = 2 * q + k
                pe.wait_ge(s_we[k % 2], 32 * (q + k // 2 + 1))
                pe.wait_ge(s_xgT, e + 1)
                for f in range(4):
                    pe.matmul(bank[hidden_bank[f]][:, 0:2 * P], we[:, k % 2, P * f:P * f + P], xgT[:],
                              start=True, stop=True).then_inc(s_h, 1)
                if not single or k + 1 < E:
                    turn_rows(None, (q, 2 * (k + 1)))
                pe.wait_ge(s_gelu, 4 * e + 4)
                if not single or k:
                    pe.wait_ge(s_ysb, 2 * e)
                for s in range(2):
                    for f in range(4):
                        mm = pe.matmul(bank[(3, 6)[s]][:, 0:P], hT[:, f, P * s:P * s + P],
                                       we[:, k % 2, F0 + P * f:F0 + P * f + P], start=(f == 0), stop=(f == 3))
                    mm.then_inc(s_y, 1)

            expert_turns(pe, expert)

            turn_x(1)
            logits(1, "Wgate")
            prefix(1)
            inverse(1, 2 * T, J1, T)

            def sum_kv(t):
                pe.wait_ge(s_kf, t + 1)
                if t % 8 == 0 and t:
                    pe.wait_ge(s_kvd, t // 8)
                mm = pe.matmul(bank[2][:, 0:P + 1], kf[:, t % 2, :], vf[:, t % 2, :], start=(t % 8 == 0), stop=(t % 8 == 7))
                mm.then_inc(s_kvsum, 1)

            for b in range(B):
                for t in range(8 * b, 8 * b + 8):
                    if t >= 2:
                        pe.wait_ge(s_kmin, t - 1)
                    pe.matmul(bank[t % 2][:, 0:2 * P], x_tile_T(t), w("Wk", 2 * P), start=True, stop=True).then_inc(s_kv, 1)
                    if t % 8:
                        sum_kv(t - 1)
                sum_kv(8 * b + 7)
                pe.wait_ge(s_kvd, b + 1)
                for h in range(2):
                    m = 2 * b + h
                    pe.matmul(bank[3][:], w("Wq"), xnT[:, b, WIN + 512 * h:WIN + 512 * h + 512], start=True, stop=True).then_inc(s_qp, 1)
                    pe.wait_ge(s_qf, m + 1)
                    pe.matmul(bank[6][:], kvd[:], qf[:], start=True, stop=True)
                    pe.matmul(bank[7][:], ksd[:], qf[:], start=True, stop=True).then_inc(s_num, 1)
                    pe.wait_ge(s_aT, m + 1)
                    if m:
                        pe.wait_ge(s_x2, m)
                    for t in range(4):
                        mm = pe.matmul(bank[4][:, P * t:P * t + P], aT[:, P * t:P * t + P], w("Wo"), start=True, stop=True)
                    mm.then_inc(s_o1, 1)
            pe.wait_ge(s_w1, 32)
            pe.wait_ge(s_x2, 4)
            pe.wait_ge(s_xg[0], 16 * (J0 // 4 + 1))
            pe.transpose(bank[4][:, 0:P], xg[:, 0, :], ident).then_inc(t_x, 1)

            def weights(e, start, width):
                return w1s[:].rearrange("p e c -> p (e c)")[:, bass.ds(e * (W12 + WGL + W3) + start, width)]

            def expert_of(i):
                return pe.value_load(te[0:1, bass.ds(i, 1)], min_val=0, max_val=E - 1)

            def tile(q, k, single):
                i = 4 * q + k
                if not single or 1 <= k <= J1:
                    pe.wait_ge(t_z, i)
                    for a in range(2):
                        mm = pe.transpose(bank[2][:, P * a:P * a + P], z[:, P * a:P * a + P], ident)
                    mm.then_inc(t_zT, 1)
                if not single or 3 <= k < J1 + 3:
                    pe.wait_ge(t_o, i - 2)
                    for a in range(2):
                        mm = pe.transpose(bank[3][:, P * a:P * a + P], og[:, (k - 3) % 2, P * a:P * a + P], ident)
                    mm.then_inc(t_oT, 1)
                if not single or k < J1:
                    pe.wait_ge(t_xTs, i + 1)
                if not single or k + 1 < J1:
                    pe.wait_ge(s_xg[(k + 1) % 4], 16 * (q + J0 // 4 + (k + 1) // 4 + 1))
                    pe.transpose(bank[4][:, 0:P], xg[:, (k + 1) % 4, :], ident).then_inc(t_x, 1)
                if not single or k < J1:
                    pe.matmul(bank[0][:], xtT[:, k % 2, :], weights(expert_of(i), 0, W12), start=True, stop=True).then_inc(t_h, 1)
                if not single or 1 <= k <= J1:
                    e = expert_of(i - 1)
                    pe.wait_ge(t_zTs, i)
                    pe.wait_ge(t_gb, i - 1)
                    for a in range(2):
                        mm = pe.matmul(bank[1][:], zT[:, P * a:P * a + P], weights(e, W12 + 2 * F1 * a, 2 * F1), start=(a == 0), stop=(a == 1))
                    mm.then_inc(t_g, 1)
                if not single or 3 <= k < J1 + 3:
                    e = expert_of(i - 3)
                    pe.wait_ge(t_oTs, i - 2)
                    pe.wait_ge(t_ysb, i - 3)
                    for a in range(2):
                        mm = pe.matmul(bank[5][:, 0:P], oT[:, P * a:P * a + P], weights(e, W12 + WGL + P * a, P), start=(a == 0), stop=(a == 1))
                    mm.then_inc(t_y, 1)

            tile_turns(pe, tile)

        @block.vector
        def _(dve):
            own = Steps(dve, dve_own)

            def tt(o, a, b_, op):
                own(dve.tensor_tensor(o, a, b_, op))

            def ts(o, a, s1, op1, s2=None, op2=None):
                own(dve.tensor_scalar(o, a, s1, s2, op1, *(() if op2 is None else (op2,))))

            def stt(o, a, s, b_, op1, op2):
                own(dve.scalar_tensor_tensor(o, a, s, b_, op1, op2))

            def reduce(o, a, op):
                own(dve.tensor_reduce(o, a, X, op))

            def over_e(ap):
                return ap.unsqueeze(2).broadcast_to([P, T, E])

            def over_t(ap):
                return ap.unsqueeze(1).broadcast_to([P, T, E])

            def norm(layer):
                for i in range(4):
                    if layer == 0:
                        dve.wait_ge(s_x[i], 16)
                    for t in range(4 * i, 4 * i + 4):
                        own.mark(dve.bn_stats(stats[:, t, :], x[:, t, :]))
                own.wait()
                for t in range(T):
                    own.mark(dve.bn_aggr(mv[:, t, :], stats[:, t, :]))
                own.wait()
                ts(var[:], mv[:, :, 1], 1e-5, ALU.add)
                own.mark(dve.tensor_scalar(rstd[:].bitcast(I32), var[:].bitcast(I32), -0.5, float(0x5F3759DF), ALU.mult, ALU.add))
                ts(var[:], var[:], -0.5, ALU.mult)
                for _ in range(3):
                    tt(sq[:], rstd[:], rstd[:], ALU.mult)
                    tt(sq[:], sq[:], var[:], ALU.mult)
                    stt(rstd[:], sq[:], 1.5, rstd[:], ALU.add, ALU.mult)
                for t in range(T):
                    last = dve.tensor_scalar(xn[:, t, :], x[:, t, :], mv[:, t, 0:1], rstd[:, t:t + 1], ALU.subtract, ALU.mult)
                    own.mark(last) if t % 4 < 3 else last.then_inc(s_xn, 1)

            def best(m, ident_, one_hot):
                reduce(m, lg[:], ALU.max)
                tt(ta[:], lg[:], over_e(m), ALU.is_lt)
                stt(ta[:], ta[:], float(E), over_t(c("iota_e", E)), ALU.mult, ALU.add)
                reduce(ident_, ta[:], ALU.min)
                tt(one_hot, over_t(c("iota_e", E)), over_e(ident_), ALU.is_equal)

            def count(layer, choices):
                own(dve.tensor_copy(chosen[:].rearrange("p e t -> p t e"), choices))
                own(dve.tensor_tensor_scan(upto[:].rearrange("p e t -> p (e t)"), c("reset", P),
                                           chosen[:].rearrange("p e t -> p (e t)"), 0.0, ALU.mult, ALU.add))
                own.mark(dve.tensor_copy(chosen_bf[:], chosen[:]))
                own.mark(dve.tensor_copy(total_bf[:], upto[:, :, T - 1]))
                own.mark(dve.tensor_tensor(earlier_bf[:], upto[:], chosen[:], ALU.subtract))
                own.wait()
                dve.sem_inc(s_cnt, 1)
                dve.wait_ge(s_pos, layer + 1)
                own(dve.tensor_copy(pos[:].rearrange("p e t -> p (e t)"), bank[5][:, 0:P]))

            def own_position(one_hot, o):
                tt(ta[:], one_hot, pos[:].rearrange("p e t -> p t e"), ALU.mult)
                reduce(o, ta[:], ALU.add)

            def invert(layer, done, n, width, trash, frm, to):
                nk = n // T
                own(dve.tensor_copy(slot_i[:, 0:nk, :], slot[:, 0:nk, :]))
                own.mark(dve.tensor_scalar(lo_i[:, 0:nk, :], slot_i[:, 0:nk, :], P - 1, None, ALU.bitwise_and))
                own.mark(dve.tensor_scalar(hi_i[:, 0:nk, :], slot_i[:, 0:nk, :], 7, None, ALU.logical_shift_right))
                own.wait()
                own.mark(dve.tensor_copy(lo[:, 0:nk, :], lo_i[:, 0:nk, :]))
                own.mark(dve.tensor_copy(hi[:, 0:nk, :], hi_i[:, 0:nk, :]))
                own.wait()
                shape = [P, n, width]
                hit = is_hi[:].rearrange("p n j -> p (n j)")[:, 0:n * width].rearrange("p (n j) -> p n j", n=n)
                hi_n, lo_n = hi[:].rearrange("p k t -> p (k t)"), lo[:].rearrange("p k t -> p (k t)")
                tt(hit, c("iota_j", width).unsqueeze(1).broadcast_to(shape), hi_n[:, 0:n].unsqueeze(2).broadcast_to(shape), ALU.is_equal)
                own.mark(dve.tensor_tensor(ids_of(layer)[:, :, 0, :], hit, c("hi", n).unsqueeze(2).broadcast_to(shape), ALU.mult))
                own.mark(dve.tensor_scalar(ids_of(layer)[:, :, 1, :], hit, c("part", 1), None, ALU.mult))
                own.wait()
                for i in range(n):
                    if i >= 4:
                        dve.wait_ge(s_inv, done + i - 3)
                    dve.tensor_scalar(is_lo[:, i % 4, :], cbf("iota", P), lo_n[:, i:i + 1], None, ALU.is_equal).then_inc(s_islo, 1)
                dve.wait_ge(s_inv, done + n)
                own(dve.tensor_copy(inv[:, :, 0:width], bank[5][:, 0:2 * width].rearrange("p (a j) -> p a j", a=2)))
                stt(ra[:, 0:width], inv[:, 0, 0:width], float(P), inv[:, 1, 0:width], ALU.mult, ALU.add)
                ts(rocc[:, 0:width], ra[:, 0:width], float(P), ALU.is_ge)
                stt(rb[:, 0:width], ra[:, 0:width], float(P), trash, ALU.subtract, ALU.subtract)
                tt(rb[:, 0:width], rb[:, 0:width], rocc[:, 0:width], ALU.mult)
                own.mark(dve.tensor_tensor(to, rb[:, 0:width], trash, ALU.add))
                ts(ra[:, 0:width], ra[:, 0:width], float(P), ALU.subtract, 0.0, ALU.max)
                ts(rb[:, 0:width], ra[:, 0:width], float(N), ALU.is_ge, float(-N), ALU.mult)
                tt(frm, ra[:, 0:width], rb[:, 0:width], ALU.add)
                dve.sem_inc(s_route, 1)

            norm(0)
            dve.wait_ge(s_cst, 32)
            dve.wait_ge(s_wts, 16)
            own.mark(dve.tensor_scalar(gate_w[:, 0, :], c("heads_hgd", P), w("glw", 1), None, ALU.mult))
            own.mark(dve.tensor_scalar(gate_w[:, 1, :], c("heads_hgd", P), w("grw", 1), None, ALU.mult))
            own.wait()
            dve.sem_inc(s_gatew, 1)
            dve.wait_ge(s_lg, 1)
            own(dve.tensor_copy(lg[:].rearrange("p t e -> p (t e)"), bank[4][:, 0:T * E]))
            best(m1[:], id1[:], oh[:])
            tt(ta[:], lg[:], over_e(m1[:]), ALU.subtract)
            dve.sem_inc(s_gin, 1)
            dve.wait_ge(s_gexp, 1)
            reduce(esum[:], tb[:], ALU.add)
            own(dve.reciprocal(gate[:], esum[:]))
            count(0, oh[:])
            own_position(oh[:], own_pos[:])
            ts(keep[:], own_pos[:], float(CAP), ALU.is_lt)
            tt(gate[:], gate[:], keep[:], ALU.mult)
            stt(slot[:, 0, :], id1[:], float(CAP), own_pos[:], ALU.mult, ALU.add)
            ts(keep[:], keep[:], float(-2 * N), ALU.mult, float(2 * N), ALU.add)
            tt(slot[:, 0, :], slot[:, 0, :], keep[:], ALU.add)
            invert(0, 0, T, J0, c("trash0", J0), from0[:], to0[:])

            dve.wait_ge(s_zero, 11)
            for free in (m0_free, m1_free, xw_free):
                dve.sem_inc(free, 1)
            att = att_flat.rearrange("p (b s) -> p b s", b=NB)
            attT = attT_flat.rearrange("p (b s i) -> p b s i", b=NB, s=2)
            with dve.Fori(0, B) as b:
                for ch in range(NCH):
                    n = b * NCH + ch
                    un = n * U
                    dve.wait_ge(s_xw, n + 1)
                    dve.tensor_reduce(sumT[:, 16 * ch:16 * ch + 16], xw[:, WIN:].rearrange("p (n k) -> p n k", k=S // NLAT),
                                      X, ALU.add).then_inc(s_sum, 1)
                    dve.wait_ge(s_p3, n + 1)
                    for blk in range(2):
                        rows = slice(64 * blk, 64 * blk + 64)
                        last = dve.tensor_copy(vd[rows, :, blk, :, 0:HD], bank[6][rows, :].rearrange("p (c h d) -> p c h d", h=4, d=HD))
                    last.then_inc(m0_free, 1)
                    for u in range(U):
                        s3 = bank[u % 2][:].rearrange("p (b j) -> p b j", j=64)
                        dve.wait_ge(s_S, un + (u + 1))
                        if u >= 2:
                            dve.wait_ge(s_tr, un + (u - 1))
                        dve.tensor_reduce(rmax[:, u % 2, :], s3, X, ALU.max).then_inc(s_max, 1)
                        dve.wait_ge(s_max, un + (u + 1))
                        dve.tensor_tensor(prob[:, u % 2, :].rearrange("p (b j) -> p b j", j=64), s3,
                                          rmax[:, u % 2, :].unsqueeze(2).broadcast_to([P, NB, 64]), ALU.subtract).then_inc(s_sub, 1)
                    dve.wait_ge(m1_free, b * (3 * NCH) + (3 * ch + 3))
                    dve.tensor_scalar(sg[:], eg[:], 1.0, None, ALU.add).then_inc(s_g1, 1)
                    dve.wait_ge(s_g1, n * 5 + 1)
                    dve.reciprocal(sg[:], sg[:]).then_inc(s_g1, 1)
                    dve.wait_ge(s_oe, un + U)
                    for hh in range(4):
                        rows = slice(32 * hh, 32 * hh + 32)
                        last = dve.reciprocal(rsum[rows, :, :], oall[rows, :, :, hh, HD])
                    last.then_inc(s_g1, 1)
                    dve.wait_ge(s_g1, n * 5 + 3)
                    for hh in range(4):
                        rows = slice(32 * hh, 32 * hh + 32)
                        for u0, u1 in ((0, U),):
                            last = dve.tensor_tensor(
                                att[rows, :, 0:8 * U].rearrange("p b (u d) -> p u b d", d=HD),
                                oall[rows, :, :, hh, 0:HD],
                                rsum[rows, :, :].unsqueeze(3).broadcast_to([32, U, NB, HD]), ALU.mult)
                    last.then_inc(s_g1, 1)
                    dve.wait_ge(s_g1, n * 5 + 4)
                    dve.transpose(attT_flat, att_flat).then_inc(s_p_att, 1)
                    dve.wait_ge(s_p_att, n + 1)
                    dve.tensor_tensor(near[:].rearrange("p (b i) -> p b i", i=32), attT[:, :, 0, :],
                                      sg[:, 0, :].rearrange("p (b i) -> p b i", i=32), ALU.mult)
                    dve.wait_ge(s_rem, n + 1)
                    dve.tensor_tensor(mix[:], bank[6][:, 0:CH], sg[:, 1, :], ALU.mult).then_inc(s_g1, 1)
                    dve.wait_ge(s_g1, n * 5 + 5)
                    dve.tensor_tensor(mix[:], mix[:], near[:], ALU.add).then_inc(s_mix, 1)
                    dve.sem_inc(m0_free, 1)
                    dve.wait_ge(s_proj, n + 1)
                    xs = x[:, bass.ds(b * 8 + 2 * ch, 2), :]
                    dve.tensor_tensor(xs, xs, bank[7][:, 0:CH].rearrange("p (t d) -> p t d", d=P), ALU.add).then_inc(s_x1, 1)
                    dve.sem_inc(m1_free, 1)

            def expert(q, k, single):
                if single and k >= E:
                    return
                for s in range(2):
                    j, kb = 4 * q + (2 * k + s), 2 * k + s
                    dve.wait_ge(s_y, j + 1)
                    if not single or k >= 2:
                        dve.wait_ge(s_ys[kb % 4], 16 * (q + kb // 4))
                    dve.tensor_tensor(ysb[:, kb % 4, :], bank[(3, 6)[s]][:, 0:P], b2e[:, k % 2, :], ALU.add).then_inc(s_ysb, 1)

            expert_turns(dve, expert)
            for i in range(4):
                dve.wait_ge(s_y0[i], 16)
                for t in range(4 * i, 4 * i + 4):
                    own.mark(dve.scalar_tensor_tensor(x[:, t, :], xn[:, t, :], gate[:, t:t + 1], x[:, t, :], ALU.mult, ALU.add))
            own.wait()

            norm(1)
            dve.wait_ge(s_rows1, 16)
            dve.wait_ge(s_lg, 2)
            tt(lg[:], bank[4][:, 0:T * E].rearrange("p (t e) -> p t e", e=E), over_t(rows1[:, 3 * P:3 * P + E]), ALU.add)
            best(m1[:], id1[:], oh[:])
            stt(lg[:], oh[:], NEG, lg[:], ALU.mult, ALU.add)
            best(m2[:], id2[:], oh2[:])
            tt(e21[:], m2[:], m1[:], ALU.subtract)
            dve.sem_inc(s_gin, 1)
            tt(tb[:], oh[:], oh2[:], ALU.add)
            count(1, tb[:])
            own(dve.tensor_copy(cnt[:], bank[5][:, P:P + E]))
            tt(over[:], cnt[:].unsqueeze(2).broadcast_to([P, E, 16]), c("thresholds", 16).unsqueeze(1).broadcast_to([P, E, 16]), ALU.is_gt)
            reduce(tiles[:], over[:], ALU.add)
            own(dve.tensor_tensor_scan(tiles_end[:], c("thresholds_one", E), tiles[:], 0.0, ALU.mult, ALU.add))
            tt(base[:], tiles_end[:], tiles[:], ALU.subtract)
            ts(base[:], base[:], float(P), ALU.mult)
            tt(pos[:], pos[:], base[:].unsqueeze(2).broadcast_to([P, E, T]), ALU.add)
            own_position(oh[:], slot[:, 0, :])
            own_position(oh2[:], slot[:, 1, :])
            tt(passed[:], c("iota_j", J1).unsqueeze(2).broadcast_to([P, J1, E]),
               tiles_end[:].unsqueeze(1).broadcast_to([P, J1, E]), ALU.is_ge)
            reduce(te_f[:], passed[:], ALU.add)
            ts(te[:], te_f[:], float(E - 1), ALU.min)
            dve.wait_ge(s_gexp, 2)
            ts(w1c[:], e21[:], 1.0, ALU.add)
            own(dve.reciprocal(w1c[:], w1c[:]))
            tt(w2c[:], w1c[:], e21[:], ALU.mult)
            invert(1, T, 2 * T, J1, c("trash1", J1), from1[:], to1[:])

            dve.wait_ge(s_bo, 1)

            def feature_k(t):
                dve.wait_ge(s_kexp, t + 1)
                dve.scalar_tensor_tensor(kf[:, t % 2, :], kraw[:, t % 2, :], 0.0, kexp[:, t % 2, :], ALU.max, ALU.add).then_inc(s_kf, 1)

            for b_ in range(B):
                for t in range(8 * b_, 8 * b_ + 8):
                    dve.wait_ge(s_kv, t + 1)
                    if t >= 2:
                        dve.wait_ge(s_kvsum, t - 1)
                    own.mark(dve.tensor_tensor(kraw[:, t % 2, :], bank[t % 2][:, 0:P], rows1[:, 0:P], ALU.add))
                    own.mark(dve.tensor_tensor(vf[:, t % 2, 0:P], bank[t % 2][:, P:2 * P], rows1[:, P:2 * P], ALU.add))
                    own.wait(0)
                    dve.tensor_scalar(kmin[:, t % 2, :], kraw[:, t % 2, :], 0.0, None, ALU.min).then_inc(s_kmin, 1)
                    if t % 8:
                        feature_k(t - 1)
                feature_k(8 * b_ + 7)
                dve.wait_ge(s_kvsum, 8 * b_ + 8)
                own.mark(dve.tensor_copy(ksum[:], bank[2][:, P:P + 1]))
                own.mark(dve.tensor_tensor(kvd[:], bank[2][:, 0:P], c("heads", P), ALU.mult))
                own.wait(1)
                own(dve.tensor_scalar(ksd[:], c("heads", P), ksum[:], None, ALU.mult))
                dve.sem_inc(s_kvd, 1)
                for h in range(2):
                    m = 2 * b_ + h
                    dve.wait_ge(s_qp, m + 1)
                    own.mark(dve.tensor_scalar(qpos[:], bank[3][:], w("bq", 1), 0.0, ALU.add, ALU.max))
                    dve.tensor_scalar(qmin[:], bank[3][:], w("bq", 1), 0.0, ALU.add, ALU.min).then_inc(s_qmin, 1)
                    dve.wait_ge(s_qexp, m + 1)
                    dve.tensor_tensor(qf[:], qpos[:], qmin[:], ALU.add).then_inc(s_qf, 1)
                    dve.wait_ge(s_num, m + 1)
                    ts(den[:], bank[7][:], 1e-6, ALU.max)
                    own(dve.reciprocal(den[:], den[:]))
                    dve.tensor_tensor(aT[:], bank[6][:], den[:], ALU.mult).then_inc(s_aT, 1)
                    dve.wait_ge(s_o1, m + 1)
                    xs = x[:, 4 * m:4 * m + 4, :]
                    dve.tensor_tensor(xs, xs, bank[4][:].rearrange("p (t d) -> p t d", d=P), ALU.add).then_inc(s_x2, 1)

            dve.wait_ge(s_bias1, 16)

            def bias(i, start, width):
                e = dve.value_load(te[0:1, bass.ds(i, 1)], min_val=0, max_val=E - 1)
                return shared[:, bass.ds(e * BIAS1 + start, width)]

            def tile(q, k, single):
                i = 4 * q + k
                if not single or k < J1:
                    bias_h = bias(i, 0, 2 * F1)
                    dve.wait_ge(t_h, i + 1)
                    dve.tensor_tensor(h12[:], bank[0][:], bias_h, ALU.add).then_inc(t_hb, 1)
                    dve.wait_ge(t_hb, i + 1)
                    dve.tensor_tensor(z[:], h12[:, 0:F1], h12[:, F1:], ALU.mult).then_inc(t_z, 1)
                if not single or 2 <= k < J1 + 2:
                    dve.wait_ge(t_sil, i - 1)
                    if not single or k >= 4:
                        dve.wait_ge(t_oT, i - 3)
                    dve.tensor_tensor(og[:, k % 2, :], sil, hgl[:, F1:], ALU.mult).then_inc(t_o, 1)
                if not single or 1 <= k <= J1:
                    bias_g = bias(i - 1, 2 * F1, 2 * F1)
                    if not single or 2 <= k:
                        dve.wait_ge(t_o, i - 1)
                    dve.wait_ge(t_g, i)
                    dve.tensor_tensor(hgl[:], bank[1][:], bias_g, ALU.add).then_inc(t_gb, 1)
                if not single or 3 <= k < J1 + 3:
                    bias_y = bias(i - 3, 4 * F1, P)
                    dve.wait_ge(t_y, i - 2)
                    dve.wait_ge(s_ys[(k - 3) % 4], 16 * (q + (J0 // 4 + (k - 3) // 4)))
                    dve.tensor_tensor(ysb[:, (k - 3) % 4, :], bank[5][:, 0:P], bias_y, ALU.add).then_inc(t_ysb, 1)

            tile_turns(dve, tile)
            for b_ in range(B):
                dve.wait_ge(s_yk[b_], 32)
                for weight, src in ((w1c, xnT[:, b_, 0:S].rearrange("p (t d) -> p t d", d=P)), (w2c, xn[:, 8 * b_:8 * b_ + 8, :])):
                    for t in range(8):
                        tt_ = 8 * b_ + t
                        ins_ = dve.scalar_tensor_tensor(x[:, tt_, :], src[:, t, :], weight[:, tt_:tt_ + 1], x[:, tt_, :], ALU.mult, ALU.add)
                        own.mark(ins_)
                    own.wait()
                dve.sem_inc(s_res, 1)


def kernel(**inputs):
    from concourse import bacc
    from concourse.bass_utils import run_bass_kernel_spmd

    a = {k: np.asarray(v) for k, v in inputs.items()}
    order = [8 * (4 * g + hh) + d for hh in range(4) for g in range(4) for d in range(HD)]
    rout = np.zeros((P, P), np.float32)
    for hh in range(4):
        for g in range(UG):
            h = 4 * g + hh
            rout[32 * hh + 8 * g:32 * hh + 8 * g + 8] = a["L0_attn_r_out_w"][8 * h:8 * h + 8][:, order]
    wts = np.concatenate(
        [a["L0_attn_wq"], a["L0_attn_wk"], a["L0_attn_wv"], a["L0_attn_w_out"][order], rout,
         a["L1_attn_Wq"], a["L1_attn_Wk"], a["L1_attn_Wv"], a["L1_attn_Wo"],
         a["L0_attn_wgq"], a["L0_attn_wgk"], a["L0_attn_wgv"], a["L0_ffn_wg"], a["L1_ffn_Wgate"],
         a["L0_attn_gate_local_w"].reshape(P, 1), a["L0_attn_gate_remote_w"].reshape(P, 1), a["L1_attn_bq"].reshape(P, 1)], axis=1)

    def chunks(m, n):
        return m.reshape(E, n, P, -1).transpose(0, 2, 1, 3).reshape(E, P, -1)

    we = np.concatenate([a["L0_ffn_w1"], chunks(a["L0_ffn_w2"], 4), chunks(a["L0_ffn_b1"].reshape(E, F0, 1), 4)], axis=2)
    w1s = np.concatenate([a["L1_ffn_W1"], a["L1_ffn_W2"],
                          chunks(np.concatenate([a["L1_ffn_Wg"], a["L1_ffn_Wl"]], axis=2), 2), chunks(a["L1_ffn_W3"], 2)], axis=2)
    bias1 = np.concatenate([a["L1_ffn_" + n] for n in ("b1", "b2", "bg", "bl", "b3")], axis=1).reshape(1, -1)
    rows1 = np.concatenate([a["L1_attn_bk"], a["L1_attn_bv"], a["L1_attn_bo"], a["L1_ffn_bgate"]]).reshape(1, -1)
    cf, cb = constants()
    arrays = {"x": a["L0_attn_x"].reshape(N, P), "wts": wts, "cf": cf, "cb": cb, "we": we, "b2": a["L0_ffn_b2"],
              "w1s": w1s.transpose(1, 0, 2), "bias1": bias1, "rows1": rows1}
    arrays = {k: np.ascontiguousarray(v) for k, v in arrays.items()}
    nc = bacc.Bacc("TRN2", target_bir_lowering=False, num_devices=1)
    ins = {k: nc.dram_tensor(f"in_{k}", v.shape, mybir.dt.from_np(v.dtype), kind="ExternalInput").ap() for k, v in arrays.items()}
    out = nc.dram_tensor("out", (N, P), F32, kind="ExternalOutput").ap()
    program(nc, ins, out)
    r = run_bass_kernel_spmd(nc, [{f"in_{k}": v for k, v in arrays.items()}], core_ids=[0])
    return r.results[0]["out"].reshape(B, S, P)
```

```python
from contextlib import ExitStack

import numpy as np

import concourse.bass as bass
from concourse import mybir

F32 = mybir.dt.float32
BF16 = mybir.dt.bfloat16
I32 = mybir.dt.int32
U32 = mybir.dt.uint32
ALU = mybir.AluOpType
ACT = mybir.ActivationFunctionType
X = mybir.AxisListType.X

P = 128
B, S = 2, 1024
N = B * S
T = N // P
E = 8
WIN = 32
NLAT = 64
CH = 256
NCH = S // CH
NB = CH // WIN
NP2 = NB // 2
UL, UG = 4, 2
U = UL + UG
HD = 8
VW = HD + 1
NEG = -1e30
F0 = 512
CAP = N // E
J0 = E * CAP // P
F1 = 256
J1 = 2 * N // P + E - 1
W12, WGL, W3 = 2 * F1, 4 * F1, 2 * P
BIAS1 = 4 * F1 + P

WEIGHTS = ["wq", "wk", "wv", "wout", "rout", "Wq", "Wk", "Wv", "Wo"]
COL = {name: 128 * i for i, name in enumerate(WEIGHTS)}
at = 128 * len(WEIGHTS)
for name, width in (("wgq", 64), ("wgk", 64), ("wgv", 64), ("wg", 8), ("Wgate", 8), ("glw", 1), ("grw", 1), ("bq", 1)):
    COL[name] = at
    at += width
NW = at
CF = {}
at = 0
for name, width in (("ident", 128), ("heads", 128), ("heads_hgd", 128), ("mine", 4), ("iota_e", 8), ("iota_j", J1),
                    ("trash0", J0), ("trash1", J1), ("reset", 128), ("thresholds", 16), ("thresholds_one", E), ("part", 1), ("hi", 2 * T)):
    CF[name] = at
    at += width
NCF = at
CB = {}
at = 0
for name, width in (("before", 128), ("ones", 128), ("iota", 128), ("spread", 128), ("local", 7 * 64), ("first", NCH * 64), ("latent", NCH * 512)):
    CB[name] = at
    at += width
NCB = at


def constants():
    p = np.arange(P)
    f = {"ident": np.eye(P), "heads": p[:, None] // HD == p[None] // HD}
    c = np.arange(P)
    head_of = 4 * (c // 8 % 4) + c // 32
    f["heads_hgd"] = p[:, None] // HD == head_of[None]
    f["mine"] = (p[:, None] // HD % 4 == np.arange(4)[None]) / np.sqrt(np.float32(HD))
    f["iota_e"] = np.broadcast_to(np.arange(E), (P, E))
    f["iota_j"] = np.broadcast_to(np.arange(J1), (P, J1))
    f["trash0"] = N + P * np.arange(J0)[None] + p[:, None]
    f["trash1"] = 2 * N + P * np.arange(J1)[None] + p[:, None]
    f["reset"] = np.broadcast_to(np.arange(P) % T != 0, (P, P))
    f["thresholds"] = np.broadcast_to(P * np.arange(16), (P, 16))
    f["thresholds_one"] = np.ones((P, E))
    f["part"] = p[:, None]
    f["hi"] = np.broadcast_to(1 + np.arange(2 * T), (P, 2 * T))
    b = {"before": p[:, None] < p[None], "ones": np.ones((P, P)), "iota": np.broadcast_to(p, (P, P))}
    i = p[:, None] % WIN
    b["spread"] = p[:, None] == p[None] % WIN
    j = np.arange(64)[None]
    local = (j > i) & (j <= i + WIN)
    b["local"] = np.where(np.tile(local, (1, NB - 1)), 0, NEG)
    b["first"] = np.where(np.concatenate([local & (j >= WIN)] + [local] * (NCH - 1), 1), 0, NEG)
    s = 32 * (np.arange(4 * 512)[None] // 64) + i
    b["latent"] = np.where(np.arange(4 * 512)[None] % 64 <= s // (S // NLAT), 0, NEG)
    cf, cb = np.zeros((P, NCF), np.float32), np.zeros((P, NCB), mybir.dt.np(BF16))
    for src, dst, cols in ((f, cf, CF), (b, cb, CB)):
        for k, v in src.items():
            dst[:, cols[k]:cols[k] + v.shape[1]] = v
    return cf, cb


class Steps:

    def __init__(self, eng, sem):
        self.eng, self.sem, self.n, self.base = eng, sem, 0, 0

    def __call__(self, ins):
        self.mark(ins)
        self.wait()

    def mark(self, ins):
        ins.then_inc(self.sem, 1)
        self.n += 1

    def wait(self, back=0):
        self.eng.wait_ge(self.sem, self.base + (self.n - back))


def turns(eng, step, peel, trips, unroll, total):
    for i in range(peel):
        step(0, i, True)
    with eng.Fori(0, trips) as q:
        for k in range(peel, peel + unroll):
            step(q, k, False)
    for i in range(peel + trips * unroll, total):
        step(0, i, True)


def attention_turns(eng, step):
    turns(eng, step, 1, 3, 2, B * NCH)


def expert_turns(eng, step):
    turns(eng, step, 2, 2, 2, E + 1)


def tile_turns(eng, step):
    turns(eng, step, 4, 8, 4, J1 + 4)


def program(nc, ins, out):
    ctx = ExitStack()

    def sb(name, shape, dt=F32):
        return ctx.enter_context(nc.sbuf_tensor(name, shape, dt))

    def sem(name):
        return ctx.enter_context(nc.semaphore(name))

    def dram(name, rows):
        return nc.dram_tensor(name, [rows, P], F32, kind="Internal").ap()

    xn0_rows, xn1_rows = dram("xn0_rows", N), dram("xn1_rows", N)
    y0_rows = dram("y0_rows", N + J0 * P)
    y1_rows = dram("y1_rows", 2 * N + J1 * P)

    with ctx:
        wts, cf, cb = sb("wts", [P, NW]), sb("cf", [P, NCF]), sb("cb", [P, NCB], BF16)
        rows1 = sb("rows1", [P, 3 * P + E])
        x = sb("x", [P, T, P])
        xn = sb("xn", [P, T, P])
        xnT = sb("xnT", [P, B, WIN + S])
        stats, mv, var, sq, rstd = sb("stats", [P, T, 6]), sb("mv", [P, T, 2]), sb("var", [P, T]), sb("sq", [P, T]), sb("rstd", [P, T])
        gate_w = sb("gate_w", [P, 2, P])
        lg, oh, oh2 = sb("lg", [P, T, E]), sb("oh", [P, T, E]), sb("oh2", [P, T, E])
        ta, tb = sb("ta", [P, T, E]), sb("tb", [P, T, E])
        chosen, upto = sb("chosen", [P, E, T]), sb("upto", [P, E, T])
        chosen_bf, earlier_bf = sb("chosen_bf", [P, E, T], BF16), sb("earlier_bf", [P, E, T], BF16)
        total_bf = sb("total_bf", [P, E], BF16)
        pos = sb("pos", [P, E, T])
        m1, m2, id1, id2, esum, gate, keep, w1c, w2c, e21, own_pos = (
            sb("r_" + n, [P, T]) for n in ("m1", "m2", "id1", "id2", "esum", "gate", "keep", "w1c", "w2c", "e21", "own_pos"))
        slot, lo, hi = sb("slot", [P, 2, T]), sb("lo", [P, 2, T]), sb("hi", [P, 2, T])
        slot_i, lo_i, hi_i = sb("slot_i", [P, 2, T], I32), sb("lo_i", [P, 2, T], I32), sb("hi_i", [P, 2, T], I32)
        is_lo = sb("is_lo", [P, 4, P], BF16)
        is_hi = sb("is_hi", [P, 2 * T, J1])
        ids = sb("ids", [P, 2 * T, 2, J1], BF16)
        cnt, tiles, tiles_end, base = (sb("e_" + n, [P, E]) for n in ("cnt", "tiles", "end", "base"))
        over = sb("over", [P, E, 16])
        passed = sb("passed", [P, J1, E])
        te_f, te = sb("te_f", [P, J1]), sb("te", [P, J1], I32)
        inv, ra, rb = sb("inv", [P, 2, J1]), sb("ra", [P, J1]), sb("rb", [P, J1])
        rocc = sb("rocc", [P, J1])
        from0, to0 = sb("from0", [P, J0], I32), sb("to0", [P, J0], I32)
        from1, to1 = sb("from1", [P, J1], I32), sb("to1", [P, J1], I32)
        xw, sumT = sb("xw", [P, NB, 2 * WIN]), sb("sumT", [P, B, NLAT])
        qT, kT, gkT = sb("qT", [P, CH]), sb("kT", [P, B, WIN + CH]), sb("gkT", [64, NLAT])
        shared = sb("shared", [P, E * BIAS1])
        bias1 = shared[:].rearrange("p (e c) -> p e c", e=E)
        off = [0]

        def part(*dims):
            n = int(np.prod(dims))
            ap = shared[:, off[0]:off[0] + n]
            off[0] += n
            return ap

        qd = part(NB, 4, WIN).rearrange("p (b h i) -> p b h i", b=NB, h=4)
        gqd = part(NB, 4, WIN).rearrange("p (b h i) -> p b h i", b=NB, h=4)
        vd_flat, gvd_flat = part(NP2, UL, 2, 4, VW), part(UG, 2, 4, VW)
        vd = vd_flat.rearrange("p (c b h o) -> p c b h o", c=NP2 * UL, b=2, h=4)
        gvd = gvd_flat.rearrange("p (g b h o) -> p g b h o", g=UG, b=2, h=4)
        prob, probT = (part(2, 512).rearrange("p (r n) -> p r n", r=2) for _ in range(2))
        oall_flat = part(U, NB, 4, VW)
        oall = oall_flat.rearrange("p (u b h o) -> p u b h o", u=U, b=NB, h=4)
        att_flat, attT_flat = part(NB, 2, 32), part(NB, 2, 32)
        rmax, rsum = sb("rmax", [P, 2, NB]), sb("rsum", [P, U, NB])
        eg, sg = sb("eg", [P, 2, CH]), sb("sg", [P, 2, CH])
        near, mix = sb("near", [P, CH]), sb("mix", [P, CH])
        we = sb("we", [P, 2, 2 * F0 + 4])
        b2e = sb("b2e", [P, 2, P])
        xg, xgT = sb("xg", [P, 4, P]), sb("xgT", [P, 2 * P])
        hT = sb("hT", [P, 4, 2 * P])
        ysb = sb("ysb", [P, 4, P])

        ig, isc = sb("ig", [P, 4], I32), sb("isc", [P, 4], I32)
        w1s = sb("w1s", [P, E, W12 + WGL + W3])
        kraw, kmin, kexp, kf = (sb(n, [P, 2, P]) for n in ("kraw", "kmin", "kexp", "kf"))
        vf = sb("vf", [P, 2, P + 1])
        kvd, ksd, ksum = sb("kvd", [P, P]), sb("ksd", [P, P]), sb("ksum", [P, 1])
        qpos, qmin, qf, den, aT = (sb(n, [P, 512]) for n in ("qpos", "qmin", "qf", "den", "aT"))
        xtT = sb("xtT", [P, 2, P])
        z, zT, oT = sb("z", [P, F1]), sb("zT", [P, F1]), sb("oT", [P, F1])
        zeros, h12, hgl, sil, og = qmin, aT, qpos, den[:, 0:F1], qf[:].rearrange("p (r f) -> p r f", r=2)

        bank = [ctx.enter_context(nc.psum_tensor(f"bank{i}", [P, 512], F32)) for i in range(8)]

        hidden_bank = (1, 2, 4, 5)

        def w(name, width=P):
            return wts[:, COL[name]:COL[name] + width]

        def c(name, width):
            return cf[:, CF[name]:CF[name] + width]

        def cbf(name, width, start=0):
            return cb[:, CB[name] + start:CB[name] + start + width]

        ident = c("ident", P)

        s_x = [sem(f"x_in{i}") for i in range(4)]
        s_cst, s_wts, s_rows1 = sem("constants_in"), sem("weights_in"), sem("rows1_in")
        s_w1, s_bias1 = sem("w1_in"), sem("bias1_in")
        dve_own, pool_own = sem("dve_own"), sem("pool_own")
        s_zero, s_y0z, s_xn, s_xt, s_xTs, s_xnd = (sem(n) for n in (
            "buffers_filled", "y0_zeroed", "xn_ready", "x_turned", "xnT_ready", "xn_in_dram"))
        s_lg, s_gin, s_gexp, s_cnt, s_pos, s_posread, s_islo, s_inv, s_route = (sem(n) for n in (
            "logits", "gate_in", "gate_exp", "choices_ready", "positions", "positions_read", "is_lo_ready", "inverse",
            "routed"))
        s_gatew, s_xw, s_sum, s_p1, s_p2, s_gkv, s_p3, s_p4 = (sem(n) for n in (
            "gate_w_ready", "xw_ready", "sums_ready", "qk_made", "latent_q_made", "latents_made", "v_made", "gates_made"))
        s_qd, s_gqd, s_kend, s_kT, s_gk, s_vd, s_eg, s_sg = (sem(n) for n in (
            "qd_ready", "gqd_ready", "k_end_kept", "kT_ready", "latents_ready", "vd_ready", "eg_ready", "sg_ready"))
        s_S, s_max, s_sub, s_exp, s_tr, s_pte, s_pv, s_oe = (sem(n) for n in (
            "scores", "maxima", "shifted", "probs", "probs_turned", "probT_ready", "weighted", "weighted_out"))
        s_g1, s_p_att, s_rsum, s_att, s_rem, s_m0read, s_mix, s_proj, s_x1 = (sem(n) for n in (
            "gates_plus_one", "attT_ready", "rsum_ready", "att_ready", "remote_made", "remote_read", "mixed", "projected", "x_added"))
        s_we = [sem(f"we_in{i}") for i in range(2)]
        s_xg = [sem(f"rows_in{i}") for i in range(4)]
        s_ys = [sem(f"rows_out{i}") for i in range(4)]
        s_ig, s_isc, s_index_seen = sem("gather_index"), sem("scatter_index"), sem("index_seen")
        s_tx, s_xgT, s_h, s_gelu, s_y, s_ysb = (sem(n) for n in (
            "rows_turned", "rowsT_ready", "hidden", "gelu_done", "y_made", "y_ready"))
        s_y0 = [sem(f"y0_back{i}") for i in range(4)]
        s_bo, s_kv, s_kmin, s_kexp, s_kf, s_kvsum, s_kvd = (sem(n) for n in (
            "bo_added", "kv_made", "kmin_ready", "kexp_ready", "kf_ready", "kv_summed", "kvd_ready"))
        s_qp, s_qmin, s_qexp, s_qf, s_num, s_aT, s_o1, s_x2 = (sem(n) for n in (
            "q1_made", "qmin_ready", "qexp_ready", "qf_ready", "num_made", "aT_ready", "att1_made", "x2_added"))
        t_x, t_xTs, t_h, t_hb, t_z, t_zT, t_zTs, t_g, t_gb, t_sil, t_o, t_oT, t_oTs, t_y, t_ysb = (
            sem("t_" + n) for n in ("x", "xTs", "h", "hb", "z", "zT", "zTs", "g", "gb", "sil", "o", "oT", "oTs", "y", "ysb"))
        s_yk = [sem(f"y1_back{i}") for i in range(2)]
        s_res, s_out = sem("result"), sem("out_done")

        block = ctx.enter_context(nc.Block())

        def ids_of(layer):
            n, width = ((T, J0), (2 * T, J1))[layer]
            return ids[:].rearrange("p n a j -> p (n a j)")[:, 0:n * 2 * width].rearrange("p (n a j) -> p n a j", n=n, a=2)

        def x_tile_T(t):
            b, o = divmod(t * P, S)
            return xnT[:, b, WIN + o:WIN + o + P]

        @block.sync
        def _(sp):
            xv = ins["x"].rearrange("(t p) d -> p t d", p=P)
            for i in range(4):
                sp.dma_start(x[:, 4 * i:4 * i + 4, :], xv[:, 4 * i:4 * i + 4, :]).then_inc(s_x[i], 16)
            sp.dma_start(wts[:], ins["wts"]).then_inc(s_wts, 16)
            xd = xn0_rows.rearrange("(t p) d -> p t d", p=P)
            for i in range(4):
                sp.wait_ge(s_xn, i + 1)
                sp.dma_start(xd[:, 4 * i:4 * i + 4, :], xn[:, 4 * i:4 * i + 4, :]).then_inc(s_xnd, 16)
            for e in range(2):
                sp.dma_start(we[:, e, :], ins["we"][e]).then_inc(s_we[e], 16)
                sp.dma_start(b2e[:, e, :], ins["b2"][e:e + 1, :].partition_broadcast(P)).then_inc(s_we[e], 16)
            for i in range(2):
                sp.dma_start(w1s[:, E // 2 * i:E // 2 * (i + 1), :], ins["w1s"][:, E // 2 * i:E // 2 * (i + 1), :]).then_inc(s_w1, 16)
            for e in range(2, E):
                sp.wait_ge(s_y, 2 * (e - 1))
                sp.dma_start(we[:, e % 2, :], ins["we"][e]).then_inc(s_we[e % 2], 16)
                sp.wait_ge(s_ysb, 2 * (e - 1))
                sp.dma_start(b2e[:, e % 2, :], ins["b2"][e:e + 1, :].partition_broadcast(P)).then_inc(s_we[e % 2], 16)
            for k in range(4):
                sp.wait_ge(s_ys[k], 16 * (J0 // 4))
            yd = y0_rows[0:N, :].rearrange("(t p) d -> p t d", p=P)
            for i in range(4):
                sp.dma_start(xn[:, 4 * i:4 * i + 4, :], yd[:, 4 * i:4 * i + 4, :]).then_inc(s_y0[i], 16)
            xd = xn1_rows.rearrange("(t p) d -> p t d", p=P)
            for i in range(4):
                sp.wait_ge(s_xn, 4 + i + 1)
                sp.dma_start(xd[:, 4 * i:4 * i + 4, :], xn[:, 4 * i:4 * i + 4, :]).then_inc(s_xnd, 16)
            for k in range(4):
                sp.wait_ge(s_ys[k], 16 * (J0 // 4 + (J1 - k + 3) // 4))
            yd = y1_rows[0:2 * N, :].rearrange("(k t p) d -> k p t d", k=2, p=P)
            for b in range(B):
                sp.dma_start(xnT[:, b, 0:S].rearrange("p (t d) -> p t d", d=P), yd[0, :, 8 * b:8 * b + 8, :]).then_inc(s_yk[b], 16)
                sp.dma_start(xn[:, 8 * b:8 * b + 8, :], yd[1, :, 8 * b:8 * b + 8, :]).then_inc(s_yk[b], 16)
            ov = out.rearrange("(t p) d -> p t d", p=P)
            for b in range(B):
                sp.wait_ge(s_res, b + 1)
                sp.dma_start(ov[:, 8 * b:8 * b + 8, :], x[:, 8 * b:8 * b + 8, :]).then_inc(s_out, 16)
            sp.wait_ge(s_out, 16 * B)

        @block.gpsimd
        def _(pool):
            pool.memset(xnT[:, :, 0:WIN], 0.0).then_inc(s_zero, 1)
            pool.memset(sumT[:], 0.0).then_inc(s_zero, 1)
            pool.memset(zeros[:], 0.0).then_inc(s_zero, 1)
            pool.memset(att_flat, 0.0).then_inc(s_zero, 1)
            pool.memset(vd_flat, 0.0).then_inc(s_zero, 1)
            pool.memset(gvd_flat, 0.0).then_inc(s_zero, 1)
            pool.memset(vf[:, :, P:P + 1], 1.0).then_inc(s_zero, 1)
            pool.memset(kT[:, :, 0:WIN], 0.0).then_inc(s_zero, 1)
            pool.wait_ge(s_zero, 8)
            for blk in range(2):
                rows = slice(64 * blk, 64 * blk + 64)
                pool.memset(vd[rows, :, blk, :, HD], 1.0).then_inc(s_zero, 1)
                pool.memset(gvd[rows, :, blk, :, HD], 1.0).then_inc(s_zero, 1)
            zrows = y0_rows[0:N, :].rearrange("(p r) d -> p (r d)", p=P)
            for i in range(4):
                pool.dma_start(zrows[:, 512 * i:512 * i + 512], zeros[:]).then_inc(s_y0z, 16)
            pool.wait_ge(s_zero, 12)
            pool.wait_ge(s_xTs, 4)

            def windows(q, k, single):
                n = 2 * q + k
                b, start = k % B, (q + k // 2) * CH
                if not single or k:
                    pool.wait_ge(s_p3, n)
                for half in range(2):
                    src = xnT[:, b, WIN * half:].rearrange("p s -> p s")[:, bass.ds(start, CH)]
                    pool.tensor_copy(xw[:, :, WIN * half:WIN * half + WIN], src.rearrange("p (b i) -> p b i", i=WIN)).then_inc(s_xw, 1)

            attention_turns(pool, windows)

            def gather(src, frm, j, k):
                slot_b = k[1] % 4
                pool.tensor_copy(ig[:, slot_b:slot_b + 1], frm[:, bass.ds(j, 1)]).then_inc(s_ig, 1)
                pool.wait_ge(s_ig, k[0] + 1)
                pool.sem_inc(s_index_seen, 1)
                pool.indirect_dma_start(
                    out=xg[:, slot_b, :], out_offset=None, in_=src,
                    in_offset=bass.IndirectOffsetOnAxis(ap=ig[:, slot_b:slot_b + 1].bitcast(U32), axis=0)
                ).then_inc(s_xg[slot_b], 16)

            def scatter(dst, to, j, k):
                slot_b = k[1] % 4
                pool.tensor_copy(isc[:, slot_b:slot_b + 1], to[:, bass.ds(j, 1)]).then_inc(s_isc, 1)
                pool.wait_ge(s_isc, k[0] + 1)
                pool.sem_inc(s_index_seen, 1)
                pool.indirect_dma_start(
                    out=dst, in_=ysb[:, slot_b, :], in_offset=None,
                    out_offset=bass.IndirectOffsetOnAxis(ap=isc[:, slot_b:slot_b + 1].bitcast(U32), axis=0)
                ).then_inc(s_ys[slot_b], 16)

            pool.wait_ge(s_cst, 32)
            pool.wait_ge(s_route, 1)
            pool.wait_ge(s_xnd, 64)
            pool.wait_ge(s_y0z, 64)
            for j in range(2):
                gather(xn0_rows, from0, j, (j, j))

            def expert(q, k, single):
                e = 2 * q + k
                if not single or k + 1 < E:
                    pool.wait_ge(s_tx, e)
                    for s in range(2):
                        j = 4 * q + (2 * (k + 1) + s)
                        gather(xn0_rows, from0, j, (j, 2 * (k + 1) + s))
                if not single or k >= 1:
                    for s in range(2):
                        j = 4 * q + (2 * (k - 1) + s)
                        pool.wait_ge(s_ysb, j + 1)
                        scatter(y0_rows, to0, j, (j, 2 * (k - 1) + s))

            expert_turns(pool, expert)
            pool.wait_ge(s_rows1, 16)
            pool.wait_ge(s_xn, 8)
            pool.tensor_tensor(x[:], x[:], rows1[:, 2 * P:3 * P].unsqueeze(1).broadcast_to([P, T, P]), ALU.add).then_inc(s_bo, 1)
            pool.wait_ge(s_route, 2)
            pool.wait_ge(s_xnd, 128)
            for j in range(3):
                gather(xn1_rows, from1, j, (J0 + j, j))

            def tile(q, k, single):
                i = 4 * q + k
                if not single or k + 3 < J1:
                    pool.wait_ge(t_x, i)
                    gather(xn1_rows, from1, i + 3, (J0 + i + 3, k + 3))
                if not single or 4 <= k:
                    pool.wait_ge(t_ysb, i - 3)
                    scatter(y1_rows, to1, i - 4, (J0 + i - 4, k - 4))

            tile_turns(pool, tile)

        @block.scalar
        def _(act):
            act.dma_start(cf[:], ins["cf"]).then_inc(s_cst, 16)
            act.dma_start(cb[:], ins["cb"]).then_inc(s_cst, 16)
            act.dma_start(rows1[:], ins["rows1"].partition_broadcast(P)).then_inc(s_rows1, 16)

            def evacuate_xT(layer):
                for i in range(4):
                    b, o = divmod(512 * i, S)
                    act.wait_ge(s_xt, 4 * layer + i + 1)
                    act.copy(xnT[:, b, WIN + o:WIN + o + 512], bank[i % 2][:]).then_inc(s_xTs, 1)

            def gate_exp(layer, n, src):
                act.wait_ge(s_gin, layer + 1)
                act.activation(n, src, ACT.Exp).then_inc(s_gexp, 1)

            evacuate_xT(0)
            gate_exp(0, tb[:], ta[:])
            act.wait_ge(s_cst, 32)
            act.wait_ge(s_zero, 12)

            def queries(n):
                act.wait_ge(s_p1, n + 1)
                for hh in range(4):
                    act.activation(qd[:, :, hh, :], bank[6][:, 0:CH].rearrange("p (b i) -> p b i", i=WIN), ACT.Copy,
                                   scale=c("mine", 4)[:, hh:hh + 1])
                act.copy(qT[:], bank[6][:, 0:CH]).then_inc(s_qd, 1)

            def latent_queries(n):
                act.wait_ge(s_p2, n + 1)
                for hh in range(4):
                    last = act.activation(gqd[0:64, :, hh, :], bank[7][0:64, 0:CH].rearrange("p (b i) -> p b i", i=WIN),
                                          ACT.Copy, scale=c("mine", 4)[0:64, hh:hh + 1])
                last.then_inc(s_gqd, 1)

            def keys(n, b, end=True):
                if end:
                    act.copy(kT[:, b, 0:WIN], kT[:, b, CH:]).then_inc(s_kend, 1)
                    act.wait_ge(s_kend, n - 1)
                act.copy(kT[:, b, WIN:], bank[6][:, CH:2 * CH]).then_inc(s_kT, 1)

            def latents(n):
                act.wait_ge(s_gkv, n + 1)
                act.activation(gkT[0:64, :], bank[7][0:64, 0:NLAT], ACT.Copy, scale=NLAT / S)
                for blk in range(2):
                    last = act.activation(gvd[64 * blk:64 * blk + 64, :, blk, :, 0:HD],
                                          bank[7][0:64, 64:128].rearrange("p (g h d) -> p g h d", g=UG, h=4), ACT.Copy, scale=NLAT / S)
                last.then_inc(s_gk, 1)

            def gates(n, wait=True):
                act.wait_ge(s_p4, n + 1)
                if wait:
                    act.wait_ge(s_g1, n)
                act.activation(eg[:], bank[7][:].rearrange("p (a c) -> p a c", a=2), ACT.Exp, scale=-1.0).then_inc(s_eg, 1)

            def exponent(un, u):
                act.wait_ge(s_sub, un + (u + 1))
                act.activation(prob[:, u % 2, :], prob[:, u % 2, :], ACT.Exp).then_inc(s_exp, 1)

            def turned(un, u):
                act.wait_ge(s_tr, un + (u + 1))
                act.copy(probT[:, u % 2, :], bank[2 + u % 2][:]).then_inc(s_pte, 1)

            def weighted(un, u):
                act.wait_ge(s_pv, un + (u + 1))
                act.copy(oall_flat.rearrange("p (u n) -> p u n", u=U)[:, u % U, :], bank[4 + u % 2][:, 0:288]).then_inc(s_oe, 1)

            queries(0)
            keys(0, 0, end=False)
            latent_queries(0)
            gates(0, wait=False)
            exponent(0, 0)
            exponent(0, 1)

            def attend(q, k, single):
                n = 2 * q + k
                un = n * U
                before, after = not single or k > 0, not single or k < B * NCH - 1
                turned(un, 0)
                if before:
                    weighted(un, -1)
                latents(n)
                exponent(un, 2)
                turned(un, 1)
                exponent(un, 3)
                turned(un, 2)
                if after:
                    queries(n + 1)
                if before:
                    act.wait_ge(s_att, n)
                weighted(un, 0)
                weighted(un, 1)
                exponent(un, 4)
                turned(un, 3)
                weighted(un, 2)
                if after:
                    keys(n + 1, (k + 1) % B, end=before)
                exponent(un, 5)
                turned(un, 4)
                weighted(un, 3)
                if after:
                    latent_queries(n + 1)
                    exponent(un, 6)
                turned(un, 5)
                weighted(un, 4)
                if after:
                    gates(n + 1)
                    exponent(un, 7)
                else:
                    weighted(un, 5)

            attention_turns(act, attend)
            act.wait_ge(s_x1, B * NCH)
            act.dma_start(shared[:], ins["bias1"].partition_broadcast(P)).then_inc(s_bias1, 16)
            act.wait_ge(s_tx, 1)
            act.copy(xgT[:], bank[0][:, 0:2 * P]).then_inc(s_xgT, 1)

            def expert(q, k, single):
                if single and k >= E:
                    return
                e = 2 * q + k
                for f in range(4):
                    act.wait_ge(s_h, 4 * e + (f + 1))
                    act.activation(hT[:, f, :], bank[hidden_bank[f]][:, 0:2 * P], ACT.Gelu_apprx_tanh,
                                   bias=we[:, k % 2, 2 * F0 + f:2 * F0 + f + 1]).then_inc(s_gelu, 1)
                if not single or k + 1 < E:
                    act.wait_ge(s_tx, e + 2)
                    act.copy(xgT[:], bank[0][:, 0:2 * P]).then_inc(s_xgT, 1)

            expert_turns(act, expert)
            evacuate_xT(1)
            act.wait_ge(s_gin, 2)
            act.activation(e21[:], e21[:], ACT.Exp).then_inc(s_gexp, 1)
            for t in range(T):
                act.wait_ge(s_kmin, t + 1)
                act.activation(kexp[:, t % 2, :], kmin[:, t % 2, :], ACT.Exp).then_inc(s_kexp, 1)
                if t % 8 == 7:
                    for h in range(2):
                        act.wait_ge(s_qmin, t // 8 * 2 + h + 1)
                        act.activation(qmin[:], qmin[:], ACT.Exp).then_inc(s_qexp, 1)
            act.wait_ge(t_x, 1)
            act.copy(xtT[:, 0, :], bank[4][:, 0:P]).then_inc(t_xTs, 1)

            def tile(q, k, single):
                i = 4 * q + k
                if not single or 1 <= k <= J1:
                    act.wait_ge(t_zT, i)
                    act.copy(zT[:], bank[2][:, 0:F1]).then_inc(t_zTs, 1)
                if not single or 3 <= k < J1 + 3:
                    act.wait_ge(t_oT, i - 2)
                    act.copy(oT[:], bank[3][:, 0:F1]).then_inc(t_oTs, 1)
                if not single or k + 1 < J1:
                    act.wait_ge(t_x, i + 2)
                    act.copy(xtT[:, (k + 1) % 2, :], bank[4][:, 0:P]).then_inc(t_xTs, 1)
                if not single or 1 <= k <= J1:
                    act.wait_ge(t_gb, i)
                    act.activation(sil, hgl[:, 0:F1], ACT.Silu).then_inc(t_sil, 1)

            tile_turns(act, tile)

        @block.tensor
        def _(pe):
            pe.wait_ge(s_cst, 32)

            def turn_x(layer):
                for i in range(4):
                    pe.wait_ge(s_xn, 4 * layer + i + 1)
                    if i >= 2:
                        pe.wait_ge(s_xTs, 4 * layer + i - 1)
                    for k in range(4):
                        mm = pe.transpose(bank[i % 2][:, P * k:P * k + P], xn[:, 4 * i + k, :], ident)
                    mm.then_inc(s_xt, 1)

            def logits(layer, name):
                pe.wait_ge(s_wts, 16)
                for t in range(T):
                    pe.wait_ge(s_xTs, 4 * layer + t // 4 + 1)
                    mm = pe.matmul(bank[4][:, E * t:E * t + E], x_tile_T(t), w(name, E), start=True, stop=True)
                mm.then_inc(s_lg, 1)

            def prefix(layer):
                pe.wait_ge(s_cnt, layer + 1)
                pe.matmul(bank[5][:, 0:P], cbf("before", P), chosen_bf[:].rearrange("p e t -> p (e t)"), start=True, stop=False)
                pe.matmul(bank[5][:, 0:P], cbf("ones", P), earlier_bf[:].rearrange("p e t -> p (e t)"), start=False, stop=True)
                pe.matmul(bank[5][:, P:P + E], cbf("ones", P), total_bf[:], start=True, stop=True).then_inc(s_pos, 1)

            def inverse(layer, n, width, done):
                for i in range(n):
                    pe.wait_ge(s_islo, done + i + 1)
                    pe.matmul(bank[5][:, 0:2 * width], is_lo[:, i % 4, :], ids_of(layer)[:, i, :, :],
                              start=(i == 0), stop=(i == n - 1)).then_inc(s_inv, 1)

            turn_x(0)
            logits(0, "wg")
            prefix(0)
            inverse(0, T, J0, 0)
            pe.wait_ge(s_zero, 12)
            pe.wait_ge(s_gatew, 1)
            M0, M1 = bank[6], bank[7]

            def tokens(n, start, width):
                q, k = n
                return xnT[:, k % B, :][:, bass.ds((q + k // 2) * CH + start, width)]

            def queries_keys(n, m, free=True):
                if free:
                    pe.wait_ge(s_vd, m)
                pe.matmul(M0[:, 0:CH], w("wq"), tokens(n, WIN, CH), start=True, stop=True)
                pe.matmul(M0[:, CH:2 * CH], w("wk"), tokens(n, WIN, CH), start=True, stop=True).then_inc(s_p1, 1)

            def latent_queries(n, m, free=True):
                if free:
                    pe.wait_ge(s_x1, m - 1)
                pe.matmul(M1[:, 0:CH], w("wgq"), tokens(n, WIN, CH), start=True, stop=True).then_inc(s_p2, 1)

            def latents(n, m):
                pe.wait_ge(s_sum, m + 1)
                pe.wait_ge(s_eg, m + 1)
                sums = sumT[:, n[1] % B, :]
                pe.matmul(M1[0:64, 0:64], w("wgk", 64), sums, start=True, stop=True)
                pe.matmul(M1[0:64, 64:128], sums, w("wgv", 64), start=True, stop=True).then_inc(s_gkv, 1)

            def values(m):
                pe.wait_ge(s_xw, 2 * m + 2)
                pe.wait_ge(s_kT, m + 1)
                for pr in range(NP2):
                    mm = pe.matmul(M0[:, P * pr:P * pr + P], xw[:, 2 * pr:2 * pr + 2, :].rearrange("p b i -> p (b i)"), w("wv"),
                                   start=True, stop=True)
                mm.then_inc(s_p3, 1)

            def gates(m):
                pe.wait_ge(s_qd, m + 1)
                pe.wait_ge(s_gqd, m + 1)
                for a in range(2):
                    mm = pe.matmul(M1[:, CH * a:CH * a + CH], gate_w[:, a, :], qT[:], start=True, stop=True)
                mm.then_inc(s_p4, 1)

            def scores(n, m, u, early=False):
                ch = n[0] + n[1] // 2
                pe_bank = bank[u % 2]
                if not early:
                    pe.wait_ge(s_sub, m * U + (u - 1))
                r = 32 * (u if u < UL else u - UL)
                if u == 0:
                    pe.wait_ge(s_qd, m + 1)
                    pe.wait_ge(s_kT, m + 1)
                if u == UL:
                    pe.wait_ge(s_gqd, m + 1)
                    pe.wait_ge(s_gk, m + 1)
                spread = cbf("spread", P)
                if u < UL:
                    first = cbf("first", NCH * 64)[:, bass.ds(ch * 64, 64)]
                    pe.matmul(pe_bank[:, 0:64], spread, first, start=True, stop=False, skip_group_check=True)
                    pe.matmul(pe_bank[:, 64:], spread, cbf("local", 448), start=False, stop=False, skip_group_check=True)
                else:
                    latent = cbf("latent", NCH * 512)[:, bass.ds(ch * 512, 512)]
                    pe.matmul(pe_bank[:], spread, latent, start=True, stop=False, skip_group_check=True)
                for blk in range(NB):
                    q_, k_ = (qd, kT[r:r + 32, n[1] % B, WIN * blk:WIN * blk + 64]) if u < UL else (gqd, gkT[r:r + 32, :])
                    mm = pe.matmul(pe_bank[:, 64 * blk:64 * blk + 64], q_[r:r + 32, blk, :, :].rearrange("p h i -> p (h i)"), k_,
                                   start=False, stop=(blk == NB - 1), skip_group_check=True)
                mm.then_inc(s_S, 1)

            def turn(un, u, early):
                pe.wait_ge(s_exp, un + (u + 1))
                if not early or u >= 2:
                    pe.wait_ge(s_pte, un + (u - 1))
                for pr in range(NP2):
                    mm = pe.transpose(bank[2 + u % 2][:, P * pr:P * pr + P], prob[:, u % 2, P * pr:P * pr + P], ident)
                mm.then_inc(s_tr, 1)

            def weigh(un, m, u, early):
                pe.wait_ge(s_pte, un + (u + 1))
                if u == 0:
                    pe.wait_ge(s_vd, m + 1)
                if u == UL:
                    pe.wait_ge(s_gk, m + 1)
                if not early or u >= 2:
                    pe.wait_ge(s_oe, un + (u - 1))
                for pr in range(NP2):
                    v_ = vd[:, UL * pr + u, :, :, :] if u < UL else gvd[:, u - UL, :, :, :]
                    mm = pe.matmul(bank[4 + u % 2][:, 72 * pr:72 * pr + 72], probT[:, u % 2, P * pr:P * pr + P],
                                   v_.rearrange("p b h o -> p (b h o)"), start=True, stop=True)
                mm.then_inc(s_pv, 1)

            def remote(m):
                pe.wait_ge(s_p_att, m)
                pe.matmul(M1[:, 0:CH].rearrange("p (b i) -> p b i", i=32), w("rout"),
                          attT_flat.rearrange("p (b s i) -> p b s i", b=NB, s=2)[:, :, 1, :], start=True, stop=True).then_inc(s_rem, 1)

            def project(m):
                pe.wait_ge(s_mix, m)
                for t in range(2):
                    mm = pe.matmul(M1[:, P * t:P * t + P], mix[:, P * t:P * t + P], w("wout"), start=True, stop=True)
                mm.then_inc(s_proj, 1)

            start = (0, 0)
            queries_keys(start, 0, free=False)
            latent_queries(start, 0, free=False)
            values(0)
            gates(0)
            scores(start, 0, 0, early=True)
            scores(start, 0, 1, early=True)

            def attend(q, k, single):
                this, next_ = (q, k), (q, k + 1)
                m = 2 * q + k
                un = m * U
                before, after = not single or k > 0, not single or k < B * NCH - 1
                early = not before
                turn(un, 0, early)
                latents(this, m)
                scores(this, m, 2)
                weigh(un, m, 0, early)
                turn(un, 1, early)
                scores(this, m, 3)
                weigh(un, m, 1, early)
                turn(un, 2, early)
                if after:
                    queries_keys(next_, m + 1, free=before)
                scores(this, m, 4)
                if before:
                    pe.wait_ge(s_gk, m + 1)
                    remote(m)
                weigh(un, m, 2, early)
                turn(un, 3, early)
                scores(this, m, 5)
                if before:
                    project(m)
                weigh(un, m, 3, early)
                turn(un, 4, early)
                if after:
                    latent_queries(next_, m + 1, free=before)
                    scores(next_, m + 1, 0)
                weigh(un, m, 4, early)
                turn(un, 5, early)
                if after:
                    scores(next_, m + 1, 1)
                    values(m + 1)
                    gates(m + 1)
                weigh(un, m, 5, early)

            attention_turns(pe, attend)
            remote(B * NCH)
            project(B * NCH)

            def turn_rows(j0, k):
                for s in range(2):
                    kb = k[1] + s
                    pe.wait_ge(s_xg[kb % 4], 16 * (k[0] + kb // 4 + 1))
                    mm = pe.transpose(bank[0][:, P * s:P * s + P], xg[:, kb % 4, :], ident)
                mm.then_inc(s_tx, 1)

            turn_rows(0, (0, 0))

            def expert(q, k, single):
                if single and k >= E:
                    return
                e = 2 * q + k
                pe.wait_ge(s_we[k % 2], 32 * (q + k // 2 + 1))
                pe.wait_ge(s_xgT, e + 1)
                for f in range(4):
                    pe.matmul(bank[hidden_bank[f]][:, 0:2 * P], we[:, k % 2, P * f:P * f + P], xgT[:],
                              start=True, stop=True).then_inc(s_h, 1)
                if not single or k + 1 < E:
                    turn_rows(None, (q, 2 * (k + 1)))
                pe.wait_ge(s_gelu, 4 * e + 4)
                if not single or k:
                    pe.wait_ge(s_ysb, 2 * e)
                for s in range(2):
                    for f in range(4):
                        mm = pe.matmul(bank[(3, 6)[s]][:, 0:P], hT[:, f, P * s:P * s + P],
                                       we[:, k % 2, F0 + P * f:F0 + P * f + P], start=(f == 0), stop=(f == 3))
                    mm.then_inc(s_y, 1)

            expert_turns(pe, expert)

            turn_x(1)
            logits(1, "Wgate")
            prefix(1)
            inverse(1, 2 * T, J1, T)

            def sum_kv(t):
                pe.wait_ge(s_kf, t + 1)
                if t % 8 == 0 and t:
                    pe.wait_ge(s_kvd, t // 8)
                mm = pe.matmul(bank[2][:, 0:P + 1], kf[:, t % 2, :], vf[:, t % 2, :], start=(t % 8 == 0), stop=(t % 8 == 7))
                mm.then_inc(s_kvsum, 1)

            for b in range(B):
                for t in range(8 * b, 8 * b + 8):
                    if t >= 2:
                        pe.wait_ge(s_kmin, t - 1)
                    pe.matmul(bank[t % 2][:, 0:2 * P], x_tile_T(t), w("Wk", 2 * P), start=True, stop=True).then_inc(s_kv, 1)
                    if t % 8:
                        sum_kv(t - 1)
                sum_kv(8 * b + 7)
                pe.wait_ge(s_kvd, b + 1)
                for h in range(2):
                    m = 2 * b + h
                    pe.matmul(bank[3][:], w("Wq"), xnT[:, b, WIN + 512 * h:WIN + 512 * h + 512], start=True, stop=True).then_inc(s_qp, 1)
                    pe.wait_ge(s_qf, m + 1)
                    pe.matmul(bank[6][:], kvd[:], qf[:], start=True, stop=True)
                    pe.matmul(bank[7][:], ksd[:], qf[:], start=True, stop=True).then_inc(s_num, 1)
                    pe.wait_ge(s_aT, m + 1)
                    if m:
                        pe.wait_ge(s_x2, m)
                    for t in range(4):
                        mm = pe.matmul(bank[4][:, P * t:P * t + P], aT[:, P * t:P * t + P], w("Wo"), start=True, stop=True)
                    mm.then_inc(s_o1, 1)
            pe.wait_ge(s_w1, 32)
            pe.wait_ge(s_x2, 4)
            pe.wait_ge(s_xg[0], 16 * (J0 // 4 + 1))
            pe.transpose(bank[4][:, 0:P], xg[:, 0, :], ident).then_inc(t_x, 1)

            def weights(e, start, width):
                return w1s[:].rearrange("p e c -> p (e c)")[:, bass.ds(e * (W12 + WGL + W3) + start, width)]

            def expert_of(i):
                return pe.value_load(te[0:1, bass.ds(i, 1)], min_val=0, max_val=E - 1)

            def tile(q, k, single):
                i = 4 * q + k
                if not single or 1 <= k <= J1:
                    pe.wait_ge(t_z, i)
                    for a in range(2):
                        mm = pe.transpose(bank[2][:, P * a:P * a + P], z[:, P * a:P * a + P], ident)
                    mm.then_inc(t_zT, 1)
                if not single or 3 <= k < J1 + 3:
                    pe.wait_ge(t_o, i - 2)
                    for a in range(2):
                        mm = pe.transpose(bank[3][:, P * a:P * a + P], og[:, (k - 3) % 2, P * a:P * a + P], ident)
                    mm.then_inc(t_oT, 1)
                if not single or k < J1:
                    pe.wait_ge(t_xTs, i + 1)
                if not single or k + 1 < J1:
                    pe.wait_ge(s_xg[(k + 1) % 4], 16 * (q + J0 // 4 + (k + 1) // 4 + 1))
                    pe.transpose(bank[4][:, 0:P], xg[:, (k + 1) % 4, :], ident).then_inc(t_x, 1)
                if not single or k < J1:
                    pe.matmul(bank[0][:], xtT[:, k % 2, :], weights(expert_of(i), 0, W12), start=True, stop=True).then_inc(t_h, 1)
                if not single or 1 <= k <= J1:
                    e = expert_of(i - 1)
                    pe.wait_ge(t_zTs, i)
                    pe.wait_ge(t_gb, i - 1)
                    for a in range(2):
                        mm = pe.matmul(bank[1][:], zT[:, P * a:P * a + P], weights(e, W12 + 2 * F1 * a, 2 * F1), start=(a == 0), stop=(a == 1))
                    mm.then_inc(t_g, 1)
                if not single or 3 <= k < J1 + 3:
                    e = expert_of(i - 3)
                    pe.wait_ge(t_oTs, i - 2)
                    pe.wait_ge(t_ysb, i - 3)
                    for a in range(2):
                        mm = pe.matmul(bank[5][:, 0:P], oT[:, P * a:P * a + P], weights(e, W12 + WGL + P * a, P), start=(a == 0), stop=(a == 1))
                    mm.then_inc(t_y, 1)

            tile_turns(pe, tile)

        @block.vector
        def _(dve):
            own = Steps(dve, dve_own)

            def tt(o, a, b_, op):
                own(dve.tensor_tensor(o, a, b_, op))

            def ts(o, a, s1, op1, s2=None, op2=None):
                own(dve.tensor_scalar(o, a, s1, s2, op1, *(() if op2 is None else (op2,))))

            def stt(o, a, s, b_, op1, op2):
                own(dve.scalar_tensor_tensor(o, a, s, b_, op1, op2))

            def reduce(o, a, op):
                own(dve.tensor_reduce(o, a, X, op))

            def over_e(ap):
                return ap.unsqueeze(2).broadcast_to([P, T, E])

            def over_t(ap):
                return ap.unsqueeze(1).broadcast_to([P, T, E])

            def norm(layer):
                for i in range(4):
                    if layer == 0:
                        dve.wait_ge(s_x[i], 16)
                    for t in range(4 * i, 4 * i + 4):
                        own.mark(dve.bn_stats(stats[:, t, :], x[:, t, :]))
                own.wait()
                for t in range(T):
                    own.mark(dve.bn_aggr(mv[:, t, :], stats[:, t, :]))
                own.wait()
                ts(var[:], mv[:, :, 1], 1e-5, ALU.add)
                own.mark(dve.tensor_scalar(rstd[:].bitcast(I32), var[:].bitcast(I32), -0.5, float(0x5F3759DF), ALU.mult, ALU.add))
                ts(var[:], var[:], -0.5, ALU.mult)
                for _ in range(3):
                    tt(sq[:], rstd[:], rstd[:], ALU.mult)
                    tt(sq[:], sq[:], var[:], ALU.mult)
                    stt(rstd[:], sq[:], 1.5, rstd[:], ALU.add, ALU.mult)
                for t in range(T):
                    last = dve.tensor_scalar(xn[:, t, :], x[:, t, :], mv[:, t, 0:1], rstd[:, t:t + 1], ALU.subtract, ALU.mult)
                    own.mark(last) if t % 4 < 3 else last.then_inc(s_xn, 1)

            def best(m, ident_, one_hot):
                reduce(m, lg[:], ALU.max)
                tt(ta[:], lg[:], over_e(m), ALU.is_lt)
                stt(ta[:], ta[:], float(E), over_t(c("iota_e", E)), ALU.mult, ALU.add)
                reduce(ident_, ta[:], ALU.min)
                tt(one_hot, over_t(c("iota_e", E)), over_e(ident_), ALU.is_equal)

            def count(layer, choices):
                own(dve.tensor_copy(chosen[:].rearrange("p e t -> p t e"), choices))
                own(dve.tensor_tensor_scan(upto[:].rearrange("p e t -> p (e t)"), c("reset", P),
                                           chosen[:].rearrange("p e t -> p (e t)"), 0.0, ALU.mult, ALU.add))
                own.mark(dve.tensor_copy(chosen_bf[:], chosen[:]))
                own.mark(dve.tensor_copy(total_bf[:], upto[:, :, T - 1]))
                own.mark(dve.tensor_tensor(earlier_bf[:], upto[:], chosen[:], ALU.subtract))
                own.wait()
                dve.sem_inc(s_cnt, 1)
                dve.wait_ge(s_pos, layer + 1)
                own(dve.tensor_copy(pos[:].rearrange("p e t -> p (e t)"), bank[5][:, 0:P]))

            def own_position(one_hot, o):
                tt(ta[:], one_hot, pos[:].rearrange("p e t -> p t e"), ALU.mult)
                reduce(o, ta[:], ALU.add)

            def invert(layer, done, n, width, trash, frm, to):
                nk = n // T
                own(dve.tensor_copy(slot_i[:, 0:nk, :], slot[:, 0:nk, :]))
                own.mark(dve.tensor_scalar(lo_i[:, 0:nk, :], slot_i[:, 0:nk, :], P - 1, None, ALU.bitwise_and))
                own.mark(dve.tensor_scalar(hi_i[:, 0:nk, :], slot_i[:, 0:nk, :], 7, None, ALU.logical_shift_right))
                own.wait()
                own.mark(dve.tensor_copy(lo[:, 0:nk, :], lo_i[:, 0:nk, :]))
                own.mark(dve.tensor_copy(hi[:, 0:nk, :], hi_i[:, 0:nk, :]))
                own.wait()
                shape = [P, n, width]
                hit = is_hi[:].rearrange("p n j -> p (n j)")[:, 0:n * width].rearrange("p (n j) -> p n j", n=n)
                hi_n, lo_n = hi[:].rearrange("p k t -> p (k t)"), lo[:].rearrange("p k t -> p (k t)")
                tt(hit, c("iota_j", width).unsqueeze(1).broadcast_to(shape), hi_n[:, 0:n].unsqueeze(2).broadcast_to(shape), ALU.is_equal)
                own.mark(dve.tensor_tensor(ids_of(layer)[:, :, 0, :], hit, c("hi", n).unsqueeze(2).broadcast_to(shape), ALU.mult))
                own.mark(dve.tensor_scalar(ids_of(layer)[:, :, 1, :], hit, c("part", 1), None, ALU.mult))
                own.wait()
                for i in range(n):
                    if i >= 4:
                        dve.wait_ge(s_inv, done + i - 3)
                    dve.tensor_scalar(is_lo[:, i % 4, :], cbf("iota", P), lo_n[:, i:i + 1], None, ALU.is_equal).then_inc(s_islo, 1)
                dve.wait_ge(s_inv, done + n)
                own(dve.tensor_copy(inv[:, :, 0:width], bank[5][:, 0:2 * width].rearrange("p (a j) -> p a j", a=2)))
                stt(ra[:, 0:width], inv[:, 0, 0:width], float(P), inv[:, 1, 0:width], ALU.mult, ALU.add)
                ts(rocc[:, 0:width], ra[:, 0:width], float(P), ALU.is_ge)
                stt(rb[:, 0:width], ra[:, 0:width], float(P), trash, ALU.subtract, ALU.subtract)
                tt(rb[:, 0:width], rb[:, 0:width], rocc[:, 0:width], ALU.mult)
                own.mark(dve.tensor_tensor(to, rb[:, 0:width], trash, ALU.add))
                ts(ra[:, 0:width], ra[:, 0:width], float(P), ALU.subtract, 0.0, ALU.max)
                ts(rb[:, 0:width], ra[:, 0:width], float(N), ALU.is_ge, float(-N), ALU.mult)
                tt(frm, ra[:, 0:width], rb[:, 0:width], ALU.add)
                dve.sem_inc(s_route, 1)

            norm(0)
            dve.wait_ge(s_cst, 32)
            dve.wait_ge(s_wts, 16)
            own.mark(dve.tensor_scalar(gate_w[:, 0, :], c("heads_hgd", P), w("glw", 1), None, ALU.mult))
            own.mark(dve.tensor_scalar(gate_w[:, 1, :], c("heads_hgd", P), w("grw", 1), None, ALU.mult))
            own.wait()
            dve.sem_inc(s_gatew, 1)
            dve.wait_ge(s_lg, 1)
            own(dve.tensor_copy(lg[:].rearrange("p t e -> p (t e)"), bank[4][:, 0:T * E]))
            best(m1[:], id1[:], oh[:])
            tt(ta[:], lg[:], over_e(m1[:]), ALU.subtract)
            dve.sem_inc(s_gin, 1)
            dve.wait_ge(s_gexp, 1)
            reduce(esum[:], tb[:], ALU.add)
            own(dve.reciprocal(gate[:], esum[:]))
            count(0, oh[:])
            own_position(oh[:], own_pos[:])
            ts(keep[:], own_pos[:], float(CAP), ALU.is_lt)
            tt(gate[:], gate[:], keep[:], ALU.mult)
            stt(slot[:, 0, :], id1[:], float(CAP), own_pos[:], ALU.mult, ALU.add)
            ts(keep[:], keep[:], float(-2 * N), ALU.mult, float(2 * N), ALU.add)
            tt(slot[:, 0, :], slot[:, 0, :], keep[:], ALU.add)
            invert(0, 0, T, J0, c("trash0", J0), from0[:], to0[:])

            dve.wait_ge(s_zero, 12)
            att = att_flat.rearrange("p (b s) -> p b s", b=NB)
            attT = attT_flat.rearrange("p (b s i) -> p b s i", b=NB, s=2)

            def sums(q, k, m):
                start = (q + k // 2) * CH
                dst = sumT[:, k % B, :][:, bass.ds((q + k // 2) * 16, 16)]
                src = xnT[:, k % B, WIN:][:, bass.ds(start, CH)].rearrange("p (n k) -> p n k", k=S // NLAT)
                dve.tensor_reduce(dst, src, X, ALU.add).then_inc(s_sum, 1)

            def values(m):
                dve.wait_ge(s_p3, m + 1)
                for blk in range(2):
                    rows = slice(64 * blk, 64 * blk + 64)
                    last = dve.tensor_copy(vd[rows, :, blk, :, 0:HD], bank[6][rows, :].rearrange("p (c h d) -> p c h d", h=4, d=HD))
                last.then_inc(s_vd, 1)

            def shift(un, u, early=False):
                s3 = bank[u % 2][:].rearrange("p (b j) -> p b j", j=64)
                dve.wait_ge(s_S, un + (u + 1))
                if not early or u >= 2:
                    dve.wait_ge(s_tr, un + (u - 1))
                dve.tensor_reduce(rmax[:, u % 2, :], s3, X, ALU.max).then_inc(s_max, 1)
                dve.wait_ge(s_max, un + (u + 1))
                dve.tensor_tensor(prob[:, u % 2, :].rearrange("p (b j) -> p b j", j=64), s3,
                                  rmax[:, u % 2, :].unsqueeze(2).broadcast_to([P, NB, 64]), ALU.subtract).then_inc(s_sub, 1)

            def own_sums(m):
                dve.wait_ge(s_oe, m * U)
                for hh in range(4):
                    rows = slice(32 * hh, 32 * hh + 32)
                    last = dve.reciprocal(rsum[rows, :, :], oall[rows, :, :, hh, HD])
                last.then_inc(s_rsum, 1)

            def own_columns(m):
                dve.wait_ge(s_rsum, m)
                for hh in range(4):
                    rows = slice(32 * hh, 32 * hh + 32)
                    last = dve.tensor_tensor(att[rows, :, 0:8 * U].rearrange("p b (u d) -> p u b d", d=HD), oall[rows, :, :, hh, 0:HD],
                                             rsum[rows, :, :].unsqueeze(3).broadcast_to([32, U, NB, HD]), ALU.mult)
                last.then_inc(s_att, 1)
                dve.wait_ge(s_att, m)
                dve.transpose(attT_flat, att_flat).then_inc(s_p_att, 1)

            def near_part(m):
                dve.wait_ge(s_p_att, m)
                dve.wait_ge(s_sg, m)
                dve.tensor_tensor(near[:].rearrange("p (b i) -> p b i", i=32), attT[:, :, 0, :],
                                  sg[:, 0, :].rearrange("p (b i) -> p b i", i=32), ALU.mult)

            def mixed(m):
                dve.wait_ge(s_rem, m)
                dve.tensor_tensor(mix[:], bank[7][:, 0:CH], sg[:, 1, :], ALU.mult).then_inc(s_m0read, 1)
                dve.wait_ge(s_m0read, m)
                dve.tensor_tensor(mix[:], mix[:], near[:], ALU.add).then_inc(s_mix, 1)

            def onto_stream(q, k):
                q, k = (q - 1, k + 1) if k == 0 else (q, k - 1)
                m = 2 * q + k
                dve.wait_ge(s_proj, m + 1)
                xs = x[:, bass.ds((q + k // 2) * 2 + (k % B) * (S // P), 2), :]
                dve.tensor_tensor(xs, xs, bank[7][:, 0:CH].rearrange("p (t d) -> p t d", d=P), ALU.add).then_inc(s_x1, 1)

            sums(0, 0, 0)
            values(0)
            shift(0, 0, early=True)
            shift(0, 1, early=True)

            def attend(q, k, single):
                m = 2 * q + k
                un = m * U
                before, after = not single or k > 0, not single or k < B * NCH - 1
                shift(un, 2)
                if before:
                    own_sums(m)
                shift(un, 3)
                if before:
                    own_columns(m)
                shift(un, 4)
                if before:
                    near_part(m)
                    mixed(m)
                shift(un, 5)
                if before:
                    onto_stream(q, k)
                dve.wait_ge(s_eg, m + 1)
                dve.tensor_scalar(sg[:], eg[:], 1.0, None, ALU.add).then_inc(s_g1, 1)
                if after:
                    sums(q, k + 1, m + 1)
                    shift(un, 6)
                dve.wait_ge(s_g1, m + 1)
                dve.reciprocal(sg[:, 0, :], sg[:, 0, :])
                if after:
                    shift(un, 7)
                    values(m + 1)
                dve.reciprocal(sg[:, 1, :], sg[:, 1, :]).then_inc(s_sg, 1)

            attention_turns(dve, attend)
            own_sums(B * NCH)
            own_columns(B * NCH)
            near_part(B * NCH)
            mixed(B * NCH)
            onto_stream(0, B * NCH)

            def expert(q, k, single):
                if single and k >= E:
                    return
                for s in range(2):
                    j, kb = 4 * q + (2 * k + s), 2 * k + s
                    dve.wait_ge(s_y, j + 1)
                    if not single or k >= 2:
                        dve.wait_ge(s_ys[kb % 4], 16 * (q + kb // 4))
                    dve.tensor_tensor(ysb[:, kb % 4, :], bank[(3, 6)[s]][:, 0:P], b2e[:, k % 2, :], ALU.add).then_inc(s_ysb, 1)

            expert_turns(dve, expert)
            for i in range(4):
                dve.wait_ge(s_y0[i], 16)
                for t in range(4 * i, 4 * i + 4):
                    own.mark(dve.scalar_tensor_tensor(x[:, t, :], xn[:, t, :], gate[:, t:t + 1], x[:, t, :], ALU.mult, ALU.add))
            own.wait()

            norm(1)
            dve.wait_ge(s_rows1, 16)
            dve.wait_ge(s_lg, 2)
            tt(lg[:], bank[4][:, 0:T * E].rearrange("p (t e) -> p t e", e=E), over_t(rows1[:, 3 * P:3 * P + E]), ALU.add)
            best(m1[:], id1[:], oh[:])
            stt(lg[:], oh[:], NEG, lg[:], ALU.mult, ALU.add)
            best(m2[:], id2[:], oh2[:])
            tt(e21[:], m2[:], m1[:], ALU.subtract)
            dve.sem_inc(s_gin, 1)
            tt(tb[:], oh[:], oh2[:], ALU.add)
            count(1, tb[:])
            own(dve.tensor_copy(cnt[:], bank[5][:, P:P + E]))
            tt(over[:], cnt[:].unsqueeze(2).broadcast_to([P, E, 16]), c("thresholds", 16).unsqueeze(1).broadcast_to([P, E, 16]), ALU.is_gt)
            reduce(tiles[:], over[:], ALU.add)
            own(dve.tensor_tensor_scan(tiles_end[:], c("thresholds_one", E), tiles[:], 0.0, ALU.mult, ALU.add))
            tt(base[:], tiles_end[:], tiles[:], ALU.subtract)
            ts(base[:], base[:], float(P), ALU.mult)
            tt(pos[:], pos[:], base[:].unsqueeze(2).broadcast_to([P, E, T]), ALU.add)
            own_position(oh[:], slot[:, 0, :])
            own_position(oh2[:], slot[:, 1, :])
            tt(passed[:], c("iota_j", J1).unsqueeze(2).broadcast_to([P, J1, E]),
               tiles_end[:].unsqueeze(1).broadcast_to([P, J1, E]), ALU.is_ge)
            reduce(te_f[:], passed[:], ALU.add)
            ts(te[:], te_f[:], float(E - 1), ALU.min)
            dve.wait_ge(s_gexp, 2)
            ts(w1c[:], e21[:], 1.0, ALU.add)
            own(dve.reciprocal(w1c[:], w1c[:]))
            tt(w2c[:], w1c[:], e21[:], ALU.mult)
            invert(1, T, 2 * T, J1, c("trash1", J1), from1[:], to1[:])

            dve.wait_ge(s_bo, 1)

            def feature_k(t):
                dve.wait_ge(s_kexp, t + 1)
                dve.scalar_tensor_tensor(kf[:, t % 2, :], kraw[:, t % 2, :], 0.0, kexp[:, t % 2, :], ALU.max, ALU.add).then_inc(s_kf, 1)

            for b_ in range(B):
                for t in range(8 * b_, 8 * b_ + 8):
                    dve.wait_ge(s_kv, t + 1)
                    if t >= 2:
                        dve.wait_ge(s_kvsum, t - 1)
                    own.mark(dve.tensor_tensor(kraw[:, t % 2, :], bank[t % 2][:, 0:P], rows1[:, 0:P], ALU.add))
                    own.mark(dve.tensor_tensor(vf[:, t % 2, 0:P], bank[t % 2][:, P:2 * P], rows1[:, P:2 * P], ALU.add))
                    own.wait(0)
                    dve.tensor_scalar(kmin[:, t % 2, :], kraw[:, t % 2, :], 0.0, None, ALU.min).then_inc(s_kmin, 1)
                    if t % 8:
                        feature_k(t - 1)
                feature_k(8 * b_ + 7)
                dve.wait_ge(s_kvsum, 8 * b_ + 8)
                own.mark(dve.tensor_copy(ksum[:], bank[2][:, P:P + 1]))
                own.mark(dve.tensor_tensor(kvd[:], bank[2][:, 0:P], c("heads", P), ALU.mult))
                own.wait(1)
                own(dve.tensor_scalar(ksd[:], c("heads", P), ksum[:], None, ALU.mult))
                dve.sem_inc(s_kvd, 1)
                for h in range(2):
                    m = 2 * b_ + h
                    dve.wait_ge(s_qp, m + 1)
                    own.mark(dve.tensor_scalar(qpos[:], bank[3][:], w("bq", 1), 0.0, ALU.add, ALU.max))
                    dve.tensor_scalar(qmin[:], bank[3][:], w("bq", 1), 0.0, ALU.add, ALU.min).then_inc(s_qmin, 1)
                    dve.wait_ge(s_qexp, m + 1)
                    dve.tensor_tensor(qf[:], qpos[:], qmin[:], ALU.add).then_inc(s_qf, 1)
                    dve.wait_ge(s_num, m + 1)
                    ts(den[:], bank[7][:], 1e-6, ALU.max)
                    own(dve.reciprocal(den[:], den[:]))
                    dve.tensor_tensor(aT[:], bank[6][:], den[:], ALU.mult).then_inc(s_aT, 1)
                    dve.wait_ge(s_o1, m + 1)
                    xs = x[:, 4 * m:4 * m + 4, :]
                    dve.tensor_tensor(xs, xs, bank[4][:].rearrange("p (t d) -> p t d", d=P), ALU.add).then_inc(s_x2, 1)

            dve.wait_ge(s_bias1, 16)

            def bias(i, start, width):
                e = dve.value_load(te[0:1, bass.ds(i, 1)], min_val=0, max_val=E - 1)
                return shared[:, bass.ds(e * BIAS1 + start, width)]

            def tile(q, k, single):
                i = 4 * q + k
                if not single or k < J1:
                    bias_h = bias(i, 0, 2 * F1)
                    dve.wait_ge(t_h, i + 1)
                    dve.tensor_tensor(h12[:], bank[0][:], bias_h, ALU.add).then_inc(t_hb, 1)
                    dve.wait_ge(t_hb, i + 1)
                    dve.tensor_tensor(z[:], h12[:, 0:F1], h12[:, F1:], ALU.mult).then_inc(t_z, 1)
                if not single or 2 <= k < J1 + 2:
                    dve.wait_ge(t_sil, i - 1)
                    if not single or k >= 4:
                        dve.wait_ge(t_oT, i - 3)
                    dve.tensor_tensor(og[:, k % 2, :], sil, hgl[:, F1:], ALU.mult).then_inc(t_o, 1)
                if not single or 1 <= k <= J1:
                    bias_g = bias(i - 1, 2 * F1, 2 * F1)
                    if not single or 2 <= k:
                        dve.wait_ge(t_o, i - 1)
                    dve.wait_ge(t_g, i)
                    dve.tensor_tensor(hgl[:], bank[1][:], bias_g, ALU.add).then_inc(t_gb, 1)
                if not single or 3 <= k < J1 + 3:
                    bias_y = bias(i - 3, 4 * F1, P)
                    dve.wait_ge(t_y, i - 2)
                    dve.wait_ge(s_ys[(k - 3) % 4], 16 * (q + (J0 // 4 + (k - 3) // 4)))
                    dve.tensor_tensor(ysb[:, (k - 3) % 4, :], bank[5][:, 0:P], bias_y, ALU.add).then_inc(t_ysb, 1)

            tile_turns(dve, tile)
            for b_ in range(B):
                dve.wait_ge(s_yk[b_], 32)
                for weight, src in ((w1c, xnT[:, b_, 0:S].rearrange("p (t d) -> p t d", d=P)), (w2c, xn[:, 8 * b_:8 * b_ + 8, :])):
                    for t in range(8):
                        tt_ = 8 * b_ + t
                        ins_ = dve.scalar_tensor_tensor(x[:, tt_, :], src[:, t, :], weight[:, tt_:tt_ + 1], x[:, tt_, :], ALU.mult, ALU.add)
                        own.mark(ins_)
                    own.wait()
                dve.sem_inc(s_res, 1)


def kernel(**inputs):
    from concourse import bacc
    from concourse.bass_utils import run_bass_kernel_spmd

    a = {k: np.asarray(v) for k, v in inputs.items()}
    order = [8 * (4 * g + hh) + d for hh in range(4) for g in range(4) for d in range(HD)]
    rout = np.zeros((P, P), np.float32)
    for hh in range(4):
        for g in range(UG):
            h = 4 * g + hh
            rout[32 * hh + 8 * g:32 * hh + 8 * g + 8] = a["L0_attn_r_out_w"][8 * h:8 * h + 8][:, order]
    wts = np.concatenate(
        [a["L0_attn_wq"], a["L0_attn_wk"], a["L0_attn_wv"], a["L0_attn_w_out"][order], rout,
         a["L1_attn_Wq"], a["L1_attn_Wk"], a["L1_attn_Wv"], a["L1_attn_Wo"],
         a["L0_attn_wgq"], a["L0_attn_wgk"], a["L0_attn_wgv"], a["L0_ffn_wg"], a["L1_ffn_Wgate"],
         a["L0_attn_gate_local_w"].reshape(P, 1), a["L0_attn_gate_remote_w"].reshape(P, 1), a["L1_attn_bq"].reshape(P, 1)], axis=1)

    def chunks(m, n):
        return m.reshape(E, n, P, -1).transpose(0, 2, 1, 3).reshape(E, P, -1)

    we = np.concatenate([a["L0_ffn_w1"], chunks(a["L0_ffn_w2"], 4), chunks(a["L0_ffn_b1"].reshape(E, F0, 1), 4)], axis=2)
    w1s = np.concatenate([a["L1_ffn_W1"], a["L1_ffn_W2"],
                          chunks(np.concatenate([a["L1_ffn_Wg"], a["L1_ffn_Wl"]], axis=2), 2), chunks(a["L1_ffn_W3"], 2)], axis=2)
    bias1 = np.concatenate([a["L1_ffn_" + n] for n in ("b1", "b2", "bg", "bl", "b3")], axis=1).reshape(1, -1)
    rows1 = np.concatenate([a["L1_attn_bk"], a["L1_attn_bv"], a["L1_attn_bo"], a["L1_ffn_bgate"]]).reshape(1, -1)
    cf, cb = constants()
    arrays = {"x": a["L0_attn_x"].reshape(N, P), "wts": wts, "cf": cf, "cb": cb, "we": we, "b2": a["L0_ffn_b2"],
              "w1s": w1s.transpose(1, 0, 2), "bias1": bias1, "rows1": rows1}
    arrays = {k: np.ascontiguousarray(v) for k, v in arrays.items()}
    nc = bacc.Bacc("TRN2", target_bir_lowering=False, num_devices=1)
    ins = {k: nc.dram_tensor(f"in_{k}", v.shape, mybir.dt.from_np(v.dtype), kind="ExternalInput").ap() for k, v in arrays.items()}
    out = nc.dram_tensor("out", (N, P), F32, kind="ExternalOutput").ap()
    program(nc, ins, out)
    r = run_bass_kernel_spmd(nc, [{f"in_{k}": v for k, v in arrays.items()}], core_ids=[0])
    return r.results[0]["out"].reshape(B, S, P)
```

```python
from contextlib import ExitStack

import numpy as np

import concourse.bass as bass
from concourse import mybir

F32 = mybir.dt.float32
BF16 = mybir.dt.bfloat16
I32 = mybir.dt.int32
U32 = mybir.dt.uint32
ALU = mybir.AluOpType
ACT = mybir.ActivationFunctionType
X = mybir.AxisListType.X

P = 128
B, S = 2, 1024
N = B * S
T = N // P
E = 8
WIN = 32
NLAT = 64
CH = 256
NCH = S // CH
NB = CH // WIN
NP2 = NB // 2
UL, UG = 4, 2
U = UL + UG
HD = 8
NQ = N // 512
WARM = {"scores": 4, "values": 3, "last_chunk": 16, "norm": 15, "start": 8, "turn_x": 2, "turn_x1": 5, "routing": 20,
        "features": 5, "after_inverse": 4, "inverse_step": 4, "mix": 5}
NH = P // HD
VW = HD + 1
NEG = -1e30
F0 = 512
CAP = N // E
J0 = E * CAP // P
F1 = 256
J1 = 2 * N // P + E - 1
W12, WGL, W3 = 2 * F1, 4 * F1, 2 * P
BIAS1 = 4 * F1 + P

WEIGHTS = ["wq", "wk", "wv", "wout", "rout", "Wq", "Wk", "Wv", "Wo"]
COL = {name: 128 * i for i, name in enumerate(WEIGHTS)}
at = 128 * len(WEIGHTS)
for name, width in (("wgq", 64), ("wgk", 64), ("wgv", 64), ("wg", 8), ("Wgate", 8), ("glw", 1), ("grw", 1), ("bq", 1)):
    COL[name] = at
    at += width
NW = at
CF = {}
at = 0
for name, width in (("ident", 128), ("heads", 128), ("heads_hgd", 128), ("mine", 4), ("head", P // 8), ("iota_e", 8), ("iota_j", J1),
                    ("trash0", J0), ("trash1", J1), ("reset", 128), ("thresholds", 16), ("thresholds_one", E), ("part", 1), ("hi", 2 * T)):
    CF[name] = at
    at += width
NCF = at
CB = {}
at = 0
for name, width in (("before", 128), ("ones", 128), ("iota", 128), ("spread", 128), ("local", 7 * 64), ("first", NCH * 64), ("latent", NCH * 512)):
    CB[name] = at
    at += width
NCB = at


def constants():
    p = np.arange(P)
    f = {"ident": np.eye(P), "heads": p[:, None] // HD == p[None] // HD}
    c = np.arange(P)
    head_of = 4 * (c // 8 % 4) + c // 32
    f["heads_hgd"] = p[:, None] // HD == head_of[None]
    f["mine"] = (p[:, None] // HD % 4 == np.arange(4)[None]) / np.sqrt(np.float32(HD))
    f["head"] = p[:, None] // HD == np.arange(P // HD)[None]
    f["iota_e"] = np.broadcast_to(np.arange(E), (P, E))
    f["iota_j"] = np.broadcast_to(np.arange(J1), (P, J1))
    f["trash0"] = N + P * np.arange(J0)[None] + p[:, None]
    f["trash1"] = 2 * N + P * np.arange(J1)[None] + p[:, None]
    f["reset"] = np.broadcast_to(np.arange(P) % T != 0, (P, P))
    f["thresholds"] = np.broadcast_to(P * np.arange(16), (P, 16))
    f["thresholds_one"] = np.ones((P, E))
    f["part"] = p[:, None]
    f["hi"] = np.broadcast_to(1 + np.arange(2 * T), (P, 2 * T))
    b = {"before": p[:, None] < p[None], "ones": np.ones((P, P)), "iota": np.broadcast_to(p, (P, P))}
    i = p[:, None] % WIN
    b["spread"] = p[:, None] == p[None] % WIN
    j = np.arange(64)[None]
    local = (j > i) & (j <= i + WIN)
    b["local"] = np.where(np.tile(local, (1, NB - 1)), 0, NEG)
    b["first"] = np.where(np.concatenate([local & (j >= WIN)] + [local] * (NCH - 1), 1), 0, NEG)
    s = 32 * (np.arange(4 * 512)[None] // 64) + i
    b["latent"] = np.where(np.arange(4 * 512)[None] % 64 <= s // (S // NLAT), 0, NEG)
    cf, cb = np.zeros((P, NCF), np.float32), np.zeros((P, NCB), mybir.dt.np(BF16))
    for src, dst, cols in ((f, cf, CF), (b, cb, CB)):
        for k, v in src.items():
            dst[:, cols[k]:cols[k] + v.shape[1]] = v
    return cf, cb


class Steps:

    def __init__(self, eng, sem):
        self.eng, self.sem, self.n, self.base = eng, sem, 0, 0

    def __call__(self, ins):
        self.mark(ins)
        self.wait()

    def mark(self, ins):
        ins.then_inc(self.sem, 1)
        self.n += 1

    def wait(self, back=0):
        self.eng.wait_ge(self.sem, self.base + (self.n - back))


def turns(eng, step, peel, trips, unroll, total):
    for i in range(peel):
        step(0, i, True)
    with eng.Fori(0, trips) as q:
        for k in range(peel, peel + unroll):
            step(q, k, False)
    for i in range(peel + trips * unroll, total):
        step(0, i, True)


def attention_turns(eng, step):
    turns(eng, step, 1, 3, 2, B * NCH)


def expert_turns(eng, step):
    turns(eng, step, 2, 2, 2, E + 1)


def tile_turns(eng, step):
    turns(eng, step, 4, 8, 4, J1 + 4)


def expert_reader(eng, te):
    loaded = {}

    def expert_of(q, k):
        key = (id(q), k)
        if key not in loaded:
            loaded[key] = (q, eng.value_load(te[0:1, bass.ds(4 * q + k, 1)], min_val=0, max_val=E - 1))
        return loaded[key][1]

    return expert_of


def program(nc, ins, out):
    ctx = ExitStack()

    def sb(name, shape, dt=F32):
        return ctx.enter_context(nc.sbuf_tensor(name, shape, dt))

    def sem(name):
        return ctx.enter_context(nc.semaphore(name))

    def dram(name, rows):
        return nc.dram_tensor(name, [rows, P], F32, kind="Internal").ap()

    xn0_rows, xn1_rows = dram("xn0_rows", N), dram("xn1_rows", N)
    y0_rows = dram("y0_rows", N + J0 * P)
    y1_rows = dram("y1_rows", 2 * N + J1 * P)

    with ctx:
        wts, cf, cb = sb("wts", [P, NW]), sb("cf", [P, NCF]), sb("cb", [P, NCB], BF16)
        rows1 = sb("rows1", [P, 3 * P + E])
        x = sb("x", [P, T, P])
        xn = sb("xn", [P, T, P])
        xnT = sb("xnT", [P, B, WIN + S])
        stats, mv, var, sq, rstd = sb("stats", [P, T, 6]), sb("mv", [P, T, 2]), sb("var", [P, T]), sb("sq", [P, T]), sb("rstd", [P, T])
        shift_by = sb("shift_by", [P, T])
        gate_w = sb("gate_w", [P, 2, P])
        lg, oh, oh2 = sb("lg", [P, T, E]), sb("oh", [P, T, E]), sb("oh2", [P, T, E])
        ta, tb = sb("ta", [P, T, E]), sb("tb", [P, T, E])
        chosen, upto = sb("chosen", [P, E, T]), sb("upto", [P, E, T])
        chosen_bf, earlier_bf = sb("chosen_bf", [P, E, T], BF16), sb("earlier_bf", [P, E, T], BF16)
        total_bf = sb("total_bf", [P, E], BF16)
        pos = sb("pos", [P, E, T])
        m1, m2, id1, id2, esum, gate, keep, w1c, w2c, e21, own_pos = (
            sb("r_" + n, [P, T]) for n in ("m1", "m2", "id1", "id2", "esum", "gate", "keep", "w1c", "w2c", "e21", "own_pos"))
        slot, lo, hi = sb("slot", [P, 2, T]), sb("lo", [P, 2, T]), sb("hi", [P, 2, T])
        slot_i, lo_i, hi_i = sb("slot_i", [P, 2, T], I32), sb("lo_i", [P, 2, T], I32), sb("hi_i", [P, 2, T], I32)
        is_lo = sb("is_lo", [P, T, P], BF16)
        is_hi = sb("is_hi", [P, 2 * T, J1])
        ids = sb("ids", [P, 2 * T, 2, J1], BF16)
        cnt, tiles, tiles_end, base = (sb("e_" + n, [P, E]) for n in ("cnt", "tiles", "end", "base"))
        over = sb("over", [P, E, 16])
        passed = sb("passed", [P, J1, E])
        te_f, te = sb("te_f", [P, J1]), sb("te", [P, J1], I32)
        inv, ra, rb = sb("inv", [P, 2, J1]), sb("ra", [P, J1]), sb("rb", [P, J1])
        rocc = sb("rocc", [P, J1])
        from0, to0 = sb("from0", [P, J0], I32), sb("to0", [P, J0], I32)
        from1, to1 = sb("from1", [P, J1], I32), sb("to1", [P, J1], I32)
        xw, sumT = sb("xw", [P, NB, 2 * WIN]), sb("sumT", [P, B, NLAT])
        qT, kT, gkT = sb("qT", [P, CH]), sb("kT", [P, B, WIN + CH]), sb("gkT", [64, NLAT])
        shared = sb("shared", [P, E * BIAS1])
        bias1 = shared[:].rearrange("p (e c) -> p e c", e=E)
        off = [0]

        def part(*dims):
            n = int(np.prod(dims))
            ap = shared[:, off[0]:off[0] + n]
            off[0] += n
            return ap

        qd = part(NB, 4, WIN).rearrange("p (b h i) -> p b h i", b=NB, h=4)
        gqd = part(NB, 4, WIN).rearrange("p (b h i) -> p b h i", b=NB, h=4)
        vd_flat, gvd_flat = part(NP2, UL, 2, 4, VW), part(UG, 2, 4, VW)
        vd = vd_flat.rearrange("p (c b h o) -> p c b h o", c=NP2 * UL, b=2, h=4)
        gvd = gvd_flat.rearrange("p (g b h o) -> p g b h o", g=UG, b=2, h=4)
        prob, probT = (part(2, 512).rearrange("p (r n) -> p r n", r=2) for _ in range(2))
        oall_flat = part(U, NB, 4, VW)
        oall = oall_flat.rearrange("p (u b h o) -> p u b h o", u=U, b=NB, h=4)
        att_flat, attT_flat = part(NB, 2, 32), part(NB, 2, 32)
        rmax, rsum = sb("rmax", [P, 2, NB]), sb("rsum", [P, U, NB])
        eg, sg = sb("eg", [P, 2, CH]), sb("sg", [P, 2, CH])
        near, mix = sb("near", [P, CH]), sb("mix", [P, CH])
        we = sb("we", [P, 2, 2 * F0 + 4])
        b2e = sb("b2e", [P, 2, P])
        xg, xgT = sb("xg", [P, 4, P]), sb("xgT", [P, 2 * P])
        hT = sb("hT", [P, 4, 2 * P])
        ysb = sb("ysb", [P, 4, P])

        ig, isc = sb("ig", [P, 4], I32), sb("isc", [P, 4], I32)
        w1s = sb("w1s", [P, E, W12 + WGL + W3])
        kexp, kf = sb("kexp", [P, 4, P]), sb("kf", [P, 4, P])
        vf = sb("vf", [P, 4, P + 1])
        bk_parts, bk_high, bk_mid = (sb(n, [P, P], BF16) for n in ("bk_parts", "bk_high", "bk_mid"))
        kvx, ksum = sb("kvx", [P, B, P + NH]), sb("ksum", [P, B])
        qe, qf0, qf1, at1, aT = (sb(n, [P, 512]) for n in ("qe", "qf0", "qf1", "at1", "aT"))
        den, rden = sb("den", [P, 2, 2 * NH]), sb("rden", [P, 2, 2 * NH])
        xtT = sb("xtT", [P, 2, P])
        z, zT, oT = (kexp[:].rearrange("p t d -> p (t d)")[:, 0:F1], kexp[:].rearrange("p t d -> p (t d)")[:, F1:],
                     kf[:].rearrange("p t d -> p (t d)")[:, 0:F1])
        zeros, h12, hgl, sil, og = qe, aT, qf0, at1[:, 0:F1], qf1[:].rearrange("p (r f) -> p r f", r=2)

        bank = [ctx.enter_context(nc.psum_tensor(f"bank{i}", [P, 512], F32)) for i in range(8)]

        q_bank, num_bank, qf = (bank[6], bank[5]), (bank[7], bank[0]), (qf0, qf1)
        hidden_bank = (1, 2, 4, 5)

        def w(name, width=P):
            return wts[:, COL[name]:COL[name] + width]

        def c(name, width):
            return cf[:, CF[name]:CF[name] + width]

        def cbf(name, width, start=0):
            return cb[:, CB[name] + start:CB[name] + start + width]

        ident = c("ident", P)

        s_x = [sem(f"x_in{i}") for i in range(4)]
        s_cf, s_cb, s_wts, s_rows1 = sem("f32_constants_in"), sem("bf16_constants_in"), sem("weights_in"), sem("rows1_in")
        s_w1, s_bias1, s_rstd, s_xn2 = sem("w1_in"), sem("bias1_in"), sem("rstd_ready"), sem("xn_ready_by_act")
        dve_own, pool_own = sem("dve_own"), sem("pool_own")
        s_zero, s_y0z, s_xn, s_xt, s_xTs, s_xnd = (sem(n) for n in (
            "buffers_filled", "y0_zeroed", "xn_ready", "x_turned", "xnT_ready", "xn_in_dram"))
        s_lg, s_gin, s_gexp, s_cnt, s_pos, s_posread, s_islo, s_inv, s_route = (sem(n) for n in (
            "logits", "gate_in", "gate_exp", "choices_ready", "positions", "positions_read", "is_lo_ready", "inverse",
            "routed"))
        s_gatew, s_xw, s_sum, s_p1, s_gkv, s_p3, s_p4 = (sem(n) for n in (
            "gate_w_ready", "xw_ready", "sums_ready", "qk_made", "latents_made", "v_made", "gates_made"))
        s_qd, s_gqd, s_kend, s_kT, s_gk, s_vd, s_eg, s_sg = (sem(n) for n in (
            "qd_ready", "gqd_ready", "k_end_kept", "kT_ready", "latents_ready", "vd_ready", "eg_ready", "sg_ready"))
        s_S, s_max, s_sub, s_exp, s_tr, s_pte, s_pv, s_oe = (sem(n) for n in (
            "scores", "maxima", "shifted", "probs", "probs_turned", "probT_ready", "weighted", "weighted_out"))
        s_lgread, s_g1, s_p_att, s_rsum, s_att, s_rem, s_m0read, s_mix, s_proj, s_x1 = (sem(n) for n in (
            "logits_read", "gates_plus_one", "attT_ready", "rsum_ready", "att_ready", "remote_made", "remote_read", "mixed", "projected", "x_added"))
        s_we = [sem(f"we_in{i}") for i in range(2)]
        s_xg = [sem(f"rows_in{i}") for i in range(4)]
        s_ys = [sem(f"rows_out{i}") for i in range(4)]
        s_ig, s_isc, s_index_seen = sem("gather_index"), sem("scatter_index"), sem("index_seen")
        s_tx, s_xgT, s_h, s_gelu, s_y, s_ysb = (sem(n) for n in (
            "rows_turned", "rowsT_ready", "hidden", "gelu_done", "y_made", "y_ready"))
        s_y0 = [sem(f"y0_back{i}") for i in range(4)]
        s_parts = sem("bk_parts_ready")
        s_stats, s_quarter, s_last_quarter = (sem(n) for n in ("statistics_ready", "quarter_added", "last_quarter_added"))
        s_hit, s_ids = sem("slot_tile_hit"), sem("high_parts_ready")
        s_bo, s_kv, s_kexp, s_vf, s_kmin, s_kf, s_kvsum, s_kvx = (sem(n) for n in (
            "bo_added", "kv_made", "kexp_ready", "vf_ready", "kexp_clipped", "kf_ready", "kv_summed", "kvx_ready"))
        s_qp, s_qe, s_qf, s_num, s_at, s_aTt, s_aT, s_o1, s_x2 = (sem(n) for n in (
            "q1_made", "qe_ready", "qf_ready", "num_made", "at_ready", "at_turned", "aT_ready", "att1_made", "x2_added"))
        t_x, t_xTs, t_h, t_hb, t_z, t_zT, t_zTs, t_g, t_gb, t_sil, t_o, t_oT, t_oTs, t_y, t_ysb = (
            sem("t_" + n) for n in ("x", "xTs", "h", "hb", "z", "zT", "zTs", "g", "gb", "sil", "o", "oT", "oTs", "y", "ysb"))
        s_yk = [sem(f"y1_back{i}") for i in range(4)]
        s_second, s_res, s_out = sem("second_shares"), sem("result"), sem("out_done")

        block = ctx.enter_context(nc.Block())

        def ids_of(layer):
            n, width = ((T, J0), (2 * T, J1))[layer]
            return ids[:].rearrange("p n a j -> p (n a j)")[:, 0:n * 2 * width].rearrange("p (n a j) -> p n a j", n=n, a=2)

        def x_tile_T(t):
            b, o = divmod(t * P, S)
            return xnT[:, b, WIN + o:WIN + o + P]

        @block.sync
        def _(sp):
            xv = ins["x"].rearrange("(t p) d -> p t d", p=P)
            for i in range(4):
                sp.dma_start(x[:, 4 * i:4 * i + 4, :], xv[:, 4 * i:4 * i + 4, :]).then_inc(s_x[i], 16)
            sp.dma_start(cf[:], ins["cf"]).then_inc(s_cf, 16)
            sp.dma_start(cb[:], ins["cb"]).then_inc(s_cb, 16)
            sp.dma_start(wts[:], ins["wts"]).then_inc(s_wts, 16)
            sp.dma_start(rows1[:], ins["rows1"].partition_broadcast(P)).then_inc(s_rows1, 16)
            xd = xn0_rows.rearrange("(t p) d -> p t d", p=P)
            for i in range(4):
                sp.wait_ge(s_xn, i + 1)
                sp.wait_ge(s_xn2, i + 1)
                sp.dma_start(xd[:, 4 * i:4 * i + 4, :], xn[:, 4 * i:4 * i + 4, :]).then_inc(s_xnd, 16)
            for e in range(2):
                sp.dma_start(we[:, e, :], ins["we"][e]).then_inc(s_we[e], 16)
                sp.dma_start(b2e[:, e, :], ins["b2"][e:e + 1, :].partition_broadcast(P)).then_inc(s_we[e], 16)
            for i in range(2):
                sp.dma_start(w1s[:, E // 2 * i:E // 2 * (i + 1), :], ins["w1s"][:, E // 2 * i:E // 2 * (i + 1), :]).then_inc(s_w1, 16)
            def biases(e):
                sp.dma_start(bias1[:, e, :], ins["bias1"][:, e, :].partition_broadcast(P)).then_inc(s_bias1, 16)

            for e in range(2, E):
                sp.wait_ge(s_y, 2 * (e - 1))
                sp.dma_start(we[:, e % 2, :], ins["we"][e]).then_inc(s_we[e % 2], 16)
                sp.wait_ge(s_ysb, 2 * (e - 1))
                sp.dma_start(b2e[:, e % 2, :], ins["b2"][e:e + 1, :].partition_broadcast(P)).then_inc(s_we[e % 2], 16)
                if e == 2:
                    sp.wait_ge(s_x1, B * NCH + 1)
                biases(e - 2)
            for k in range(4):
                sp.wait_ge(s_ys[k], 16 * (J0 // 4))
            yd = y0_rows[0:N, :].rearrange("(t p) d -> p t d", p=P)
            for i in range(4):
                sp.dma_start(xn[:, 4 * i:4 * i + 4, :], yd[:, 4 * i:4 * i + 4, :]).then_inc(s_y0[i], 16)
            for e in range(E - 2, E):
                biases(e)
            xd = xn1_rows.rearrange("(t p) d -> p t d", p=P)
            for i in range(4):
                sp.wait_ge(s_xn, 4 + i + 1)
                sp.wait_ge(s_xn2, 4 + i + 1)
                sp.dma_start(xd[:, 4 * i:4 * i + 4, :], xn[:, 4 * i:4 * i + 4, :]).then_inc(s_xnd, 16)
            for k in range(4):
                sp.wait_ge(s_ys[k], 16 * (J0 // 4 + (J1 - k + 3) // 4))
            yd = y1_rows[0:2 * N, :].rearrange("(k t p) d -> k p t d", k=2, p=P)
            for i in range(4):
                b, o = divmod(512 * i, S)
                sp.dma_start(xn[:, 4 * i:4 * i + 4, :], yd[1, :, 4 * i:4 * i + 4, :]).then_inc(s_yk[i], 16)
                sp.dma_start(xnT[:, b, o:o + 512].rearrange("p (t d) -> p t d", d=P), yd[0, :, 4 * i:4 * i + 4, :]).then_inc(s_yk[i], 16)
            ov = out.rearrange("(t p) d -> p t d", p=P)
            for i, done in ((0, 1), (2, 2), (1, None), (3, 3)):
                if done:
                    sp.wait_ge(s_res, done)
                else:
                    sp.wait_ge(s_last_quarter, 3)
                sp.dma_start(ov[:, 4 * i:4 * i + 4, :], x[:, 4 * i:4 * i + 4, :]).then_inc(s_out, 16)
            sp.wait_ge(s_out, 64)

        @block.gpsimd
        def _(pool):
            pool.memset(xnT[:, :, 0:WIN], 0.0).then_inc(s_zero, 1)
            pool.memset(sumT[:], 0.0).then_inc(s_zero, 1)
            pool.memset(zeros[:], 0.0).then_inc(s_zero, 1)
            pool.memset(att_flat, 0.0).then_inc(s_zero, 1)
            pool.memset(vd_flat, 0.0).then_inc(s_zero, 1)
            pool.memset(gvd_flat, 0.0).then_inc(s_zero, 1)
            pool.memset(vf[:, :, P:P + 1], 1.0).then_inc(s_zero, 1)
            pool.memset(kT[:, :, 0:WIN], 0.0).then_inc(s_zero, 1)
            pool.wait_ge(s_zero, 8)
            for blk in range(2):
                rows = slice(64 * blk, 64 * blk + 64)
                pool.memset(vd[rows, :, blk, :, HD], 1.0).then_inc(s_zero, 1)
                pool.memset(gvd[rows, :, blk, :, HD], 1.0).then_inc(s_zero, 1)
            zrows = y0_rows[0:N, :].rearrange("(p r) d -> p (r d)", p=P)
            for i in range(4):
                pool.dma_start(zrows[:, 512 * i:512 * i + 512], zeros[:]).then_inc(s_y0z, 16)
            pool.wait_ge(s_zero, 12)
            pool.wait_ge(s_xTs, 4)

            def windows(q, k, single):
                n = 2 * q + k
                b, start = k % B, (q + k // 2) * CH
                if not single or k:
                    pool.wait_ge(s_p3, n)
                for half in range(2):
                    src = xnT[:, b, WIN * half:].rearrange("p s -> p s")[:, bass.ds(start, CH)]
                    pool.tensor_copy(xw[:, :, WIN * half:WIN * half + WIN], src.rearrange("p (b i) -> p b i", i=WIN)).then_inc(s_xw, 1)

            attention_turns(pool, windows)
            bk, left, left2 = rows1[:, 0:P], kexp[:, 0, :], kexp[:, 1, :]
            pool.wait_ge(s_rows1, 16)
            for n, (o, a, b_) in enumerate(((bk_high[:], bk, None), (left, bk, bk_high[:]), (bk_mid[:], left, None),
                                            (left2, left, bk_mid[:]), (bk_parts[:], None, None))):
                if n:
                    pool.wait_ge(s_parts, n)
                if a is None:
                    pool.memset(o, 0.0).then_inc(s_parts, 1)
                elif b_ is None:
                    pool.tensor_copy(o, a).then_inc(s_parts, 1)
                else:
                    pool.tensor_tensor(o, a, b_, ALU.subtract).then_inc(s_parts, 1)
            for n, (row, src) in enumerate(((0, bk_high), (32, bk_mid), (64, left2))):
                pool.wait_ge(s_parts, 5 + n)
                pool.tensor_copy(bk_parts[row:row + 1, :], src[row:row + 1, :]).then_inc(s_parts, 1)
            pool.wait_ge(s_parts, 8)

            def gather(src, frm, j, k):
                slot_b = k[1] % 4
                index = ig[:, slot_b:slot_b + 1]
                if isinstance(j, int):
                    index = frm[:, j:j + 1]
                    pool.sem_inc(s_ig, 1)
                else:
                    pool.tensor_copy(index, frm[:, bass.ds(j, 1)]).then_inc(s_ig, 1)
                    pool.wait_ge(s_ig, k[0] + 1)
                    pool.sem_inc(s_index_seen, 1)
                pool.indirect_dma_start(
                    out=xg[:, slot_b, :], out_offset=None, in_=src,
                    in_offset=bass.IndirectOffsetOnAxis(ap=index.bitcast(U32), axis=0)
                ).then_inc(s_xg[slot_b], 16)

            def scatter(dst, to, j, k):
                slot_b = k[1] % 4
                index = isc[:, slot_b:slot_b + 1]
                if isinstance(j, int):
                    index = to[:, j:j + 1]
                    pool.sem_inc(s_isc, 1)
                else:
                    pool.tensor_copy(index, to[:, bass.ds(j, 1)]).then_inc(s_isc, 1)
                    pool.wait_ge(s_isc, k[0] + 1)
                    pool.sem_inc(s_index_seen, 1)
                pool.indirect_dma_start(
                    out=dst, in_=ysb[:, slot_b, :], in_offset=None,
                    out_offset=bass.IndirectOffsetOnAxis(ap=index.bitcast(U32), axis=0)
                ).then_inc(s_ys[slot_b], 16)

            pool.wait_ge(s_route, 1)
            pool.wait_ge(s_xnd, 64)
            pool.wait_ge(s_y0z, 64)
            for j in range(4):
                gather(xn0_rows, from0, j, (j, j))

            def expert(q, k, single):
                e = 2 * q + k
                if not single or k + 2 < E:
                    pool.wait_ge(s_tx, e + 1)
                    for s in range(2):
                        j = 4 * q + (2 * (k + 2) + s)
                        gather(xn0_rows, from0, j, (j, 2 * (k + 2) + s))
                if not single or k >= 1:
                    for s in range(2):
                        j = 4 * q + (2 * (k - 1) + s)
                        pool.wait_ge(s_ysb, j + 1)
                        scatter(y0_rows, to0, j, (j, 2 * (k - 1) + s))

            expert_turns(pool, expert)
            pool.wait_ge(s_y0[1], 16)
            tiles_ = slice(4, 8)
            pool.tensor_tensor(xn[:, tiles_, :], xn[:, tiles_, :], gate[:, tiles_].unsqueeze(2).broadcast_to([P, 4, P]), ALU.mult).then_inc(s_quarter, 1)
            pool.wait_ge(s_quarter, 1)
            pool.tensor_tensor(x[:, tiles_, :], x[:, tiles_, :], xn[:, tiles_, :], ALU.add).then_inc(s_quarter, 1)
            pool.wait_ge(s_rows1, 16)
            pool.wait_ge(s_xn, 8)
            pool.wait_ge(s_xn2, 8)
            pool.tensor_tensor(x[:], x[:], rows1[:, 2 * P:3 * P].unsqueeze(1).broadcast_to([P, T, P]), ALU.add).then_inc(s_bo, 1)
            pool.wait_ge(s_hit, 1)
            shape = [P, 2 * T, J1]
            pool.tensor_tensor(ids_of(1)[:, :, 0, :], is_hi[:], c("hi", 2 * T).unsqueeze(2).broadcast_to(shape), ALU.mult).then_inc(s_ids, 1)
            pool.wait_ge(s_route, 2)
            pool.wait_ge(s_xnd, 128)
            for j in range(3):
                gather(xn1_rows, from1, j, (J0 + j, j))

            def tile(q, k, single):
                i = 4 * q + k
                if not single or k + 3 < J1:
                    pool.wait_ge(t_x, i)
                    gather(xn1_rows, from1, i + 3, (J0 + i + 3, k + 3))
                if not single or 4 <= k:
                    pool.wait_ge(t_ysb, i - 3)
                    scatter(y1_rows, to1, i - 4, (J0 + i - 4, k - 4))

            tile_turns(pool, tile)
            pool.wait_ge(s_yk[1], 32)
            b, o = divmod(512, S)
            first = xnT[:, b, o:o + 512].rearrange("p (t d) -> p t d", d=P)
            pool.tensor_tensor(first, first, w1c[:, tiles_].unsqueeze(2).broadcast_to([P, 4, P]), ALU.mult).then_inc(s_last_quarter, 1)
            pool.wait_ge(s_last_quarter, 1)
            pool.tensor_tensor(x[:, tiles_, :], x[:, tiles_, :], first, ALU.add).then_inc(s_last_quarter, 1)
            pool.wait_ge(s_last_quarter, 2)
            pool.wait_ge(s_second, 2)
            pool.tensor_tensor(x[:, tiles_, :], x[:, tiles_, :], xn[:, tiles_, :], ALU.add).then_inc(s_last_quarter, 1)

        @block.scalar
        def _(act):
            def normalise(layer):
                act.wait_ge(s_rstd, layer + 1)
                for t in range(T):
                    if t % 4 >= 2:
                        last = act.activation(xn[:, t, :], x[:, t, :], ACT.Identity, bias=shift_by[:, t:t + 1], scale=rstd[:, t:t + 1])
                    if t % 4 == 3:
                        last.then_inc(s_xn2, 1)

            def evacuate_xT(layer):
                for i in range(4):
                    b, o = divmod(512 * i, S)
                    act.wait_ge(s_xt, 4 * layer + i + 1)
                    act.copy(xnT[:, b, WIN + o:WIN + o + 512], bank[i % 2][:]).then_inc(s_xTs, 1)

            def gate_exp(layer, n, src):
                act.wait_ge(s_gin, layer + 1)
                act.activation(n, src, ACT.Exp).then_inc(s_gexp, 1)

            normalise(0)
            evacuate_xT(0)
            act.wait_ge(s_cf, 16)
            act.wait_ge(s_zero, 12)

            def queries(n):
                act.wait_ge(s_p1, n + 1)
                for hh in range(4):
                    act.activation(qd[:, :, hh, :], bank[6][:, 0:CH].rearrange("p (b i) -> p b i", i=WIN), ACT.Copy,
                                   scale=c("mine", 4)[:, hh:hh + 1])
                act.copy(qT[:], bank[6][:, 0:CH]).then_inc(s_qd, 1)

            def latent_queries(n):
                for hh in range(4):
                    last = act.activation(gqd[0:64, :, hh, :], bank[7][0:64, CH:2 * CH].rearrange("p (b i) -> p b i", i=WIN),
                                          ACT.Copy, scale=c("mine", 4)[0:64, hh:hh + 1])
                last.then_inc(s_gqd, 1)

            def keys(n, b, end=True):
                if end:
                    act.copy(kT[:, b, 0:WIN], kT[:, b, CH:]).then_inc(s_kend, 1)
                    act.wait_ge(s_kend, n - 1)
                act.copy(kT[:, b, WIN:], bank[6][:, CH:2 * CH]).then_inc(s_kT, 1)

            def latents(n):
                act.wait_ge(s_gkv, n + 1)
                act.activation(gkT[0:64, :], bank[7][0:64, 0:NLAT], ACT.Copy, scale=NLAT / S)
                for blk in range(2):
                    last = act.activation(gvd[64 * blk:64 * blk + 64, :, blk, :, 0:HD],
                                          bank[7][0:64, 64:128].rearrange("p (g h d) -> p g h d", g=UG, h=4), ACT.Copy, scale=NLAT / S)
                last.then_inc(s_gk, 1)

            def gates(n, wait=True):
                act.wait_ge(s_p4, n + 1)
                if wait:
                    act.wait_ge(s_g1, n)
                act.activation(eg[:], bank[7][:].rearrange("p (a c) -> p a c", a=2), ACT.Exp, scale=-1.0).then_inc(s_eg, 1)

            def exponent(un, u):
                act.wait_ge(s_sub, un + (u + 1))
                act.activation(prob[:, u % 2, :], prob[:, u % 2, :], ACT.Exp).then_inc(s_exp, 1)

            def turned(un, u):
                act.wait_ge(s_tr, un + (u + 1))
                act.copy(probT[:, u % 2, :], bank[2 + u % 2][:]).then_inc(s_pte, 1)

            def weighted(un, u):
                act.wait_ge(s_pv, un + (u + 1))
                act.copy(oall_flat.rearrange("p (u n) -> p u n", u=U)[:, u % U, :], bank[4 + u % 2][:, 0:288]).then_inc(s_oe, 1)

            queries(0)
            keys(0, 0, end=False)
            exponent(0, 0)
            exponent(0, 1)

            def attend(q, k, single):
                n = 2 * q + k
                un = n * U
                before, after = not single or k > 0, not single or k < B * NCH - 1
                turned(un, 0)
                if before:
                    weighted(un, -1)
                latents(n)
                latent_queries(n)
                exponent(un, 2)
                turned(un, 1)
                gates(n, wait=before)
                if not before:
                    gate_exp(0, tb[:], ta[:])
                exponent(un, 3)
                turned(un, 2)
                if after:
                    queries(n + 1)
                if before:
                    act.wait_ge(s_att, n)
                weighted(un, 0)
                weighted(un, 1)
                exponent(un, 4)
                turned(un, 3)
                weighted(un, 2)
                if after:
                    keys(n + 1, (k + 1) % B, end=before)
                exponent(un, 5)
                turned(un, 4)
                weighted(un, 3)
                if after:
                    exponent(un, 6)
                turned(un, 5)
                weighted(un, 4)
                if after:
                    exponent(un, 7)
                else:
                    weighted(un, 5)

            attention_turns(act, attend)
            act.wait_ge(s_tx, 1)
            act.copy(xgT[:], bank[0][:, 0:2 * P]).then_inc(s_xgT, 1)

            def expert(q, k, single):
                if single and k >= E:
                    return
                e = 2 * q + k
                for f in range(4):
                    act.wait_ge(s_h, 4 * e + (f + 1))
                    act.activation(hT[:, f, :], bank[hidden_bank[f]][:, 0:2 * P], ACT.Gelu_apprx_tanh,
                                   bias=we[:, k % 2, 2 * F0 + f:2 * F0 + f + 1]).then_inc(s_gelu, 1)
                if not single or k + 1 < E:
                    act.wait_ge(s_tx, e + 2)
                    act.copy(xgT[:], bank[0][:, 0:2 * P]).then_inc(s_xgT, 1)

            expert_turns(act, expert)
            normalise(1)
            evacuate_xT(1)

            def keys_values(g):
                act.wait_ge(s_kv, g + 1)
                if g >= 2:
                    act.wait_ge(s_kvsum, 2 * g - 2)
                kv = bank[g % 2][:].rearrange("p (t c) -> p t c", t=2)
                four = slice(2 * (g % 2), 2 * (g % 2) + 2)
                act.activation(kexp[:, four, :], kv[:, :, 0:P], ACT.Exp).then_inc(s_kexp, 1)
                act.copy(vf[:, four, 0:P], kv[:, :, P:2 * P]).then_inc(s_vf, 1)

            for g in range(T // 2):
                keys_values(g)
                if g == 1:
                    act.wait_ge(s_gin, 2)
                    act.activation(e21[:], e21[:], ACT.Exp).then_inc(s_gexp, 1)
            for i in range(NQ + 2):
                if i < NQ:
                    act.wait_ge(s_qp, i + 1)
                    if i >= 1:
                        act.wait_ge(s_qf, i)
                    if i >= 2:
                        act.wait_ge(s_num, 2 * (i - 1))
                    act.activation(qe[:], q_bank[i % 2][:], ACT.Exp, bias=w("bq", 1))
                    act.activation(qf[i % 2][:], q_bank[i % 2][:], ACT.Relu, bias=w("bq", 1)).then_inc(s_qe, 1)
                if i >= 2:
                    m = i - 2
                    act.wait_ge(s_aTt, m + 1)
                    if m:
                        act.wait_ge(s_o1, m)
                    act.copy(aT[:], bank[1][:]).then_inc(s_aT, 1)
            act.wait_ge(t_x, 1)
            act.copy(xtT[:, 0, :], bank[6][:, 0:P]).then_inc(t_xTs, 1)

            def tile(q, k, single):
                i = 4 * q + k
                if not single or 1 <= k <= J1:
                    act.wait_ge(t_zT, i)
                    act.copy(zT, bank[2][:, 0:F1]).then_inc(t_zTs, 1)
                if not single or 3 <= k < J1 + 3:
                    act.wait_ge(t_oT, i - 2)
                    act.copy(oT, bank[3][:, 0:F1]).then_inc(t_oTs, 1)
                if not single or k + 1 < J1:
                    act.wait_ge(t_x, i + 2)
                    act.copy(xtT[:, (k + 1) % 2, :], bank[6][:, 0:P]).then_inc(t_xTs, 1)
                if not single or 1 <= k <= J1:
                    act.wait_ge(t_gb, i)
                    act.activation(sil, hgl[:, 0:F1], ACT.Silu).then_inc(t_sil, 1)

            tile_turns(act, tile)
            for i in range(4):
                act.wait_ge(s_yk[i], 32)
                for t in range(4 * i, 4 * i + 4):
                    last = act.activation(xn[:, t, :], xn[:, t, :], ACT.Copy, scale=w2c[:, t:t + 1])
                last.then_inc(s_second, 1)

        @block.tensor
        def _(pe):
            pe.wait_ge(s_cf, 16)

            logits_bank, prefix_bank, inverse_bank = (bank[5], bank[4]), (bank[7], bank[5]), (bank[6], bank[4])

            def keep_warm(b, n):
                for _ in range(n):
                    pe.matmul(bank[b][:], cbf("ones", P), cbf("before", 4 * P), start=True, stop=True)

            def logits(layer, name, tiles):
                for t in tiles:
                    pe.wait_ge(s_xTs, 4 * layer + t // 4 + 1)
                    mm = pe.matmul(logits_bank[layer][:, E * t:E * t + E], x_tile_T(t), w(name, E), start=True, stop=True)
                if t == T - 1:
                    mm.then_inc(s_lg, 1)

            def turn_x(layer):
                for i in range(4):
                    pe.wait_ge(s_xn, 4 * layer + i + 1)
                    pe.wait_ge(s_xn2, 4 * layer + i + 1)
                    if i >= 2:
                        pe.wait_ge(s_xTs, 4 * layer + i - 1)
                    if i:
                        keep_warm(7, WARM["turn_x1" if layer and i == 1 else "turn_x"])
                    for k in range(4):
                        mm = pe.transpose(bank[i % 2][:, P * k:P * k + P], xn[:, 4 * i + k, :], ident)
                    mm.then_inc(s_xt, 1)
                    if i == 3 and layer == 0:
                        pe.wait_ge(s_wts, 16)
                        logits(0, "wg", range(T // 4))
                    if i and layer == 1:
                        logits(1, "Wgate", range(4 * i - 4, 4 * i))

            def prefix(layer):
                pe.wait_ge(s_cnt, layer + 1)
                pe.matmul(prefix_bank[layer][:, 0:P], cbf("before", P), chosen_bf[:].rearrange("p e t -> p (e t)"), start=True, stop=False)
                pe.matmul(prefix_bank[layer][:, 0:P], cbf("ones", P), earlier_bf[:].rearrange("p e t -> p (e t)"), start=False, stop=True)
                pe.matmul(prefix_bank[layer][:, P:P + E], cbf("ones", P), total_bf[:], start=True, stop=True).then_inc(s_pos, 1)

            def inverse(layer, n, width, done):
                if layer == 1:
                    pe.wait_ge(s_ids, 1)
                for i in range(n):
                    if layer == 1 and i % WARM["inverse_step"] == 0:
                        keep_warm(2, 1)
                    pe.wait_ge(s_islo, done + i + 1)
                    pe.matmul(inverse_bank[layer][:, 0:2 * width], is_lo[:, i % T, :], ids_of(layer)[:, i, :, :],
                              start=(i == 0), stop=(i == n - 1)).then_inc(s_inv, 1)

            pe.wait_ge(s_cb, 16)
            keep_warm(7, WARM["start"])
            turn_x(0)
            pe.wait_ge(s_xTs, 4)
            pe.wait_ge(s_zero, 12)
            pe.wait_ge(s_gatew, 1)
            M0, M1 = bank[6], bank[7]

            def tokens(n, start, width):
                q, k = n
                return xnT[:, k % B, :][:, bass.ds((q + k // 2) * CH + start, width)]

            def queries_keys(n, m, free=True):
                if free:
                    pe.wait_ge(s_vd, m)
                pe.matmul(M0[:, 0:CH], w("wq"), tokens(n, WIN, CH), start=True, stop=True)
                pe.matmul(M0[:, CH:2 * CH], w("wk"), tokens(n, WIN, CH), start=True, stop=True).then_inc(s_p1, 1)

            def latents(n, m, free=True):
                pe.wait_ge(s_sum, m + 1)
                if free:
                    pe.wait_ge(s_x1, m)
                sums = sumT[:, n[1] % B, :]
                pe.matmul(M1[:, CH:2 * CH], w("wgq"), tokens(n, WIN, CH), start=True, stop=True)
                pe.matmul(M1[0:64, 0:64], w("wgk", 64), sums, start=True, stop=True)
                pe.matmul(M1[0:64, 64:128], sums, w("wgv", 64), start=True, stop=True).then_inc(s_gkv, 1)

            def values(m, half):
                if half == 0:
                    pe.wait_ge(s_xw, 2 * m + 2)
                    pe.wait_ge(s_kT, m + 1)
                for pr in range(2 * half, 2 * half + 2):
                    mm = pe.matmul(M0[:, P * pr:P * pr + P], xw[:, 2 * pr:2 * pr + 2, :].rearrange("p b i -> p (b i)"), w("wv"),
                                   start=True, stop=True)
                if half:
                    mm.then_inc(s_p3, 1)

            def gates(m):
                pe.wait_ge(s_qd, m + 1)
                pe.wait_ge(s_gk, m + 1)
                pe.wait_ge(s_gqd, m + 1)
                for a in range(2):
                    mm = pe.matmul(M1[:, CH * a:CH * a + CH], gate_w[:, a, :], qT[:], start=True, stop=True)
                mm.then_inc(s_p4, 1)

            def scores(n, m, u, early=False):
                ch = n[0] + n[1] // 2
                pe_bank = bank[u % 2]
                if not early:
                    pe.wait_ge(s_sub, m * U + (u - 1))
                r = 32 * (u if u < UL else u - UL)
                if u == 0:
                    pe.wait_ge(s_qd, m + 1)
                    pe.wait_ge(s_kT, m + 1)
                if u == UL:
                    pe.wait_ge(s_gqd, m + 1)
                    pe.wait_ge(s_gk, m + 1)
                spread = cbf("spread", P)
                if u < UL:
                    first = cbf("first", NCH * 64)[:, bass.ds(ch * 64, 64)]
                    pe.matmul(pe_bank[:, 0:64], spread, first, start=True, stop=False, skip_group_check=True)
                    pe.matmul(pe_bank[:, 64:], spread, cbf("local", 448), start=False, stop=False, skip_group_check=True)
                else:
                    latent = cbf("latent", NCH * 512)[:, bass.ds(ch * 512, 512)]
                    pe.matmul(pe_bank[:], spread, latent, start=True, stop=False, skip_group_check=True)
                for blk in range(NB):
                    q_, k_ = (qd, kT[r:r + 32, n[1] % B, WIN * blk:WIN * blk + 64]) if u < UL else (gqd, gkT[r:r + 32, :])
                    mm = pe.matmul(pe_bank[:, 64 * blk:64 * blk + 64], q_[r:r + 32, blk, :, :].rearrange("p h i -> p (h i)"), k_,
                                   start=False, stop=(blk == NB - 1), skip_group_check=True)
                mm.then_inc(s_S, 1)

            def turn(un, u, early):
                pe.wait_ge(s_exp, un + (u + 1))
                if not early or u >= 2:
                    pe.wait_ge(s_pte, un + (u - 1))
                for pr in range(NP2):
                    mm = pe.transpose(bank[2 + u % 2][:, P * pr:P * pr + P], prob[:, u % 2, P * pr:P * pr + P], ident)
                mm.then_inc(s_tr, 1)

            def weigh(un, m, u, early):
                pe.wait_ge(s_pte, un + (u + 1))
                if u == 0:
                    pe.wait_ge(s_vd, m + 1)
                if u == UL:
                    pe.wait_ge(s_gk, m + 1)
                if not early or u >= 2:
                    pe.wait_ge(s_oe, un + (u - 1))
                for pr in range(NP2):
                    v_ = vd[:, UL * pr + u, :, :, :] if u < UL else gvd[:, u - UL, :, :, :]
                    mm = pe.matmul(bank[4 + u % 2][:, 72 * pr:72 * pr + 72], probT[:, u % 2, P * pr:P * pr + P],
                                   v_.rearrange("p b h o -> p (b h o)"), start=True, stop=True)
                mm.then_inc(s_pv, 1)

            def remote(m):
                pe.wait_ge(s_p_att, m)
                pe.matmul(M1[:, 0:CH].rearrange("p (b i) -> p b i", i=32), w("rout"),
                          attT_flat.rearrange("p (b s i) -> p b s i", b=NB, s=2)[:, :, 1, :], start=True, stop=True).then_inc(s_rem, 1)

            def project(m):
                pe.wait_ge(s_mix, m)
                for t in range(2):
                    mm = pe.matmul(M1[:, P * t:P * t + P], mix[:, P * t:P * t + P], w("wout"), start=True, stop=True)
                mm.then_inc(s_proj, 1)

            start = (0, 0)
            queries_keys(start, 0, free=False)
            logits(0, "wg", range(T // 4, T))
            keep_warm(4, WARM["values"])
            values(0, 0)
            values(0, 1)
            scores(start, 0, 0, early=True)
            keep_warm(7, WARM["scores"])
            scores(start, 0, 1, early=True)
            keep_warm(7, WARM["scores"])

            def attend(q, k, single):
                this, next_ = (q, k), (q, k + 1)
                m = 2 * q + k
                un = m * U
                before, after = not single or k > 0, not single or k < B * NCH - 1
                early = not before
                turn(un, 0, early)
                scores(this, m, 2)
                if early:
                    keep_warm(7, WARM["scores"])
                latents(this, m, free=before)
                weigh(un, m, 0, early)
                turn(un, 1, early)
                scores(this, m, 3)
                gates(m)
                if early:
                    pe.wait_ge(s_lgread, 1)
                weigh(un, m, 1, early)
                turn(un, 2, early)
                if after:
                    queries_keys(next_, m + 1, free=before)
                scores(this, m, 4)
                if early:
                    pe.wait_ge(s_eg, 1)
                    prefix(0)
                weigh(un, m, 2, early)
                turn(un, 3, early)
                scores(this, m, 5)
                weigh(un, m, 3, early)
                if not after:
                    inverse(0, T, J0, 0)
                if before:
                    pe.wait_ge(s_eg, m + 1)
                    remote(m)
                turn(un, 4, early)
                if after:
                    scores(next_, m + 1, 0)
                    values(m + 1, 0)
                if before:
                    project(m)
                weigh(un, m, 4, early)
                turn(un, 5, early)
                if after:
                    scores(next_, m + 1, 1)
                    values(m + 1, 1)
                if early:
                    pe.wait_ge(s_posread, 1)
                weigh(un, m, 5, early)

            attention_turns(pe, attend)

            def turn_rows(j0, k):
                for s in range(2):
                    kb = k[1] + s
                    pe.wait_ge(s_xg[kb % 4], 16 * (k[0] + kb // 4 + 1))
                    mm = pe.transpose(bank[0][:, P * s:P * s + P], xg[:, kb % 4, :], ident)
                mm.then_inc(s_tx, 1)

            keep_warm(0, WARM["last_chunk"])
            turn_rows(0, (0, 0))
            remote(B * NCH)
            keep_warm(1, WARM["mix"])
            project(B * NCH)

            def expert(q, k, single):
                if single and k >= E:
                    return
                e = 2 * q + k
                pe.wait_ge(s_we[k % 2], 32 * (q + k // 2 + 1))
                pe.wait_ge(s_xgT, e + 1)
                for f in range(4):
                    pe.matmul(bank[hidden_bank[f]][:, 0:2 * P], we[:, k % 2, P * f:P * f + P], xgT[:],
                              start=True, stop=True).then_inc(s_h, 1)
                if not single or k + 1 < E:
                    turn_rows(None, (q, 2 * (k + 1)))
                if not single or k:
                    pe.wait_ge(s_ysb, 2 * e)
                for f in range(4):
                    pe.wait_ge(s_gelu, 4 * e + (f + 1))
                    for s in range(2):
                        mm = pe.matmul(bank[(3, 6)[s]][:, 0:P], hT[:, f, P * s:P * s + P],
                                       we[:, k % 2, F0 + P * f:F0 + P * f + P], start=(f == 0), stop=(f == 3))
                        if f == 3:
                            mm.then_inc(s_y, 1)

            expert_turns(pe, expert)

            pe.wait_ge(s_stats, 2)
            keep_warm(2, WARM["norm"])
            turn_x(1)
            logits(1, "Wgate", range(T - 4, T))

            def keys_values(g):
                if g >= 2:
                    pe.wait_ge(s_kf, g - 1)
                    pe.wait_ge(s_vf, g - 1)
                pe.matmul(bank[g % 2][:].rearrange("p (t c) -> p t c", t=2)[:, :, 0:P], cbf("ones", P),
                          bk_parts[:].unsqueeze(1).broadcast_to([P, 2, P]), start=True, stop=False, skip_group_check=True)
                for t in range(2):
                    mm = pe.matmul(bank[g % 2][:, 2 * P * t:2 * P * t + 2 * P], x_tile_T(2 * g + t), w("Wk", 2 * P),
                                   start=False, stop=(t == 1), skip_group_check=True)
                mm.then_inc(s_kv, 1)

            def sum_kv(g):
                pe.wait_ge(s_kf, g + 1)
                for t in range(2 * g, 2 * g + 2):
                    pe.matmul(bank[2 + g // 4][:, 0:P + 1], kf[:, t % 4, :], vf[:, t % 4, :],
                              start=(t % 8 == 0), stop=(t % 8 == 7)).then_inc(s_kvsum, 1)

            pe.wait_ge(s_parts, 8)
            for g in range(T // 2):
                keys_values(g)
                if g == 1:
                    keep_warm(6, WARM["routing"])
                if g:
                    sum_kv(g - 1)
                if g == 1:
                    prefix(1)

            def queries(i):
                b, o = divmod(512 * i, S)
                pe.matmul(q_bank[i % 2][:], w("Wq"), xnT[:, b, WIN + o:WIN + o + 512], start=True, stop=True).then_inc(s_qp, 1)

            queries(0)
            keep_warm(4, WARM["features"])
            sum_kv(T // 2 - 1)

            for i in range(NQ + 3):
                if 1 <= i < NQ:
                    if i >= 2:
                        pe.wait_ge(s_qe, i - 1)
                    queries(i)
                if i == 1:
                    keep_warm(4, WARM["features"])
                if 1 <= i <= NQ:
                    m = i - 1
                    pe.wait_ge(s_qf, m + 1)
                    pe.wait_ge(s_kvx, m // 2 + 1)
                    for pr in range(2):
                        if m:
                            pe.wait_ge(s_at, 2 * (m - 1) + pr + 1)
                        for t in range(2):
                            mm = pe.matmul(num_bank[pr][:, (P + NH) * t:(P + NH) * (t + 1)], qf[m % 2][:, P * (2 * pr + t):P * (2 * pr + t) + P],
                                           kvx[:, m // 2, :], start=True, stop=True)
                        mm.then_inc(s_num, 1)
                if i == 3:
                    pe.wait_ge(s_route, 2)
                if 2 <= i <= NQ + 1:
                    m = i - 2
                    pe.wait_ge(s_at, 2 * m + 2)
                    if m:
                        pe.wait_ge(s_aT, m)
                    for t in range(4):
                        mm = pe.transpose(bank[1][:, P * t:P * t + P], at1[:, P * t:P * t + P], ident)
                    mm.then_inc(s_aTt, 1)
                if i == 2:
                    inverse(1, 2 * T, J1, T)
                    keep_warm(2, WARM["after_inverse"])
                if i == NQ + 2:
                    pe.wait_ge(s_xg[0], 16 * (J0 // 4 + 1))
                    pe.transpose(bank[6][:, 0:P], xg[:, 0, :], ident).then_inc(t_x, 1)
                if i >= 3:
                    m = i - 3
                    pe.wait_ge(s_aT, m + 1)
                    if m:
                        pe.wait_ge(s_x2, m)
                    for t in range(4):
                        mm = pe.matmul(bank[4][:, P * t:P * t + P], aT[:, P * t:P * t + P], w("Wo"), start=True, stop=True)
                    mm.then_inc(s_o1, 1)
            pe.wait_ge(s_w1, 32)

            def weights(e, start, width):
                return w1s[:].rearrange("p e c -> p (e c)")[:, bass.ds(e * (W12 + WGL + W3) + start, width)]

            expert_of = expert_reader(pe, te)

            def tile(q, k, single):
                i = 4 * q + k
                if not single or k < J1:
                    expert_of(q, k)
                if not single or 1 <= k <= J1:
                    pe.wait_ge(t_z, i)
                    for a in range(2):
                        mm = pe.transpose(bank[2][:, P * a:P * a + P], z[:, P * a:P * a + P], ident)
                    mm.then_inc(t_zT, 1)
                if not single or 3 <= k < J1 + 3:
                    pe.wait_ge(t_o, i - 2)
                    for a in range(2):
                        mm = pe.transpose(bank[3][:, P * a:P * a + P], og[:, (k - 3) % 2, P * a:P * a + P], ident)
                    mm.then_inc(t_oT, 1)
                if not single or k < J1:
                    pe.wait_ge(t_xTs, i + 1)
                if not single or k + 1 < J1:
                    pe.wait_ge(s_xg[(k + 1) % 4], 16 * (q + J0 // 4 + (k + 1) // 4 + 1))
                    pe.transpose(bank[6][:, 0:P], xg[:, (k + 1) % 4, :], ident).then_inc(t_x, 1)
                if not single or k < J1:
                    pe.matmul(bank[0][:], xtT[:, k % 2, :], weights(expert_of(q, k), 0, W12), start=True, stop=True).then_inc(t_h, 1)
                if not single or 1 <= k <= J1:
                    e = expert_of(q, k - 1)
                    pe.wait_ge(t_zTs, i)
                    pe.wait_ge(t_gb, i - 1)
                    for a in range(2):
                        mm = pe.matmul(bank[1][:], zT[:, P * a:P * a + P], weights(e, W12 + 2 * F1 * a, 2 * F1), start=(a == 0), stop=(a == 1))
                    mm.then_inc(t_g, 1)
                if not single or 3 <= k < J1 + 3:
                    e = expert_of(q, k - 3)
                    pe.wait_ge(t_oTs, i - 2)
                    pe.wait_ge(t_ysb, i - 3)
                    for a in range(2):
                        mm = pe.matmul(bank[5][:, 0:P], oT[:, P * a:P * a + P], weights(e, W12 + WGL + P * a, P), start=(a == 0), stop=(a == 1))
                    mm.then_inc(t_y, 1)

            tile_turns(pe, tile)

        @block.vector
        def _(dve):
            own = Steps(dve, dve_own)

            def tt(o, a, b_, op):
                own(dve.tensor_tensor(o, a, b_, op))

            def ts(o, a, s1, op1, s2=None, op2=None):
                own(dve.tensor_scalar(o, a, s1, s2, op1, *(() if op2 is None else (op2,))))

            def stt(o, a, s, b_, op1, op2):
                own(dve.scalar_tensor_tensor(o, a, s, b_, op1, op2))

            def reduce(o, a, op):
                own(dve.tensor_reduce(o, a, X, op))

            def over_e(ap):
                return ap.unsqueeze(2).broadcast_to([P, T, E])

            def over_t(ap):
                return ap.unsqueeze(1).broadcast_to([P, T, E])

            def norm(layer):
                for i in ((0, 1, 2, 3), (0, 2, 3, 1))[layer]:
                    if layer == 0:
                        dve.wait_ge(s_x[i], 16)
                    elif i == 1:
                        dve.wait_ge(s_quarter, 2)
                    for t in range(4 * i, 4 * i + 4):
                        own.mark(dve.bn_stats(stats[:, t, :], x[:, t, :]))
                own.wait()
                dve.sem_inc(s_stats, 1)
                for t in range(T):
                    own.mark(dve.bn_aggr(mv[:, t, :], stats[:, t, :]))
                own.wait()
                ts(var[:], mv[:, :, 1], 1e-5, ALU.add)
                own.mark(dve.tensor_scalar(rstd[:].bitcast(I32), var[:].bitcast(I32), -0.5, float(0x5F3759DF), ALU.mult, ALU.add))
                ts(var[:], var[:], -0.5, ALU.mult)
                for _ in range(3):
                    tt(sq[:], rstd[:], rstd[:], ALU.mult)
                    tt(sq[:], sq[:], var[:], ALU.mult)
                    stt(rstd[:], sq[:], 1.5, rstd[:], ALU.add, ALU.mult)
                stt(shift_by[:], mv[:, :, 0], -1.0, rstd[:], ALU.mult, ALU.mult)
                dve.sem_inc(s_rstd, 1)
                for t in range(T):
                    if t % 4 < 2:
                        last = dve.tensor_scalar(xn[:, t, :], x[:, t, :], mv[:, t, 0:1], rstd[:, t:t + 1], ALU.subtract, ALU.mult)
                        own.mark(last) if t % 4 < 1 else last.then_inc(s_xn, 1)

            def best(m, ident_, one_hot):
                reduce(m, lg[:], ALU.max)
                tt(ta[:], lg[:], over_e(m), ALU.is_lt)
                stt(ta[:], ta[:], float(E), over_t(c("iota_e", E)), ALU.mult, ALU.add)
                reduce(ident_, ta[:], ALU.min)
                tt(one_hot, over_t(c("iota_e", E)), over_e(ident_), ALU.is_equal)

            def count(layer, choices):
                own(dve.tensor_copy(chosen[:].rearrange("p e t -> p t e"), choices))
                own(dve.tensor_tensor_scan(upto[:].rearrange("p e t -> p (e t)"), c("reset", P),
                                           chosen[:].rearrange("p e t -> p (e t)"), 0.0, ALU.mult, ALU.add))
                own.mark(dve.tensor_copy(chosen_bf[:], chosen[:]))
                own.mark(dve.tensor_copy(total_bf[:], upto[:, :, T - 1]))
                own.mark(dve.tensor_tensor(earlier_bf[:], upto[:], chosen[:], ALU.subtract))
                own.wait()
                dve.sem_inc(s_cnt, 1)

            def positions(layer):
                dve.wait_ge(s_pos, layer + 1)
                own(dve.tensor_copy(pos[:].rearrange("p e t -> p (e t)"), (bank[7], bank[5])[layer][:, 0:P]))
                dve.sem_inc(s_posread, 1)

            def own_position(one_hot, o):
                tt(ta[:], one_hot, pos[:].rearrange("p e t -> p t e"), ALU.mult)
                reduce(o, ta[:], ALU.add)

            def slot_factors(layer, n, width):
                nk = n // T
                own(dve.tensor_copy(slot_i[:, 0:nk, :], slot[:, 0:nk, :]))
                own.mark(dve.tensor_scalar(lo_i[:, 0:nk, :], slot_i[:, 0:nk, :], P - 1, None, ALU.bitwise_and))
                own.mark(dve.tensor_scalar(hi_i[:, 0:nk, :], slot_i[:, 0:nk, :], 7, None, ALU.logical_shift_right))
                own.wait()
                own.mark(dve.tensor_copy(lo[:, 0:nk, :], lo_i[:, 0:nk, :]))
                own.mark(dve.tensor_copy(hi[:, 0:nk, :], hi_i[:, 0:nk, :]))
                own.wait()
                shape = [P, n, width]
                hit = is_hi[:].rearrange("p n j -> p (n j)")[:, 0:n * width].rearrange("p (n j) -> p n j", n=n)
                hi_n = hi[:].rearrange("p k t -> p (k t)")
                tt(hit, c("iota_j", width).unsqueeze(1).broadcast_to(shape), hi_n[:, 0:n].unsqueeze(2).broadcast_to(shape), ALU.is_equal)
                if layer == 1:
                    dve.sem_inc(s_hit, 1)
                if layer == 0:
                    own.mark(dve.tensor_tensor(ids_of(layer)[:, :, 0, :], hit, c("hi", n).unsqueeze(2).broadcast_to(shape), ALU.mult))
                own.mark(dve.tensor_scalar(ids_of(layer)[:, :, 1, :], hit, c("part", 1), None, ALU.mult))
                own.wait()

            def one_hot_slots(done, n):
                lo_n = lo[:].rearrange("p k t -> p (k t)")
                for i in range(n):
                    if i >= T:
                        dve.wait_ge(s_inv, done + i - T + 1)
                    dve.tensor_scalar(is_lo[:, i % T, :], cbf("iota", P), lo_n[:, i:i + 1], None, ALU.is_equal).then_inc(s_islo, 1)

            def invert(layer, done, n, width, trash, frm, to):
                dve.wait_ge(s_inv, done + n)
                own(dve.tensor_copy(inv[:, :, 0:width], (bank[6], bank[4])[layer][:, 0:2 * width].rearrange("p (a j) -> p a j", a=2)))
                stt(ra[:, 0:width], inv[:, 0, 0:width], float(P), inv[:, 1, 0:width], ALU.mult, ALU.add)
                ts(rocc[:, 0:width], ra[:, 0:width], float(P), ALU.is_ge)
                stt(rb[:, 0:width], ra[:, 0:width], float(P), trash, ALU.subtract, ALU.subtract)
                tt(rb[:, 0:width], rb[:, 0:width], rocc[:, 0:width], ALU.mult)
                own.mark(dve.tensor_tensor(to, rb[:, 0:width], trash, ALU.add))
                ts(ra[:, 0:width], ra[:, 0:width], float(P), ALU.subtract, 0.0, ALU.max)
                ts(rb[:, 0:width], ra[:, 0:width], float(N), ALU.is_ge, float(-N), ALU.mult)
                tt(frm, ra[:, 0:width], rb[:, 0:width], ALU.add)
                dve.sem_inc(s_route, 1)

            norm(0)
            dve.wait_ge(s_cf, 16)
            dve.wait_ge(s_wts, 16)
            own.mark(dve.tensor_scalar(gate_w[:, 0, :], c("heads_hgd", P), w("glw", 1), None, ALU.mult))
            own.mark(dve.tensor_scalar(gate_w[:, 1, :], c("heads_hgd", P), w("grw", 1), None, ALU.mult))
            own.wait()
            dve.sem_inc(s_gatew, 1)

            def choose_expert():
                dve.wait_ge(s_lg, 1)
                dve.tensor_copy(lg[:].rearrange("p t e -> p (t e)"), bank[5][:, 0:T * E]).then_inc(s_lgread, 1)
                dve.wait_ge(s_lgread, 1)
                best(m1[:], id1[:], oh[:])
                tt(ta[:], lg[:], over_e(m1[:]), ALU.subtract)
                dve.sem_inc(s_gin, 1)
                count(0, oh[:])

            def place():
                dve.wait_ge(s_gexp, 1)
                reduce(esum[:], tb[:], ALU.add)
                own(dve.reciprocal(gate[:], esum[:]))
                own_position(oh[:], own_pos[:])
                ts(keep[:], own_pos[:], float(CAP), ALU.is_lt)
                tt(gate[:], gate[:], keep[:], ALU.mult)
                stt(slot[:, 0, :], id1[:], float(CAP), own_pos[:], ALU.mult, ALU.add)
                ts(keep[:], keep[:], float(-2 * N), ALU.mult, float(2 * N), ALU.add)
                tt(slot[:, 0, :], slot[:, 0, :], keep[:], ALU.add)

            dve.wait_ge(s_zero, 12)
            att = att_flat.rearrange("p (b s) -> p b s", b=NB)
            attT = attT_flat.rearrange("p (b s i) -> p b s i", b=NB, s=2)

            def sums(q, k, m):
                start = (q + k // 2) * CH
                dst = sumT[:, k % B, :][:, bass.ds((q + k // 2) * 16, 16)]
                src = xnT[:, k % B, WIN:][:, bass.ds(start, CH)].rearrange("p (n k) -> p n k", k=S // NLAT)
                dve.tensor_reduce(dst, src, X, ALU.add).then_inc(s_sum, 1)

            def values(m):
                dve.wait_ge(s_p3, m + 1)
                for blk in range(2):
                    rows = slice(64 * blk, 64 * blk + 64)
                    last = dve.tensor_copy(vd[rows, :, blk, :, 0:HD], bank[6][rows, :].rearrange("p (c h d) -> p c h d", h=4, d=HD))
                last.then_inc(s_vd, 1)

            def shift(un, u, early=False):
                s3 = bank[u % 2][:].rearrange("p (b j) -> p b j", j=64)
                dve.wait_ge(s_S, un + (u + 1))
                if not early or u >= 2:
                    dve.wait_ge(s_tr, un + (u - 1))
                dve.tensor_reduce(rmax[:, u % 2, :], s3, X, ALU.max).then_inc(s_max, 1)
                dve.wait_ge(s_max, un + (u + 1))
                dve.tensor_tensor(prob[:, u % 2, :].rearrange("p (b j) -> p b j", j=64), s3,
                                  rmax[:, u % 2, :].unsqueeze(2).broadcast_to([P, NB, 64]), ALU.subtract).then_inc(s_sub, 1)

            def own_sums(m):
                dve.wait_ge(s_oe, m * U)
                for hh in range(4):
                    rows = slice(32 * hh, 32 * hh + 32)
                    last = dve.reciprocal(rsum[rows, :, :], oall[rows, :, :, hh, HD])
                last.then_inc(s_rsum, 1)

            def own_columns(m):
                dve.wait_ge(s_rsum, m)
                for hh in range(4):
                    rows = slice(32 * hh, 32 * hh + 32)
                    last = dve.tensor_tensor(att[rows, :, 0:8 * U].rearrange("p b (u d) -> p u b d", d=HD), oall[rows, :, :, hh, 0:HD],
                                             rsum[rows, :, :].unsqueeze(3).broadcast_to([32, U, NB, HD]), ALU.mult)
                last.then_inc(s_att, 1)
                dve.wait_ge(s_att, m)
                dve.transpose(attT_flat, att_flat).then_inc(s_p_att, 1)

            def near_part(m):
                dve.wait_ge(s_p_att, m)
                dve.wait_ge(s_sg, m)
                dve.tensor_tensor(near[:].rearrange("p (b i) -> p b i", i=32), attT[:, :, 0, :],
                                  sg[:, 0, :].rearrange("p (b i) -> p b i", i=32), ALU.mult)

            def mixed(m):
                dve.wait_ge(s_rem, m)
                dve.tensor_tensor(mix[:], bank[7][:, 0:CH], sg[:, 1, :], ALU.mult).then_inc(s_m0read, 1)
                dve.wait_ge(s_m0read, m)
                dve.tensor_tensor(mix[:], mix[:], near[:], ALU.add).then_inc(s_mix, 1)

            def onto_stream(q, k):
                q, k = (q - 1, k + 1) if k == 0 else (q, k - 1)
                m = 2 * q + k
                dve.wait_ge(s_proj, m + 1)
                xs = x[:, bass.ds((q + k // 2) * 2 + (k % B) * (S // P), 2), :]
                dve.tensor_tensor(xs, xs, bank[7][:, 0:CH].rearrange("p (t d) -> p t d", d=P), ALU.add).then_inc(s_x1, 1)

            dve.wait_ge(s_xTs, 4)
            sums(0, 0, 0)
            values(0)
            shift(0, 0, early=True)
            shift(0, 1, early=True)

            def attend(q, k, single):
                m = 2 * q + k
                un = m * U
                before, after = not single or k > 0, not single or k < B * NCH - 1
                shift(un, 2)
                if before:
                    own_sums(m)
                else:
                    dve.sem_inc(s_x1, 1)
                    choose_expert()
                shift(un, 3)
                if before:
                    own_columns(m)
                shift(un, 4)
                if before:
                    near_part(m)
                else:
                    positions(0)
                if after:
                    sums(q, k + 1, m + 1)
                    if not before:
                        place()
                else:
                    dve.wait_ge(s_cb, 16)
                    one_hot_slots(0, T)
                shift(un, 5)
                if before:
                    mixed(m)
                dve.wait_ge(s_eg, m + 1)
                dve.tensor_scalar(sg[:], eg[:], 1.0, None, ALU.add).then_inc(s_g1, 1)
                if after:
                    shift(un, 6)
                if before:
                    onto_stream(q, k)
                else:
                    slot_factors(0, T, J0)
                if not after:
                    invert(0, 0, T, J0, c("trash0", J0), from0[:], to0[:])
                dve.wait_ge(s_g1, m + 1)
                dve.reciprocal(sg[:, 0, :], sg[:, 0, :])
                if after:
                    shift(un, 7)
                    values(m + 1)
                dve.reciprocal(sg[:, 1, :], sg[:, 1, :]).then_inc(s_sg, 1)

            attention_turns(dve, attend)
            own_sums(B * NCH)
            own_columns(B * NCH)
            near_part(B * NCH)
            mixed(B * NCH)
            onto_stream(0, B * NCH)

            def expert(q, k, single):
                if single and k >= E:
                    return
                for s in range(2):
                    j, kb = 4 * q + (2 * k + s), 2 * k + s
                    dve.wait_ge(s_y, j + 1)
                    if not single or k >= 2:
                        dve.wait_ge(s_ys[kb % 4], 16 * (q + kb // 4))
                    dve.tensor_tensor(ysb[:, kb % 4, :], bank[(3, 6)[s]][:, 0:P], b2e[:, k % 2, :], ALU.add).then_inc(s_ysb, 1)

            expert_turns(dve, expert)
            for i in (0, 2, 3):
                dve.wait_ge(s_y0[i], 16)
                for t in range(4 * i, 4 * i + 4):
                    own.mark(dve.scalar_tensor_tensor(x[:, t, :], xn[:, t, :], gate[:, t:t + 1], x[:, t, :], ALU.mult, ALU.add))
            own.wait()

            norm(1)
            dve.wait_ge(s_rows1, 16)
            dve.wait_ge(s_lg, 2)
            tt(lg[:], bank[4][:, 0:T * E].rearrange("p (t e) -> p t e", e=E), over_t(rows1[:, 3 * P:3 * P + E]), ALU.add)

            def keys(g):
                four = slice(2 * (g % 2), 2 * (g % 2) + 2)
                dve.wait_ge(s_kexp, g + 1)
                dve.tensor_scalar(kexp[:, four, :], kexp[:, four, :], 1.0, None, ALU.min).then_inc(s_kmin, 1)
                dve.wait_ge(s_kmin, g + 1)
                dve.wait_ge(s_vf, g + 1)
                kv = bank[g % 2][:].rearrange("p (t c) -> p t c", t=2)
                dve.scalar_tensor_tensor(kf[:, four, :], kv[:, :, 0:P], 0.0, kexp[:, four, :], ALU.max, ALU.add).then_inc(s_kf, 1)

            best(m1[:], id1[:], oh[:])
            stt(lg[:], oh[:], NEG, lg[:], ALU.mult, ALU.add)
            best(m2[:], id2[:], oh2[:])
            tt(e21[:], m2[:], m1[:], ALU.subtract)
            dve.sem_inc(s_gin, 1)
            tt(tb[:], oh[:], oh2[:], ALU.add)
            count(1, tb[:])
            keys(0)
            keys(1)
            positions(1)
            keys(2)
            own(dve.tensor_copy(cnt[:], bank[5][:, P:P + E]))
            tt(over[:], cnt[:].unsqueeze(2).broadcast_to([P, E, 16]), c("thresholds", 16).unsqueeze(1).broadcast_to([P, E, 16]), ALU.is_gt)
            reduce(tiles[:], over[:], ALU.add)
            keys(3)
            own(dve.tensor_tensor_scan(tiles_end[:], c("thresholds_one", E), tiles[:], 0.0, ALU.mult, ALU.add))
            tt(base[:], tiles_end[:], tiles[:], ALU.subtract)
            ts(base[:], base[:], float(P), ALU.mult)
            tt(pos[:], pos[:], base[:].unsqueeze(2).broadcast_to([P, E, T]), ALU.add)
            keys(4)
            own_position(oh[:], slot[:, 0, :])
            keys(5)
            own_position(oh2[:], slot[:, 1, :])
            keys(6)
            tt(passed[:], c("iota_j", J1).unsqueeze(2).broadcast_to([P, J1, E]),
               tiles_end[:].unsqueeze(1).broadcast_to([P, J1, E]), ALU.is_ge)
            reduce(te_f[:], passed[:], ALU.add)
            ts(te[:], te_f[:], float(E - 1), ALU.min)
            dve.wait_ge(s_gexp, 2)
            ts(w1c[:], e21[:], 1.0, ALU.add)
            own(dve.reciprocal(w1c[:], w1c[:]))
            tt(w2c[:], w1c[:], e21[:], ALU.mult)
            keys(7)

            for b_ in range(B):
                sums_ = bank[2 + b_]
                dve.wait_ge(s_kvsum, 8 * b_ + 8)
                own(dve.tensor_copy(ksum[:, b_:b_ + 1], sums_[:, P:P + 1]))
                stt(kvx[:, b_, 0:P], rows1[:, P:2 * P], ksum[:, b_:b_ + 1], sums_[:, 0:P], ALU.mult, ALU.add)
                own.mark(dve.tensor_tensor(kvx[:, b_, 0:P], kvx[:, b_, 0:P], c("heads", P), ALU.mult))
                own(dve.tensor_scalar(kvx[:, b_, P:], c("head", NH), ksum[:, b_:b_ + 1], None, ALU.mult))
                dve.sem_inc(s_kvx, 1)
            dve.wait_ge(s_bo, 1)
            for i in range(NQ + 3):
                if i < NQ:
                    dve.wait_ge(s_qe, i + 1)
                    q_ = qf[i % 2][:]
                    dve.scalar_tensor_tensor(q_, qe[:], 1.0, q_, ALU.min, ALU.add).then_inc(s_qf, 1)
                if i == 0:
                    slot_factors(1, 2 * T, J1)
                if 1 <= i <= NQ:
                    m = i - 1
                    for pr in range(2):
                        dve.wait_ge(s_num, 2 * m + pr + 1)
                        num = num_bank[pr][:, 0:2 * (P + NH)].rearrange("p (t c) -> p t c", t=2)
                        ts(den[:, pr, :].rearrange("p (t h) -> p t h", t=2), num[:, :, P:], 1e-6, ALU.max)
                        own(dve.reciprocal(rden[:, pr, :], den[:, pr, :]))
                        if m:
                            dve.wait_ge(s_aTt, m)
                        for t in range(2):
                            last = dve.tensor_tensor(at1[:, P * (2 * pr + t):P * (2 * pr + t) + P].rearrange("p (h d) -> p h d", d=HD),
                                                     num[:, t, 0:P].rearrange("p (h d) -> p h d", d=HD),
                                                     rden[:, pr, NH * t:NH * t + NH].unsqueeze(2).broadcast_to([P, NH, HD]), ALU.mult)
                        last.then_inc(s_at, 1)
                if i == 1:
                    one_hot_slots(T, 2 * T)
                    invert(1, T, 2 * T, J1, c("trash1", J1), from1[:], to1[:])
                if i >= 3:
                    m = i - 3
                    dve.wait_ge(s_o1, m + 1)
                    xs = x[:, 4 * m:4 * m + 4, :]
                    dve.tensor_tensor(xs, xs, bank[4][:].rearrange("p (t d) -> p t d", d=P), ALU.add).then_inc(s_x2, 1)

            dve.wait_ge(s_bias1, 16 * E)

            expert_of = expert_reader(dve, te)

            def bias(e, start, width):
                return shared[:, bass.ds(e * BIAS1 + start, width)]

            def tile(q, k, single):
                i = 4 * q + k
                if not single or k < J1:
                    bias_h = bias(expert_of(q, k), 0, 2 * F1)
                    dve.wait_ge(t_h, i + 1)
                    dve.tensor_tensor(h12[:], bank[0][:], bias_h, ALU.add).then_inc(t_hb, 1)
                    dve.wait_ge(t_hb, i + 1)
                    dve.tensor_tensor(z, h12[:, 0:F1], h12[:, F1:], ALU.mult).then_inc(t_z, 1)
                if not single or 2 <= k < J1 + 2:
                    dve.wait_ge(t_sil, i - 1)
                    if not single or k >= 4:
                        dve.wait_ge(t_oT, i - 3)
                    dve.tensor_tensor(og[:, k % 2, :], sil, hgl[:, F1:], ALU.mult).then_inc(t_o, 1)
                if not single or 1 <= k <= J1:
                    bias_g = bias(expert_of(q, k - 1), 2 * F1, 2 * F1)
                    if not single or 2 <= k:
                        dve.wait_ge(t_o, i - 1)
                    dve.wait_ge(t_g, i)
                    dve.tensor_tensor(hgl[:], bank[1][:], bias_g, ALU.add).then_inc(t_gb, 1)
                if not single or 3 <= k < J1 + 3:
                    bias_y = bias(expert_of(q, k - 3), 4 * F1, P)
                    dve.wait_ge(t_y, i - 2)
                    dve.wait_ge(s_ys[(k - 3) % 4], 16 * (q + (J0 // 4 + (k - 3) // 4)))
                    dve.tensor_tensor(ysb[:, (k - 3) % 4, :], bank[5][:, 0:P], bias_y, ALU.add).then_inc(t_ysb, 1)

            tile_turns(dve, tile)
            for i in (0, 2, 3):
                dve.wait_ge(s_yk[i], 32)
                b_, o = divmod(512 * i, S)
                first = xnT[:, b_, o:o + 512].rearrange("p (t d) -> p t d", d=P)
                for t in range(4):
                    n = 4 * i + t
                    own.mark(dve.scalar_tensor_tensor(x[:, n, :], first[:, t, :], w1c[:, n:n + 1], x[:, n, :], ALU.mult, ALU.add))
                own.wait()
                dve.wait_ge(s_second, i + 1)
                xs = x[:, 4 * i:4 * i + 4, :]
                dve.tensor_tensor(xs, xs, xn[:, 4 * i:4 * i + 4, :], ALU.add).then_inc(s_res, 1)


def kernel(**inputs):
    from concourse import bacc
    from concourse.bass_utils import run_bass_kernel_spmd

    a = {k: np.asarray(v) for k, v in inputs.items()}
    order = [8 * (4 * g + hh) + d for hh in range(4) for g in range(4) for d in range(HD)]
    rout = np.zeros((P, P), np.float32)
    for hh in range(4):
        for g in range(UG):
            h = 4 * g + hh
            rout[32 * hh + 8 * g:32 * hh + 8 * g + 8] = a["L0_attn_r_out_w"][8 * h:8 * h + 8][:, order]
    wts = np.concatenate(
        [a["L0_attn_wq"], a["L0_attn_wk"], a["L0_attn_wv"], a["L0_attn_w_out"][order], rout,
         a["L1_attn_Wq"], a["L1_attn_Wk"], a["L1_attn_Wv"], a["L1_attn_Wo"],
         a["L0_attn_wgq"], a["L0_attn_wgk"], a["L0_attn_wgv"], a["L0_ffn_wg"], a["L1_ffn_Wgate"],
         a["L0_attn_gate_local_w"].reshape(P, 1), a["L0_attn_gate_remote_w"].reshape(P, 1), a["L1_attn_bq"].reshape(P, 1)], axis=1)

    def chunks(m, n):
        return m.reshape(E, n, P, -1).transpose(0, 2, 1, 3).reshape(E, P, -1)

    we = np.concatenate([a["L0_ffn_w1"], chunks(a["L0_ffn_w2"], 4), chunks(a["L0_ffn_b1"].reshape(E, F0, 1), 4)], axis=2)
    w1s = np.concatenate([a["L1_ffn_W1"], a["L1_ffn_W2"],
                          chunks(np.concatenate([a["L1_ffn_Wg"], a["L1_ffn_Wl"]], axis=2), 2), chunks(a["L1_ffn_W3"], 2)], axis=2)
    bias1 = np.concatenate([a["L1_ffn_" + n] for n in ("b1", "b2", "bg", "bl", "b3")], axis=1)[None]
    rows1 = np.concatenate([a["L1_attn_bk"], a["L1_attn_bv"], a["L1_attn_bo"], a["L1_ffn_bgate"]]).reshape(1, -1)
    cf, cb = constants()
    arrays = {"x": a["L0_attn_x"].reshape(N, P), "wts": wts, "cf": cf, "cb": cb, "we": we, "b2": a["L0_ffn_b2"],
              "w1s": w1s.transpose(1, 0, 2), "bias1": bias1, "rows1": rows1}
    arrays = {k: np.ascontiguousarray(v) for k, v in arrays.items()}
    nc = bacc.Bacc("TRN2", target_bir_lowering=False, num_devices=1)
    ins = {k: nc.dram_tensor(f"in_{k}", v.shape, mybir.dt.from_np(v.dtype), kind="ExternalInput").ap() for k, v in arrays.items()}
    out = nc.dram_tensor("out", (N, P), F32, kind="ExternalOutput").ap()
    program(nc, ins, out)
    r = run_bass_kernel_spmd(nc, [{f"in_{k}": v for k, v in arrays.items()}], core_ids=[0])
    return r.results[0]["out"].reshape(B, S, P)
```
